# Optimizing a Trainium2 kernel written in Bass

```python
import numpy as np
import jax
import jax.numpy as jnp

def _softmax(x, axis=-1):
    return jax.nn.softmax(x, axis=axis)

def _gelu(x):
    return jax.nn.gelu(x, approximate=True)

def _silu(x):
    return jax.nn.silu(x)

def _sigmoid(x):
    return jax.nn.sigmoid(x)

def _layernorm(x, axis=-1, eps=1e-05):
    m = jnp.mean(x, axis=axis, keepdims=True)
    v = jnp.var(x, axis=axis, keepdims=True)
    return (x - m) / jnp.sqrt(v + eps)

def _scatter_add(tgt, idx, src, axis=0):
    return tgt.at[idx].add(src)

def _segment_sum(src, seg, n):
    return jax.ops.segment_sum(src, seg, n)
kernel_name = 'mk_recurrent_d2_jaxref_r8_c73e27'

def setup_inputs(seed: int=0):
    np.random.seed(seed)
    _w = jnp.asarray

    def _L0_attn_setup():
        import jax, jax.numpy as jnp
        import numpy as np
        HDC_DIM = 512
        N_HEADS = 4
        HEAD_DIM = HDC_DIM // N_HEADS

        def _ste_sign(w):
            alpha = jnp.mean(jnp.abs(w), axis=-1, keepdims=True)
            hard = alpha * jnp.sign(w)
            hard = jnp.where(hard == 0, alpha, hard)
            return jax.lax.stop_gradient(hard - w) + w
        key = jax.random.key(seed)
        kx, kq, kk, kv = jax.random.split(key, 4)
        B, T = (4, 256)
        x = jax.random.normal(kx, (B, T, HDC_DIM), dtype=jnp.float32)
        bv_q = jax.random.normal(kq, (N_HEADS, HEAD_DIM), dtype=jnp.float32) * 0.02
        bv_k = jax.random.normal(kk, (N_HEADS, HEAD_DIM), dtype=jnp.float32) * 0.02
        bv_v = jax.random.normal(kv, (N_HEADS, HEAD_DIM), dtype=jnp.float32) * 0.02
        return {'x': x, 'bv_q': bv_q, 'bv_k': bv_k, 'bv_v': bv_v}
    _L0_attn_in = _L0_attn_setup()

    def _L0_ffn_setup():
        import jax, jax.numpy as jnp
        import numpy as np
        NUM_EXPERTS = 8
        D_IN = 512
        D_OUT = 512
        key = jax.random.key(seed)
        k_x, k_gw, k_gb, k_ew, k_eb = jax.random.split(key, 5)
        x = jax.random.normal(k_x, (4, 256, D_IN), dtype=jnp.float32)
        gate_w = jax.random.normal(k_gw, (NUM_EXPERTS, D_IN), dtype=jnp.float32) * 0.02
        gate_b = jax.random.normal(k_gb, (NUM_EXPERTS,), dtype=jnp.float32) * 0.02
        expert_w = jax.random.normal(k_ew, (NUM_EXPERTS, D_OUT, D_IN), dtype=jnp.float32) * 0.02
        expert_b = jax.random.normal(k_eb, (NUM_EXPERTS, D_OUT), dtype=jnp.float32) * 0.02
        return {'x': x, 'gate_w': gate_w, 'gate_b': gate_b, 'expert_w': expert_w, 'expert_b': expert_b}
    _L0_ffn_in = _L0_ffn_setup()

    def _L1_attn_setup():
        import jax, jax.numpy as jnp
        import numpy as np
        H = 32
        KV = 8
        D = 128
        WINDOW = 128
        THETA = 10000.0

        def _rope_tables(seq_len, dtype=jnp.float32):
            inv_freq = 1.0 / THETA ** (jnp.arange(0, D, 2, dtype=jnp.float32) / D)
            t = jnp.arange(seq_len, dtype=jnp.float32)
            freqs = t[:, None] * inv_freq[None, :]
            emb = jnp.concatenate([freqs, freqs], axis=-1)
            return (jnp.cos(emb).astype(dtype), jnp.sin(emb).astype(dtype))

        def _rotate_half(x):
            x1, x2 = (x[..., :D // 2], x[..., D // 2:])
            return jnp.concatenate([-x2, x1], axis=-1)
        key = jax.random.key(seed)
        ks = jax.random.split(key, 5)
        B, S, E = (1, 256, 512)
        sc = 0.02
        return {'hidden_states': jax.random.normal(ks[0], (B, S, E), jnp.float32), 'Wq': jax.random.normal(ks[1], (H * D, E), jnp.float32) * sc, 'Wk': jax.random.normal(ks[2], (KV * D, E), jnp.float32) * sc, 'Wv': jax.random.normal(ks[3], (KV * D, E), jnp.float32) * sc, 'Wo': jax.random.normal(ks[4], (E, H * D), jnp.float32) * sc}
    _L1_attn_in = _L1_attn_setup()

    def _L1_ffn_setup():
        import jax, jax.numpy as jnp
        import numpy as np
        B, S, D, O, E, R = (4, 256, 512, 512, 8, 16)
        SCALING = 32.0 / 16.0
        MAX_THRESHOLD = 0.125
        key = jax.random.key(seed)
        ks = jax.random.split(key, 8)
        return {'x': jax.random.normal(ks[0], (B, S, D), jnp.float32), 'W_base': jax.random.normal(ks[1], (O, D), jnp.float32) * (1.0 / np.sqrt(D)), 'b_base': jax.random.normal(ks[2], (O,), jnp.float32) * 0.02, 'W_gate': jax.random.normal(ks[3], (E, D), jnp.float32) * (1.0 / np.sqrt(D)), 'W_thr': jax.random.normal(ks[4], (D,), jnp.float32) * (1.0 / np.sqrt(D)), 'b_thr': jax.random.normal(ks[5], (1,), jnp.float32) * 0.02, 'A_w': jax.random.normal(ks[6], (E, R, D), jnp.float32) * (1.0 / np.sqrt(D)), 'B_w': jax.random.normal(ks[7], (E, O, R), jnp.float32) * (1.0 / np.sqrt(R))}
    _L1_ffn_in = _L1_ffn_setup()
    _d = {'L0_attn_x': _L0_attn_in['x'], 'L0_attn_bv_q': _L0_attn_in['bv_q'], 'L0_attn_bv_k': _L0_attn_in['bv_k'], 'L0_attn_bv_v': _L0_attn_in['bv_v'], 'L0_ffn_gate_w': _L0_ffn_in['gate_w'], 'L0_ffn_gate_b': _L0_ffn_in['gate_b'], 'L0_ffn_expert_w': _L0_ffn_in['expert_w'], 'L0_ffn_expert_b': _L0_ffn_in['expert_b'], 'L1_attn_Wq': _L1_attn_in['Wq'], 'L1_attn_Wk': _L1_attn_in['Wk'], 'L1_attn_Wv': _L1_attn_in['Wv'], 'L1_attn_Wo': _L1_attn_in['Wo'], 'L1_ffn_W_base': _L1_ffn_in['W_base'], 'L1_ffn_b_base': _L1_ffn_in['b_base'], 'L1_ffn_W_gate': _L1_ffn_in['W_gate'], 'L1_ffn_W_thr': _L1_ffn_in['W_thr'], 'L1_ffn_b_thr': _L1_ffn_in['b_thr'], 'L1_ffn_A_w': _L1_ffn_in['A_w'], 'L1_ffn_B_w': _L1_ffn_in['B_w']}
    _x0 = _d['L0_attn_x']
    _d['L0_attn_x'] = jax.random.normal(jax.random.fold_in(jax.random.key(seed), 1), (2, 512, 512), dtype=_x0.dtype)
    del _x0
    return _d

def reference(L0_attn_x, L0_attn_bv_q, L0_attn_bv_k, L0_attn_bv_v, L0_ffn_gate_w, L0_ffn_gate_b, L0_ffn_expert_w, L0_ffn_expert_b, L1_attn_Wq, L1_attn_Wk, L1_attn_Wv, L1_attn_Wo, L1_ffn_W_base, L1_ffn_b_base, L1_ffn_W_gate, L1_ffn_W_thr, L1_ffn_b_thr, L1_ffn_A_w, L1_ffn_B_w):

    def _L0_attn_ref(x, bv_q, bv_k, bv_v):
        import jax, jax.numpy as jnp
        import numpy as np
        HDC_DIM = 512
        N_HEADS = 4
        HEAD_DIM = HDC_DIM // N_HEADS

        def _ste_sign(w):
            alpha = jnp.mean(jnp.abs(w), axis=-1, keepdims=True)
            hard = alpha * jnp.sign(w)
            hard = jnp.where(hard == 0, alpha, hard)
            return jax.lax.stop_gradient(hard - w) + w
        B, T, D = x.shape
        H, HD = (N_HEADS, HEAD_DIM)
        scale = HD ** (-0.5)
        q_bind = _ste_sign(bv_q)
        k_bind = _ste_sign(bv_k)
        v_bind = _ste_sign(bv_v)
        xh = x.reshape(B, T, H, HD)
        Q = xh * q_bind
        K = xh * k_bind
        V = xh * v_bind
        scores = jnp.einsum('bthd,bshd->bhts', Q, K) * scale
        causal = jnp.tril(jnp.ones((T, T), dtype=bool))
        attn = jnp.where(causal, jax.nn.sigmoid(scores * 4.0), 0.0)
        out = jnp.einsum('bhts,bshd->bthd', attn, V)
        return out.reshape(B, T, D)

    def _L0_ffn_ref(x, gate_w, gate_b, expert_w, expert_b):
        import jax, jax.numpy as jnp
        import numpy as np
        NUM_EXPERTS = 8
        D_IN = 512
        D_OUT = 512
        orig_shape = x.shape
        xf = x.reshape(-1, x.shape[-1])
        gate_logits = xf @ gate_w.T + gate_b
        gates = jax.nn.softmax(gate_logits, axis=-1)
        selected = jnp.argmax(gates, axis=-1)
        out = jnp.zeros((xf.shape[0], expert_w.shape[1]), dtype=xf.dtype)
        for j in range(expert_w.shape[0]):
            yj = xf @ expert_w[j].T + expert_b[j]
            out = out + jnp.where((selected == j)[:, None], yj, 0.0)
        return out.reshape(*orig_shape[:-1], expert_w.shape[1])

    def _L1_attn_ref(hidden_states, Wq, Wk, Wv, Wo):
        import jax, jax.numpy as jnp
        import numpy as np
        H = 32
        KV = 8
        D = 128
        WINDOW = 128
        THETA = 10000.0

        def _rope_tables(seq_len, dtype=jnp.float32):
            inv_freq = 1.0 / THETA ** (jnp.arange(0, D, 2, dtype=jnp.float32) / D)
            t = jnp.arange(seq_len, dtype=jnp.float32)
            freqs = t[:, None] * inv_freq[None, :]
            emb = jnp.concatenate([freqs, freqs], axis=-1)
            return (jnp.cos(emb).astype(dtype), jnp.sin(emb).astype(dtype))

        def _rotate_half(x):
            x1, x2 = (x[..., :D // 2], x[..., D // 2:])
            return jnp.concatenate([-x2, x1], axis=-1)
        B, S, E = hidden_states.shape
        q = (hidden_states @ Wq.T).reshape(B, S, H, D).transpose(0, 2, 1, 3)
        k = (hidden_states @ Wk.T).reshape(B, S, KV, D).transpose(0, 2, 1, 3)
        v = (hidden_states @ Wv.T).reshape(B, S, KV, D).transpose(0, 2, 1, 3)
        cos, sin = _rope_tables(S, hidden_states.dtype)
        cos = cos[None, None]
        sin = sin[None, None]
        q = q * cos + _rotate_half(q) * sin
        k = k * cos + _rotate_half(k) * sin
        k = jnp.repeat(k, H // KV, axis=1)
        v = jnp.repeat(v, H // KV, axis=1)
        scores = jnp.einsum('bhqd,bhkd->bhqk', q, k) / jnp.sqrt(jnp.asarray(D, q.dtype))
        i = jnp.arange(S)[:, None]
        j = jnp.arange(S)[None, :]
        band = jnp.abs(i - j) < WINDOW
        scores = jnp.where(band[None, None], -jnp.inf, scores)
        attn = jax.nn.softmax(scores, axis=-1)
        out = jnp.einsum('bhqk,bhkd->bhqd', attn, v)
        out = out.transpose(0, 2, 1, 3).reshape(B, S, H * D)
        return out @ Wo.T

    def _L1_ffn_ref(x, W_base, b_base, W_gate, W_thr, b_thr, A_w, B_w):
        import jax, jax.numpy as jnp
        import numpy as np
        B, S, D, O, E, R = (4, 256, 512, 512, 8, 16)
        SCALING = 32.0 / 16.0
        MAX_THRESHOLD = 0.125
        base = jnp.einsum('bsd,od->bso', x, W_base) + b_base
        xf = x.reshape(-1, D)
        gate = jax.nn.softmax(xf @ W_gate.T, axis=-1)
        thr = jax.nn.sigmoid(xf @ W_thr + b_thr[0]) * MAX_THRESHOLD
        adapted = gate - thr[:, None]
        selected = (adapted >= 0).astype(x.dtype)
        w = adapted * selected
        wsum = jnp.sum(w, axis=-1, keepdims=True)
        wsum = jnp.where(wsum == 0, jnp.ones_like(wsum), wsum)
        w = w / wsum
        h = jnp.einsum('nd,erd->ner', xf, A_w)
        moe = jnp.einsum('ner,ne,eor->no', h, w, B_w) * SCALING
        return base + moe.reshape(base.shape)
    x = L0_attn_x
    xn = _layernorm(x, axis=-1)
    s = _L0_attn_ref(xn, L0_attn_bv_q, L0_attn_bv_k, L0_attn_bv_v)
    g = _silu(_L0_ffn_ref(xn, L0_ffn_gate_w, L0_ffn_gate_b, L0_ffn_expert_w, L0_ffn_expert_b))
    x = x + s * g
    xn = _layernorm(x, axis=-1)
    s = _L1_attn_ref(xn, L1_attn_Wq, L1_attn_Wk, L1_attn_Wv, L1_attn_Wo)
    g = _silu(_L1_ffn_ref(xn, L1_ffn_W_base, L1_ffn_b_base, L1_ffn_W_gate, L1_ffn_W_thr, L1_ffn_b_thr, L1_ffn_A_w, L1_ffn_B_w))
    x = x + s * g
    return x

_drawn_inputs = setup_inputs


def setup_inputs(seed=0):
    import zlib

    import numpy as np

    out = dict(_drawn_inputs(seed))
    spreads = {}
    factors = {'L0_attn_bv_q': 64.0,
     'L0_attn_bv_k': 64.0,
     'L0_ffn_gate_b': 8.0,
     'L0_ffn_expert_b': 22.295,
     'L1_attn_Wq': 5.728,
     'L1_attn_Wk': 5.403,
     'L1_ffn_b_base': 8.0,
     'L1_ffn_W_thr': 8.0}
    for name, (base, spread) in spreads.items():
        noise = np.random.default_rng([zlib.crc32(name.encode()), seed]).standard_normal(out[name].shape)
        drawn = base * np.exp(spread * noise) if base else spread * noise
        out[name] = jnp.asarray(drawn.astype(out[name].dtype))
    for name, factor in factors.items():
        out[name] = (out[name] * factor).astype(out[name].dtype)
    return out
```

```python
from contextlib import ExitStack

import numpy as np

import concourse.bass as bass
from concourse import mybir
from concourse.alu_op_type import AluOpType as ALU

ACT = mybir.ActivationFunctionType
AX = mybir.AxisListType
F32 = mybir.dt.float32
F32R = mybir.dt.float32r

P = 128
BATCH, T, D = 2, 512, 512
N = BATCH * T
NT = N // P
TB = T // P
KD = D // P
EPS = 1e-5
H0 = 4
E0 = 8
HQ, HKV, DH = 32, 8, 128
GQ = HQ // HKV
WIN = P * (TB - 1)
NPROJ = GQ + 2
E1, R1 = 8, 16
THRESHOLD, SCALING = 0.125, 2.0
SMALL = E1 + 1 + E1 * R1
SMALL_PAD = 256
HIDDEN = -3.0e38

RAW_SLOTS = 4
Y_BANKS = 4


def f32(ap):
    return ap.bitcast(F32)


def mm3(pe, out, w, m, start, stop):
    pe.matmul(out, w[0], m[0], start=start, stop=False)
    pe.matmul(out, w[0], m[1], start=False, stop=False)
    return pe.matmul(out, w[1], m[0], start=False, stop=stop)


class Steps:

    def __init__(self, eng, sem):
        self.eng, self.sem, self.n = eng, sem, 0

    def __call__(self, ins, wait=True):
        self.n += 1
        ins.then_inc(self.sem, 1)
        if wait:
            self.wait()

    def wait(self):
        self.eng.wait_ge(self.sem, self.n)


def program(nc, A):
    with ExitStack() as outer:
        def sem(name):
            return outer.enter_context(nc.semaphore(name))

        def sb(ctx, name, shape, dt=F32):
            return ctx.enter_context(nc.sbuf_tensor(name, shape, dt))

        PS = outer.enter_context(nc.psum_tensor("PS", [P, 8, 512], F32))
        ident = sb(outer, "ident", [P, P])
        xT = [sb(outer, f"xT_{s}", [P, KD, N], F32R) for s in ("hi", "lo")]
        x1_dram = nc.dram_tensor("x1_spill", [N, D], F32, kind="Internal").ap()
        x1_rows = x1_dram.rearrange("(t p) d -> t p d", p=P)
        x1_stored = sem("x1_stored")

        block_a(nc, A, outer, sem, sb, PS, ident, xT, x1_rows, x1_stored)
        attn = sb(outer, "attn", [P, NT, D])
        block_b(nc, A, outer, sem, sb, PS, ident, xT, attn)
        block_c(nc, A, outer, sem, sb, PS, ident, xT, attn, x1_rows, x1_stored)


class Norm:

    def __init__(self, sem, name, src, xn, xT, PS, ident, scratch):
        self.src, self.xn, self.xT, self.PS, self.ident = src, xn, xT, PS, ident
        self.st, self.mv, self.ve, self.sd, self.rs, self.tmp = scratch
        self.var_ready = sem(f"{name}_var_ready")
        self.sd_ready = sem(f"{name}_sd_ready")
        self.xn_ready = sem(f"{name}_xn_ready")
        self.turned = sem(f"{name}_turned")
        self.hi_ready = sem(f"{name}_hi_ready")
        self.lo_ready = sem(f"{name}_lo_ready")

    def statistics(self, dve, step, half, src_wait):
        ts = range(TB * half, TB * (half + 1))
        for t in ts:
            src_wait(t)
            step(dve.bn_stats(self.st[:, t, :], self.src[:, t, :]), wait=False)
        step.wait()
        for t in ts:
            step(dve.bn_aggr(self.mv[:, t, :], self.st[:, t, :]), wait=False)
        step.wait()
        h = slice(TB * half, TB * (half + 1))
        dve.tensor_scalar(self.ve[:, h], self.mv[:, h, 1], EPS, None, ALU.add).then_inc(self.var_ready, 1)

    def deviations(self, act):
        for half in range(BATCH):
            h = slice(TB * half, TB * (half + 1))
            act.wait_ge(self.var_ready, half + 1)
            act.activation(self.sd[:, h], self.ve[:, h], ACT.Sqrt).then_inc(self.sd_ready, 1)

    def normalise(self, dve, step, half):
        h = slice(TB * half, TB * (half + 1))
        rs, tmp = self.rs[:, h], self.tmp[:, h]
        dve.wait_ge(self.sd_ready, half + 1)
        step(dve.reciprocal(rs, self.sd[:, h]))
        step(dve.tensor_tensor(tmp, rs, rs, ALU.mult))
        step(dve.tensor_tensor(tmp, tmp, self.ve[:, h], ALU.mult))
        step(dve.tensor_scalar(tmp, tmp, -0.5, 1.5, ALU.mult, ALU.add))
        step(dve.tensor_tensor(rs, rs, tmp, ALU.mult))
        for t in range(TB * half, TB * (half + 1)):
            dve.tensor_scalar(self.xn[:, t, :], self.src[:, t, :], self.mv[:, t, 0:1], self.rs[:, t:t + 1],
                              ALU.subtract, ALU.mult).then_inc(self.xn_ready, 1)

    def turn(self, pe, t):
        pe.wait_ge(self.xn_ready, t + 1)
        if t >= 2:
            pe.wait_ge(self.lo_ready, t - 1)
        for k in range(KD):
            ins = pe.transpose(self.PS[:, t % 2, k * P:(k + 1) * P], self.xn[:, t, k * P:(k + 1) * P], self.ident[:, :])
        ins.then_inc(self.turned, 1)

    def bank(self, t):
        return self.PS[:, t % 2, :].rearrange("p (k n) -> p k n", k=KD)

    def high(self, act, t):
        act.wait_ge(self.turned, t + 1)
        act.activation(self.xT[0][:, :, t * P:(t + 1) * P], self.bank(t), ACT.Copy).then_inc(self.hi_ready, 1)

    def low(self, dve, t):
        dve.wait_ge(self.hi_ready, t + 1)
        s = slice(t * P, (t + 1) * P)
        dve.tensor_tensor(self.xT[1][:, :, s], self.bank(t), f32(self.xT[0][:, :, s]),
                          ALU.subtract).then_inc(self.lo_ready, 1)


def block_a(nc, A, outer, sem, sb, PS, ident, xT, x1_rows, x1_stored):
    with ExitStack() as ctx:
        x = sb(ctx, "x", [P, NT, D])
        xn = sb(ctx, "xn", [P, NT, D])
        xv = [sb(ctx, f"xv_{s}", [P, NT, D], F32R) for s in ("hi", "lo")]
        y = sb(ctx, "y", [P, NT, D])
        st = sb(ctx, "st", [P, NT, 6])
        mv = sb(ctx, "mv", [P, NT, 2])
        ve, sd, rs, tmp8 = (sb(ctx, n, [P, NT]) for n in ("ve", "sd", "rs", "tmp8"))
        scratch = (st, mv, ve, sd, rs, tmp8)
        bv = sb(ctx, "bv", [3 * H0, P])
        bw = sb(ctx, "bw", [3 * H0, P])
        alpha = sb(ctx, "alpha", [3 * H0, 1])
        bind = sb(ctx, "bind", [P, 3 * H0])
        qk = sb(ctx, "qk", [P, H0])
        xf = [sb(ctx, f"xf{i}", [P, T]) for i in range(2)]
        q = [[sb(ctx, f"q{i}_{s}", [P, T], F32R) for s in ("hi", "lo")] for i in range(2)]
        tri = sb(ctx, "tri", [P, P])
        af = y[:, 0:TB, :]
        a = [sb(ctx, f"a_{s}", [P, TB, T], F32R) for s in ("hi", "lo")]
        sT = [sb(ctx, f"sT{i}", [P, T]) for i in range(2)]
        gw = sb(ctx, "gw", [P, KD, E0])
        gwp = [sb(ctx, f"gwp_{s}", [P, KD, P], F32R) for s in ("hi", "lo")]
        gb = sb(ctx, "gb", [E0, 1])
        lT = sb(ctx, "lT", [E0, N])
        order = sb(ctx, "order", [P, E0])
        lg, ex, oh = (sb(ctx, n, [P, NT, E0]) for n in ("lg", "ex", "oh"))
        oh_et = sb(ctx, "oh_et", [P, E0, NT])
        ohc = [sb(ctx, f"ohc{i}", [P, NT]) for i in range(2)]
        m8, s8 = (sb(ctx, n, [P, NT]) for n in ("m8", "s8"))
        ohT = sb(ctx, "ohT", [E0, N], F32R)
        eb = sb(ctx, "eb", [E0, D])
        ebs = [sb(ctx, f"eb_{s}", [E0, D], F32R) for s in ("hi", "lo")]
        raw = sb(ctx, "raw", [P, RAW_SLOTS, D])
        w = [[sb(ctx, f"w{i}_{s}", [P, KD, D], F32R) for s in ("hi", "lo")] for i in range(2)]

        x_in = [sem(f"x_in{t}") for t in range(NT)]
        const_in = sem("const_in")
        raw_in = [sem(f"raw_in{i}") for i in range(RAW_SLOTS)]
        a_dve = sem("a_dve")
        gw_zero, gw_hi, gw_lo = sem("gw_zero"), sem("gw_hi"), sem("gw_lo")
        bind_rows, bind_turned, bind_ready = sem("bind_rows"), sem("bind_turned"), sem("bind_ready")
        xv_hi, xv_lo = sem("xv_hi"), sem("xv_lo")
        xf_ready, q_hi, q_ready = sem("xf_ready"), sem("q_hi"), sem("q_ready")
        s_full, sig_done = sem("s_full"), sem("sig_done")
        a_hi, a_ready = sem("a_hi"), sem("a_ready")
        o_full, sT_ready, sT_turned, s_done = sem("o_full"), sem("sT_ready"), sem("sT_turned"), sem("s_done")
        gl_full, gl_done, lg_turned, lg_shifted, ex_ready = (
            sem(n) for n in ("gl_full", "gl_done", "lg_turned", "lg_shifted", "ex_ready"))
        oh_ready, oh_turned, ohT_ready = sem("oh_ready"), sem("oh_turned"), sem("ohT_ready")
        bias_full, bias_done = sem("bias_full"), sem("bias_done")
        w_hi, w_lo, y_full, y_done, ohc_ready = (sem(n) for n in ("w_hi", "w_lo", "y_full", "y_done", "ohc_ready"))
        g_ready, x1_ready = sem("g_ready"), sem("x1_ready")
        norm0 = Norm(sem, "norm0", x, xn, xT, PS, ident, scratch)
        norm1 = Norm(sem, "norm1", x, xn, xT, PS, ident, scratch)
        s_rows = xn

        x_rows = A["x"].rearrange("(t p) d -> t p d", p=P)
        consts = [(ident[:, :], A["ident"]), (tri[:, :], A["tri"]), (order[:, :], A["order"]),
                  (gw[:, :, :], A["gate_w"]), (gb[:, :], A["gate_b"]), (eb[:, :], A["expert_b"]),
                  (bv[0:H0, :], A["bv_q"]), (bv[H0:2 * H0, :], A["bv_k"]), (bv[2 * H0:3 * H0, :], A["bv_v"])]
        N_CONST = 16 * len(consts)
        heads = [(b, h) for b in range(BATCH) for h in range(H0)]
        NH = len(heads)
        W0, YF0, YD0 = RAW_SLOTS, 2 * NT, NT

        def col0(j):
            return min(P * j, T - 2 * P)

        block = ctx.enter_context(nc.Block())

        @block.sync
        def _(sp):
            for t in range(NT):
                sp.dma_start(x[:, t, :], x_rows[t]).then_inc(x_in[t], 16)
                if t == 0:
                    for dst, src in consts:
                        sp.dma_start(dst, src).then_inc(const_in, 16)
            with sp.Fori(0, E0) as e:
                for k in range(KD):
                    sp.wait_ge(w_lo, KD * e + k + 1)
                    sp.dma_start(raw[:, k, :], A["expert_w"][bass.ds(e * KD + k, 1)].rearrange("o p n -> (o p) n")
                                 ).then_inc(raw_in[k], 16)
            for t in range(NT):
                sp.wait_ge(x1_ready, t + 1)
                sp.dma_start(x1_rows[t], x[:, t, :]).then_inc(x1_stored, 16)
            sp.wait_ge(x1_stored, 16 * NT)

        @block.gpsimd
        def _(pool):
            pool.sem_inc(w_lo, W0)
            for t in range(NT):
                pool.wait_ge(xv_hi, t + 1)
                pool.tensor_tensor(xv[1][:, t, :], xn[:, t, :], f32(xv[0][:, t, :]), ALU.subtract).then_inc(xv_lo, 1)
            for n, (b, h) in enumerate(heads):
                pool.wait_ge(norm0.lo_ready, TB * (b + 1))
                if n >= 2:
                    pool.wait_ge(q_ready, n - 1)
                s = slice(b * T, (b + 1) * T)
                pool.tensor_tensor(xf[n % 2][:, :], f32(xT[0][:, h, s]), f32(xT[1][:, h, s]), ALU.add).then_inc(xf_ready, 1)
            with pool.Fori(0, E0 // 2) as i:
                for p in range(2):
                    for k in range(KD):
                        pool.wait_ge(w_hi, (2 * i + p) * KD + k + 1)
                        pool.tensor_tensor(w[p][1][:, k, :], raw[:, k, :], f32(w[p][0][:, k, :]),
                                           ALU.subtract).then_inc(w_lo, 1)

        @block.scalar
        def _(act):
            norm0.deviations(act)
            for t in range(NT):
                norm0.high(act, t)
            act.wait_ge(const_in, N_CONST)
            for b in range(BATCH):
                act.wait_ge(gl_full, b + 1)
                act.activation(lT[:, b * T:(b + 1) * T], PS[0:E0, 6 + b, :], ACT.Identity,
                               bias=gb[:, 0:1]).then_inc(gl_done, 1)

            def sigmoids(n):
                for j in range(TB):
                    act.wait_ge(s_full, TB * n + j + 1)
                    if n >= 1:
                        act.wait_ge(a_ready, TB * (n - 1) + j + 1)
                    act.activation(af[:, j, P * j:], PS[:, j, P * j:], ACT.Sigmoid).then_inc(sig_done, 1)

            def scale_out(n):
                act.wait_ge(o_full, n + 1)
                act.wait_ge(bind_ready, 1)
                if n >= 2:
                    act.wait_ge(sT_turned, n - 1)
                h = heads[n][1]
                act.activation(sT[n % 2][:, :], PS[:, 4, :], ACT.Copy,
                               scale=bind[:, 2 * H0 + h:2 * H0 + h + 1]).then_inc(sT_ready, 1)

            def rows_out(n):
                b, h = heads[n]
                act.wait_ge(sT_turned, n + 1)
                act.wait_ge(xv_lo, NT)
                act.activation(s_rows[:, b * TB:(b + 1) * TB, h * P:(h + 1) * P],
                               PS[:, 5, :].rearrange("p (t d) -> p t d", t=TB), ACT.Copy).then_inc(s_done, 1)

            sigmoids(0)
            for n in range(NH):
                if n + 1 < NH:
                    sigmoids(n + 1)
                scale_out(n)
                if n >= 1:
                    rows_out(n - 1)
            rows_out(NH - 1)
            act.wait_ge(lg_shifted, 1)
            act.activation(ex[:, :, :], lg[:, :, :], ACT.Exp).then_inc(ex_ready, 1)
            for b in range(BATCH):
                act.wait_ge(oh_turned, b + 1)
                act.activation(ohT[:, b * T:(b + 1) * T], PS[0:E0, 6 + b, :], ACT.Copy).then_inc(ohT_ready, 1)
            act.wait_ge(a_ready, TB * NH)
            for t in range(NT):
                act.wait_ge(bias_full, t + 1)
                act.activation(y[:, t, :], PS[:, t % Y_BANKS, :], ACT.Copy).then_inc(bias_done, 1)
            with act.Fori(0, E0 // 2) as i:
                for p in range(2):
                    act.wait_ge(y_full, YF0 + NT * (2 * i + p - 1))
                    for k in range(KD):
                        act.wait_ge(raw_in[k], 16 * (2 * i + p) + 16)
                        act.activation(w[p][0][:, k, :], raw[:, k, :], ACT.Copy).then_inc(w_hi, 1)
            for t in range(NT):
                act.wait_ge(y_done, YD0 + NT * (E0 - 1) + t + 1)
                act.activation(y[:, t, :], y[:, t, :], ACT.Silu).then_inc(g_ready, 1)
            norm1.deviations(act)
            for t in range(NT):
                norm1.high(act, t)

        @block.vector
        def _(dve):
            step = Steps(dve, a_dve)
            dve.sem_inc(y_done, YD0)
            for half in range(BATCH):
                norm0.statistics(dve, step, half, lambda t: dve.wait_ge(x_in[t], 16))
            dve.wait_ge(const_in, N_CONST)
            step(dve.tensor_reduce(alpha[:, :], bv[:, :], AX.X, ALU.add, apply_absolute_value=True), wait=False)
            step(dve.tensor_scalar(bw[:, :], bv[:, :], 0.0, 2.0, ALU.is_ge, ALU.mult))
            step(dve.tensor_scalar(alpha[:, :], alpha[:, :], 1.0 / P, None, ALU.mult))
            step(dve.tensor_scalar(bw[:, :], bw[:, :], -1.0, alpha[:, 0:1], ALU.add, ALU.mult))
            step(dve.tensor_tensor(bw[:, :], bw[:, :], bv[:, :], ALU.subtract))
            dve.tensor_tensor(bw[:, :], bw[:, :], bv[:, :], ALU.add).then_inc(bind_rows, 1)
            for s in range(2):
                step(dve.memset(f32(gwp[s][:, :, :]), 0.0), wait=False)
            step.wait()
            step(dve.tensor_copy(gwp[0][:, :, 0:E0], gw[:, :, :]))
            dve.tensor_tensor(gwp[1][:, :, 0:E0], gw[:, :, :], f32(gwp[0][:, :, 0:E0]), ALU.subtract).then_inc(gw_lo, 1)
            step(dve.tensor_copy(ebs[0][:, :], eb[:, :]))
            step(dve.tensor_tensor(ebs[1][:, :], eb[:, :], f32(ebs[0][:, :]), ALU.subtract))
            dve.wait_ge(bind_turned, 1)
            step(dve.tensor_copy(bind[:, :], PS[:, 7, 0:3 * H0]))
            step(dve.tensor_tensor(qk[:, :], bind[:, 0:H0], bind[:, H0:2 * H0], ALU.mult))
            dve.tensor_scalar(qk[:, :], qk[:, :], 4.0 * P ** -0.5, None, ALU.mult).then_inc(bind_ready, 1)
            for half in range(BATCH):
                norm0.normalise(dve, step, half)
                for t in range(TB * half, TB * (half + 1)):
                    dve.wait_ge(norm0.xn_ready, t + 1)
                    dve.tensor_copy(xv[0][:, t, :], xn[:, t, :]).then_inc(xv_hi, 1)
            for t in range(NT):
                norm0.low(dve, t)

            def bind_query(n):
                h = heads[n][1]
                dve.wait_ge(xf_ready, n + 1)
                dve.wait_ge(bind_ready, 1)
                if n >= 2:
                    dve.wait_ge(s_full, TB * (n - 1))
                qh, ql = q[n % 2]
                dve.tensor_scalar(qh[:, :], xf[n % 2][:, :], qk[:, h:h + 1], None, ALU.mult).then_inc(q_hi, 1)
                dve.wait_ge(q_hi, n + 1)
                dve.scalar_tensor_tensor(out=ql[:, :], in0=xf[n % 2][:, :], scalar=qk[:, h:h + 1],
                                         in1=f32(qh[:, :]), op0=ALU.mult, op1=ALU.subtract).then_inc(q_ready, 1)

            def split_weights(n):
                for j in range(TB):
                    dve.wait_ge(sig_done, TB * n + j + 1)
                    diag = slice(P * j, P * (j + 1))
                    step(dve.tensor_tensor(af[:, j, diag], af[:, j, diag], tri[:, :], ALU.mult), wait=False)
                step.wait()
                if n >= 1:
                    dve.wait_ge(o_full, n)
                for j in range(TB):
                    dve.tensor_copy(a[0][:, j, P * j:], af[:, j, P * j:]).then_inc(a_hi, 1)
                for j in range(TB):
                    dve.wait_ge(a_hi, TB * n + j + 1)
                    dve.tensor_tensor(a[1][:, j, P * j:], af[:, j, P * j:], f32(a[0][:, j, P * j:]),
                                      ALU.subtract).then_inc(a_ready, 1)

            bind_query(0)
            for n in range(NH):
                if n + 1 < NH:
                    bind_query(n + 1)
                split_weights(n)
            dve.wait_ge(lg_turned, 1)
            step(dve.tensor_copy(lg[:, :, :], PS[:, 6, 0:NT * E0].rearrange("p (t e) -> p t e", t=NT)))
            wide = lambda v: v[:, :].unsqueeze(2).broadcast_to([P, NT, E0])
            step(dve.tensor_reduce(m8[:, :], lg[:, :, :], AX.X, ALU.max))
            dve.tensor_tensor(lg[:, :, :], lg[:, :, :], wide(m8), ALU.subtract).then_inc(lg_shifted, 1)
            dve.wait_ge(ex_ready, 1)
            step(dve.tensor_reduce(s8[:, :], ex[:, :, :], AX.X, ALU.add))
            step(dve.reciprocal(s8[:, :], s8[:, :]))
            step(dve.tensor_tensor(ex[:, :, :], ex[:, :, :], wide(s8), ALU.mult))
            step(dve.tensor_reduce(m8[:, :], ex[:, :, :], AX.X, ALU.max))
            step(dve.tensor_tensor(oh[:, :, :], ex[:, :, :], wide(m8), ALU.is_ge))
            step(dve.tensor_tensor(oh[:, :, :], oh[:, :, :], order[:, :].unsqueeze(1).broadcast_to([P, NT, E0]), ALU.mult))
            step(dve.tensor_reduce(m8[:, :], oh[:, :, :], AX.X, ALU.max))
            step(dve.tensor_tensor(ex[:, :, :], oh[:, :, :], wide(m8), ALU.is_equal))
            dve.tensor_copy(oh_et[:, :, :], ex[:, :, :].rearrange("p t e -> p e t")).then_inc(oh_ready, 1)
            dve.wait_ge(bias_done, NT)
            dve.wait_ge(oh_ready, 1)
            with dve.Fori(0, E0 // 2) as i:
                for p in range(2):
                    e = 2 * i + p
                    dve.tensor_copy(ohc[p][:, :], oh_et[:, bass.ds(e, 1), :].rearrange("p o t -> p (o t)")).then_inc(ohc_ready, 1)
                    dve.wait_ge(ohc_ready, e + 1)
                    for t in range(NT):
                        dve.wait_ge(y_full, YF0 + NT * e + t + 1)
                        dve.wait_ge(y_done, YD0 + NT * (e - 1) + t + 1)
                        dve.scalar_tensor_tensor(out=y[:, t, :], in0=PS[:, t % Y_BANKS, :], scalar=ohc[p][:, t:t + 1],
                                                 in1=y[:, t, :], op0=ALU.mult, op1=ALU.add).then_inc(y_done, 1)
            dve.wait_ge(s_done, NH)
            for t in range(NT):
                dve.wait_ge(g_ready, t + 1)
                step(dve.tensor_tensor(y[:, t, :], y[:, t, :], s_rows[:, t, :], ALU.mult))
                dve.tensor_tensor(x[:, t, :], x[:, t, :], y[:, t, :], ALU.add).then_inc(x1_ready, 1)
            for half in range(BATCH):
                norm1.statistics(dve, step, half, lambda t: dve.wait_ge(x1_ready, t + 1))
            for half in range(BATCH):
                norm1.normalise(dve, step, half)
            for t in range(NT):
                norm1.low(dve, t)

        @block.tensor
        def _(pe):
            pe.sem_inc(y_full, YF0)
            pe.wait_ge(const_in, N_CONST)
            pe.wait_ge(bind_rows, 1)
            pe.transpose(PS[:, 7, 0:3 * H0], bw[:, :], ident[0:3 * H0, 0:3 * H0]).then_inc(bind_turned, 1)
            for t in range(NT):
                norm0.turn(pe, t)
            pe.wait_ge(gw_lo, 1)
            pe.wait_ge(bind_ready, 1)
            for b in range(BATCH):
                pe.wait_ge(norm0.lo_ready, TB * (b + 1))
                for k in range(KD):
                    ins = mm3(pe, PS[:, 6 + b, :], [g[:, k, :] for g in gwp],
                              [v[:, k, b * T:(b + 1) * T] for v in xT], k == 0, k == KD - 1)
                ins.then_inc(gl_full, 1)

            def scores(n):
                b, h = heads[n]
                pe.wait_ge(q_ready, n + 1)
                for j in range(TB):
                    if n >= 1:
                        pe.wait_ge(sig_done, TB * (n - 1) + j + 1)
                    keys = slice(b * T + j * P, b * T + (j + 1) * P)
                    mm3(pe, PS[:, j, col0(j):], [v[:, h, keys] for v in xT],
                        [v[:, col0(j):] for v in q[n % 2]], True, True).then_inc(s_full, 1)

            def outputs(n):
                b, h = heads[n]
                pe.wait_ge(xv_lo, NT)
                if n >= 1:
                    pe.wait_ge(sT_ready, n)
                for j in range(TB):
                    pe.wait_ge(a_ready, TB * n + j + 1)
                    ins = mm3(pe, PS[:, 4, P * j:], [v[:, b * TB + j, h * P:(h + 1) * P] for v in xv],
                              [v[:, j, P * j:] for v in a], j == 0, j == TB - 1)
                ins.then_inc(o_full, 1)

            def turn_out(n):
                pe.wait_ge(sT_ready, n + 1)
                if n >= 1:
                    pe.wait_ge(s_done, n)
                for t in range(TB):
                    ins = pe.transpose(PS[:, 5, t * P:(t + 1) * P], sT[n % 2][:, t * P:(t + 1) * P], ident[:, :])
                ins.then_inc(sT_turned, 1)

            scores(0)
            for n in range(NH):
                if n + 1 < NH:
                    scores(n + 1)
                if n == 1:
                    pe.wait_ge(gl_done, BATCH)
                    for t in range(NT):
                        ins = pe.transpose(PS[:, 6, t * E0:(t + 1) * E0], lT[:, t * P:(t + 1) * P], ident[0:E0, 0:E0])
                    ins.then_inc(lg_turned, 1)
                outputs(n)
                if n >= 1:
                    turn_out(n - 1)
            turn_out(NH - 1)
            pe.wait_ge(oh_ready, 1)
            for b in range(BATCH):
                for t in range(TB):
                    ins = pe.transpose(PS[0:E0, 6 + b, t * P:(t + 1) * P], ex[:, b * TB + t, :], ident[:, :])
                ins.then_inc(oh_turned, 1)
            pe.wait_ge(sig_done, TB * NH)
            for t in range(NT):
                pe.wait_ge(ohT_ready, t // TB + 1)
                if t >= Y_BANKS:
                    pe.wait_ge(bias_done, t - Y_BANKS + 1)
                pe.matmul(PS[:, t % Y_BANKS, :], ohT[:, t * P:(t + 1) * P], ebs[0][:, :], start=True, stop=False)
                pe.matmul(PS[:, t % Y_BANKS, :], ohT[:, t * P:(t + 1) * P], ebs[1][:, :], start=False,
                          stop=True).then_inc(bias_full, 1)
            pe.wait_ge(bias_done, NT)
            with pe.Fori(0, E0 // 2) as i:
                for p in range(2):
                    e = 2 * i + p
                    pe.wait_ge(w_lo, W0 + KD * (e + 1))
                    for t in range(NT):
                        pe.wait_ge(y_done, YD0 + NT * e + t + 1 - Y_BANKS)
                        for k in range(KD):
                            ins = mm3(pe, PS[:, t % Y_BANKS, :], [v[:, k, t * P:(t + 1) * P] for v in xT],
                                      [v[:, k, :] for v in w[p]], k == 0, k == KD - 1)
                        ins.then_inc(y_full, 1)
            pe.wait_ge(y_done, YD0 + NT * E0)
            for t in range(NT):
                norm1.turn(pe, t)




def block_b(nc, A, outer, sem, sb, PS, ident, xT, attn):
    with ExitStack() as ctx:
        cos, sin = (sb(ctx, n, [P, T]) for n in ("cos", "sin"))
        edge = sb(ctx, "edge", [P, TB * P])
        both = sb(ctx, "both", [P, WIN])
        raw = sb(ctx, "rawb", [P, RAW_SLOTS, D])
        wp = [[sb(ctx, f"wp{j}_{s}", [P, D], F32R) for s in ("hi", "lo")] for j in range(NPROJ)]
        wo = [[[sb(ctx, f"wo{o}{h}_{s}", [P, D], F32R) for s in ("hi", "lo")] for h in range(GQ)] for o in range(2)]
        kT = [[sb(ctx, f"kT{b}_{s}", [P, T + 2 * P], F32R) for s in ("hi", "lo")] for b in range(BATCH)]
        qT = [[sb(ctx, f"qT{b}_{s}", [P, GQ, T], F32R) for s in ("hi", "lo")] for b in range(BATCH)]
        vT = sb(ctx, "vT", [P, T])
        v = [sb(ctx, f"v_{s}", [P, TB, DH], F32R) for s in ("hi", "lo")]
        rot = [sb(ctx, f"rot{i}", [P, T]) for i in range(2)]
        full = [sb(ctx, f"full{i}", [P, T]) for i in range(2)]
        pr = [sb(ctx, f"pr{i}", [P, GQ, WIN]) for i in range(2)]
        pT = [sb(ctx, f"pT_{s}", [P, TB - 1, GQ * P], F32R) for s in ("hi", "lo")]
        oT = [sb(ctx, f"oT_{s}", [P, GQ * P], F32R) for s in ("hi", "lo")]
        nmax, rsum, rinv = ([sb(ctx, f"{n}{i}", [P, GQ]) for i in range(2)] for n in ("nmax", "rsum", "rinv"))

        table_in = sem("table_in")
        raw_in = [sem(f"rawb_in{i}") for i in range(RAW_SLOTS)]
        wb_hi, wb_lo = sem("wb_hi"), sem("wb_lo")
        proj_full = sem("proj_full")
        rope_read, roped = sem("rope_read"), sem("roped")
        kq_hi, kq_lo = sem("kq_hi"), sem("kq_lo")
        vT_done, v_turned, v_hi, v_lo = (sem(n) for n in ("vT_done", "v_turned", "v_hi", "v_lo"))
        sb_full, max_done, exp_done = sem("sb_full"), sem("max_done"), sem("exp_done")
        rinv_done = sem("rinv_done")
        max_wait, norm_wait = sem("max_wait"), sem("norm_wait")
        pr_first, pr_last = sem("pr_first"), sem("pr_last")
        pT_full, pT_hi, pT_lo = sem("pT_full"), sem("pT_hi"), sem("pT_lo")
        pv_full, oT_hi, oT_lo = sem("pv_full"), sem("oT_hi"), sem("oT_lo")
        wo_full, wo_done = sem("wo_full"), sem("wo_done")

        SEQ = NPROJ + GQ
        TURNS = HKV // 2
        PP = 2 * BATCH
        KQ = NPROJ
        HALF = DH // 2
        SCALE = float(np.float32(1.0) / np.sqrt(np.float32(DH)))
        PJ, OB = 6, 7
        WB0, KQ0, PT0, WD0, WF0 = RAW_SLOTS, 2, 2, NT, 1
        FILLERS = {0: (0, 1), 1: (2, 3), 2: (4, None), 3: (None, NPROJ - 1)}
        SPLITS = {(0, 1): (0, 1), (0, 2): (2, 3), (0, 3): (4,), (1, 0): (5, 6), (1, 1): (7,), (1, 2): (8,), (1, 3): (9,)}

        def mask(i):
            return {0: edge[:, 0:WIN], TB - 1: edge[:, P:P + WIN]}.get(i, both[:, :])

        def keys(b, i):
            first = ((i + 1) % TB) * P
            return [t[:, first:first + WIN] for t in kT[b]]

        def kq_count(p, j):
            return KQ * p + j + 2

        def kq_before(p, j):
            return kq_count(p, j - 2) if j >= 2 else kq_count(p - 1, j + GQ - 1)

        def following(pp, i):
            return (pp, i + 1) if i + 1 < TB else (pp + 1, 0)

        def stages(last):
            for pp in range(PP):
                for i in range(TB):
                    pair_follows = not (last and pp == PP - 1)
                    yield pp, i, pair_follows or i + 1 < TB, pair_follows

        def splits(gg, pp, i, last):
            odd, b = divmod(pp, BATCH)
            if last and odd == 1:
                return
            for r in SPLITS.get((b, i), ()):
                yield weight_tile(gg, odd + 1, r)

        def weight_tile(gg, go, r):
            c = SEQ * go + r
            return (2 * SEQ * gg + c, c % RAW_SLOTS, (2 * SEQ // RAW_SLOTS) * gg + c // RAW_SLOTS + 1,
                    2 * gg + go, r, wp[r] if r < NPROJ else wo[go % 2][r - NPROJ])

        block = ctx.enter_context(nc.Block())

        @block.sync
        def _(sp):
            for dst, src in ((cos[:, :], A["cos"]), (sin[:, :], A["sin"]), (edge[:, :], A["edge"]), (both[:, :], A["both"])):
                sp.dma_start(dst, src).then_inc(table_in, 16)
            with sp.Fori(0, TURNS) as gg:
                for c in range(2 * SEQ):
                    sp.wait_ge(wb_lo, 2 * SEQ * gg + c + 1)
                    sp.dma_start(raw[:, c % RAW_SLOTS, :],
                                 A["attn_w"][bass.ds(2 * SEQ * gg + c, 1)].rearrange("o p n -> (o p) n")
                                 ).then_inc(raw_in[c % RAW_SLOTS], 16)

        @block.gpsimd
        def _(pool):
            pool.sem_inc(wb_lo, WB0)
            pool.sem_inc(kq_lo, KQ0)

            def split_low(tile):
                at, slot, _, _, _, halves = tile
                pool.wait_ge(wb_hi, at + 1)
                pool.tensor_tensor(halves[1][:, :], raw[:, slot, :], f32(halves[0][:, :]), ALU.subtract).then_inc(wb_lo, 1)

            def rope_sum(gg, pp, j):
                m, p = (NPROJ - 1) * pp + j, PP * gg + pp
                pool.wait_ge(rope_read, 3 * ((NPROJ - 1) * p + j + 1))
                pool.tensor_tensor(full[m % 2][:, :], full[m % 2][:, :], rot[m % 2][:, :], ALU.add).then_inc(roped, 1)

            def rope_low(gg, pp, j):
                m, p, b = (NPROJ - 1) * pp + j, PP * gg + pp, pp % BATCH
                if j == 0:
                    for at, n in ((0, T), (T, 2 * P)):
                        pool.wait_ge(kq_hi, kq_count(p, 0) - (at == 0))
                        pool.tensor_tensor(kT[b][1][:, at:at + n], full[m % 2][:, 0:n], f32(kT[b][0][:, at:at + n]),
                                           ALU.subtract).then_inc(kq_lo, 1)
                else:
                    pool.wait_ge(kq_hi, kq_count(p, j))
                    pool.tensor_tensor(qT[b][1][:, j - 1, :], full[m % 2][:, :], f32(qT[b][0][:, j - 1, :]),
                                       ALU.subtract).then_inc(kq_lo, 1)

            def norm_first(gg, pp, i):
                s, par = TB * (PP * gg + pp) + i, (TB * pp + i) % 2
                pool.wait_ge(rinv_done, 2 * s + 1)
                pool.sem_inc(norm_wait, 1)
                for h in range(2):
                    pool.tensor_scalar(pr[par][:, h, :], pr[par][:, h, :], rinv[par][:, h:h + 1], 1.0,
                                       ALU.mult, ALU.mult).then_inc(pr_first, 1)

            def turn(gg, last):
                for pp, i, stage_follows, pair_follows in stages(last):
                    fa, fb = FILLERS[i]
                    if fa is not None and pair_follows:
                        rope_sum(gg, pp + 1, fa)
                        rope_low(gg, pp + 1, fa)
                    for tile in splits(gg, pp, i, last):
                        split_low(tile)
                    roping = fb is not None and fb < NPROJ - 1 and pair_follows
                    if roping:
                        rope_sum(gg, pp + 1, fb)
                    if stage_follows:
                        norm_first(gg, *following(pp, i))
                    if roping:
                        rope_low(gg, pp + 1, fb)

            for r in range(NPROJ):
                split_low(weight_tile(0, 0, r))
            for j in range(NPROJ - 1):
                rope_sum(0, 0, j)
                rope_low(0, 0, j)
            for r in range(NPROJ, SEQ):
                split_low(weight_tile(0, 0, r))
            norm_first(0, 0, 0)
            with pool.Fori(0, TURNS - 1) as gg:
                turn(gg, False)
            turn(TURNS - 1, True)

        @block.scalar
        def _(act):
            def split_high(tile):
                at, slot, loads, g, r, halves = tile
                act.wait_ge(raw_in[slot], 16 * loads)
                if not (isinstance(g, int) and g == 0):
                    if r < NPROJ:
                        act.wait_ge(proj_full, NPROJ * (2 * g - 1) + r + 1)
                    else:
                        act.wait_ge(wo_full, WF0 + BATCH * TB * (g - 1))
                act.activation(halves[0][:, :], raw[:, slot, :], ACT.Copy).then_inc(wb_hi, 1)

            def rope_high(gg, pp, j):
                m, p, b = (NPROJ - 1) * pp + j, PP * gg + pp, pp % BATCH
                act.wait_ge(roped, (NPROJ - 1) * p + j + 1)
                if j == 0:
                    act.activation(kT[b][0][:, 0:T], full[m % 2][:, :], ACT.Copy).then_inc(kq_hi, 1)
                    act.activation(kT[b][0][:, T:], full[m % 2][:, 0:2 * P], ACT.Copy).then_inc(kq_hi, 1)
                else:
                    act.activation(qT[b][0][:, j - 1, :], full[m % 2][:, :], ACT.Copy).then_inc(kq_hi, 1)

            def value_out(gg, pp):
                p = PP * gg + pp
                act.wait_ge(proj_full, NPROJ * (p + 1))
                act.activation(vT[:, :], PS[:, PJ, :], ACT.Copy).then_inc(vT_done, 1)

            def value_high(gg, pp):
                p = PP * gg + pp
                act.wait_ge(v_turned, p + 1)
                act.activation(v[0][:, :, :], PS[:, PJ, :].rearrange("p (t d) -> p t d", t=TB), ACT.Copy).then_inc(v_hi, 1)

            def exps(gg, pp, i, hs):
                s, par = TB * (PP * gg + pp) + i, (TB * pp + i) % 2
                for h in hs:
                    act.wait_ge(max_done, GQ * s + h + 1)
                    act.activation(pr[par][:, h, :], PS[:, h, 0:WIN], ACT.Exp, bias=nmax[par][:, h:h + 1], scale=-1.0,
                                   accum_out=rsum[par][:, h:h + 1]).then_inc(exp_done, 1)

            def turned_high(gg, pp, i):
                s = TB * (PP * gg + pp) + i
                for c in range(TB - 1):
                    bank = 4 + ((TB - 1) * (TB * pp + i) + c) % 2
                    act.wait_ge(pT_full, (TB - 1) * s + c + 1)
                    act.activation(pT[0][:, c, :], PS[:, bank, :], ACT.Copy).then_inc(pT_hi, 1)

            def out_high(gg, pp, i):
                s = TB * (PP * gg + pp) + i
                act.wait_ge(pv_full, s + 1)
                act.activation(oT[0][:, :], PS[:, OB, :], ACT.Copy).then_inc(oT_hi, 1)

            def turn(gg, last):
                for pp, i, stage_follows, pair_follows in stages(last):
                    fa, fb = FILLERS[i]
                    turned_high(gg, pp, i)
                    if stage_follows:
                        exps(gg, *following(pp, i), (0, 1))
                    if fa is not None and pair_follows:
                        rope_high(gg, pp + 1, fa)
                    out_high(gg, pp, i)
                    if fb == NPROJ - 1 and pair_follows:
                        value_out(gg, pp + 1)
                    if stage_follows:
                        exps(gg, *following(pp, i), (2, 3))
                    for tile in splits(gg, pp, i, last):
                        split_high(tile)
                    if fb is not None and pair_follows:
                        if fb < NPROJ - 1:
                            rope_high(gg, pp + 1, fb)
                        else:
                            value_high(gg, pp + 1)

            for r in range(NPROJ):
                split_high(weight_tile(0, 0, r))
            for j in range(NPROJ - 1):
                rope_high(0, 0, j)
            value_out(0, 0)
            value_high(0, 0)
            for r in range(NPROJ, SEQ):
                split_high(weight_tile(0, 0, r))
            exps(0, 0, 0, range(GQ))
            with act.Fori(0, TURNS - 1) as gg:
                turn(gg, False)
            turn(TURNS - 1, True)

        @block.vector
        def _(dve):
            dve.sem_inc(pT_lo, PT0)
            for t in range(NT):
                dve.memset(attn[:, t, :], 0.0).then_inc(wo_done, 1)
            dve.wait_ge(table_in, 64)

            def rope(gg, pp, j):
                m, p = (NPROJ - 1) * pp + j, PP * gg + pp
                dve.wait_ge(proj_full, NPROJ * p + j + 1)
                dve.wait_ge(kq_lo, KQ0 + kq_before(p, j))
                dve.tensor_tensor(full[m % 2][:, :], PS[:, PJ, :], cos[:, :], ALU.mult).then_inc(rope_read, 1)
                for to, at in ((0, HALF), (HALF, 0)):
                    dve.tensor_tensor(rot[m % 2][to:to + HALF, :], PS[at:at + HALF, PJ, :], sin[to:to + HALF, :],
                                      ALU.mult).then_inc(rope_read, 1)

            def value_low(gg, pp):
                p = PP * gg + pp
                dve.wait_ge(v_hi, p + 1)
                dve.tensor_tensor(v[1][:, :, :], PS[:, PJ, :].rearrange("p (t d) -> p t d", t=TB), f32(v[0][:, :, :]),
                                  ALU.subtract).then_inc(v_lo, 1)

            def maxima(gg, pp, i, hs):
                s, par = TB * (PP * gg + pp) + i, (TB * pp + i) % 2
                for h in hs:
                    dve.wait_ge(sb_full, GQ * s + h + 1)
                    dve.sem_inc(max_wait, 1)
                    dve.tensor_tensor_reduce(PS[:, h, 0:WIN], PS[:, h, 0:WIN], mask(i), -SCALE, 3.0e38,
                                             ALU.add, ALU.min, nmax[par][:, h:h + 1]).then_inc(max_done, 1)

            def inverses(gg, pp, i, half):
                s, par = TB * (PP * gg + pp) + i, (TB * pp + i) % 2
                hs = slice(2 * half, 2 * half + 2)
                dve.wait_ge(exp_done, GQ * s + 2 * half + 2)
                dve.reciprocal(rinv[par][:, hs], rsum[par][:, hs]).then_inc(rinv_done, 1)

            def norm_last(gg, pp, i):
                s, par = TB * (PP * gg + pp) + i, (TB * pp + i) % 2
                dve.wait_ge(rinv_done, 2 * s + 2)
                for h in (2, 3):
                    dve.tensor_scalar(pr[par][:, h, :], pr[par][:, h, :], rinv[par][:, h:h + 1], None,
                                      ALU.mult).then_inc(pr_last, 1)

            def turned_low(gg, pp, i):
                s = TB * (PP * gg + pp) + i
                for c in range(TB - 1):
                    bank = 4 + ((TB - 1) * (TB * pp + i) + c) % 2
                    dve.wait_ge(pT_hi, (TB - 1) * s + c + 1)
                    dve.tensor_tensor(pT[1][:, c, :], PS[:, bank, :], f32(pT[0][:, c, :]), ALU.subtract).then_inc(pT_lo, 1)

            def out_low(gg, pp, i):
                s = TB * (PP * gg + pp) + i
                dve.wait_ge(oT_hi, s + 1)
                dve.tensor_tensor(oT[1][:, :], PS[:, OB, :], f32(oT[0][:, :]), ALU.subtract).then_inc(oT_lo, 1)

            def accumulate(gg, pp, i):
                s, t = TB * (PP * gg + pp) + i, TB * (pp % BATCH) + i
                dve.wait_ge(wo_full, WF0 + s + 1)
                dve.wait_ge(wo_done, WD0 + s + 1 - NT)
                dve.tensor_tensor(attn[:, t, :], PS[:, OB, :], attn[:, t, :], ALU.add).then_inc(wo_done, 1)

            def turn(gg, last):
                for pp, i, stage_follows, pair_follows in stages(last):
                    fa, fb = FILLERS[i]
                    turned_low(gg, pp, i)
                    if fa is not None and pair_follows:
                        rope(gg, pp + 1, fa)
                    if stage_follows:
                        maxima(gg, *following(pp, i), (0, 1))
                    out_low(gg, pp, i)
                    if fb is not None and fb < NPROJ - 1 and pair_follows:
                        rope(gg, pp + 1, fb)
                    if stage_follows:
                        inverses(gg, *following(pp, i), 0)
                        maxima(gg, *following(pp, i), (2, 3))
                        inverses(gg, *following(pp, i), 1)
                        norm_last(gg, *following(pp, i))
                    accumulate(gg, pp, i)
                    if fb == NPROJ - 1 and pair_follows:
                        value_low(gg, pp + 1)

            for j in range(NPROJ - 1):
                rope(0, 0, j)
            value_low(0, 0)
            maxima(0, 0, 0, range(GQ))
            inverses(0, 0, 0, 0)
            inverses(0, 0, 0, 1)
            norm_last(0, 0, 0)
            with dve.Fori(0, TURNS - 1) as gg:
                turn(gg, False)
            turn(TURNS - 1, True)

        @block.tensor
        def _(pe):
            pe.sem_inc(wo_full, WF0)

            def project(gg, pp, j):
                p, b = PP * gg + pp, pp % BATCH
                go = pp // BATCH
                if not (isinstance(p, int) and p == 0 and j == 0):
                    pe.wait_ge(v_lo, p) if j == 0 else pe.wait_ge(rope_read, 3 * ((NPROJ - 1) * p + j))
                pe.wait_ge(wb_lo, WB0 + 2 * SEQ * gg + SEQ * go + j + 1)
                for k in range(KD):
                    ins = mm3(pe, PS[:, PJ, :], [w[:, k * DH:(k + 1) * DH] for w in wp[j]],
                              [x[:, k, b * T:(b + 1) * T] for x in xT], k == 0, k == KD - 1)
                ins.then_inc(proj_full, 1)

            def turn_values(gg, pp):
                p = PP * gg + pp
                pe.wait_ge(vT_done, p + 1)
                for t in range(TB):
                    ins = pe.transpose(PS[:, PJ, t * P:(t + 1) * P], vT[:, t * P:(t + 1) * P], ident[:, :])
                ins.then_inc(v_turned, 1)

            def scores(gg, pp, i, hs):
                s, p, b = TB * (PP * gg + pp) + i, PP * gg + pp, pp % BATCH
                for h in hs:
                    pe.wait_ge(kq_lo, KQ0 + kq_count(p, h + 1))
                    if not (isinstance(s, int) and s == 0):
                        pe.wait_ge(exp_done, GQ * (s - 1) + h + 1)
                    mm3(pe, PS[:, h, 0:WIN], [q[:, h, i * P:(i + 1) * P] for q in qT[b]], keys(b, i),
                        True, True).then_inc(sb_full, 1)

            def turn_weights(gg, pp, i):
                s, par = TB * (PP * gg + pp) + i, (TB * pp + i) % 2
                pe.wait_ge(pr_first, 2 * s + 2)
                pe.wait_ge(pr_last, 2 * s + 2)
                for c in range(TB - 1):
                    bank = 4 + ((TB - 1) * (TB * pp + i) + c) % 2
                    pe.wait_ge(pT_lo, PT0 + (TB - 1) * s + c - 1)
                    for h in range(GQ):
                        ins = pe.transpose(PS[:, bank, h * P:(h + 1) * P], pr[par][:, h, c * P:(c + 1) * P], ident[:, :])
                    ins.then_inc(pT_full, 1)

            def values(gg, pp, i):
                s, p = TB * (PP * gg + pp) + i, PP * gg + pp
                pe.wait_ge(v_lo, p + 1)
                pe.wait_ge(wo_done, WD0 + s)
                for c in range(TB - 1):
                    pe.wait_ge(pT_lo, PT0 + (TB - 1) * s + c + 1)
                    tile = (i + 1 + c) % TB
                    ins = mm3(pe, PS[:, OB, :], [x[:, tile, :] for x in v], [x[:, c, :] for x in pT], c == 0, c == TB - 2)
                ins.then_inc(pv_full, 1)

            def out_project(gg, pp, i):
                s, go = TB * (PP * gg + pp) + i, pp // BATCH
                pe.wait_ge(oT_lo, s + 1)
                pe.wait_ge(wb_lo, WB0 + 2 * SEQ * gg + SEQ * (go + 1))
                for h in range(GQ):
                    ins = mm3(pe, PS[:, OB, :], [x[:, h * P:(h + 1) * P] for x in oT], [x[:, :] for x in wo[go][h]],
                              h == 0, h == GQ - 1)
                ins.then_inc(wo_full, 1)

            def turn(gg, last):
                for pp, i, stage_follows, pair_follows in stages(last):
                    fa, fb = FILLERS[i]
                    turn_weights(gg, pp, i)
                    if fa is not None and pair_follows:
                        project(gg, pp + 1, fa)
                    if stage_follows:
                        scores(gg, *following(pp, i), (0, 1))
                    values(gg, pp, i)
                    if fb is not None and pair_follows:
                        project(gg, pp + 1, fb)
                    if stage_follows:
                        scores(gg, *following(pp, i), (2, 3))
                    out_project(gg, pp, i)
                    if fb == NPROJ - 1 and pair_follows:
                        turn_values(gg, pp + 1)

            for j in range(NPROJ):
                project(0, 0, j)
            turn_values(0, 0)
            scores(0, 0, 0, range(GQ))
            with pe.Fori(0, TURNS - 1) as gg:
                turn(gg, False)
            turn(TURNS - 1, True)


def block_c(nc, A, outer, sem, sb, PS, ident, xT, attn, x1_rows, x1_stored):
    with ExitStack() as ctx:
        x = sb(ctx, "x1", [P, NT, D])
        sw_raw, sw = sb(ctx, "sw_raw", [P, KD, SMALL]), [sb(ctx, f"sw_{s}", [P, KD, SMALL_PAD], F32R) for s in ("hi", "lo")]
        bw_raw, bw = sb(ctx, "bw_raw", [P, KD, D]), [sb(ctx, f"basew_{s}", [P, KD, D], F32R) for s in ("hi", "lo")]
        lw_raw, lw = sb(ctx, "lw_raw", [P, D]), [sb(ctx, f"lw_{s}", [P, D], F32R) for s in ("hi", "lo")]
        bias = sb(ctx, "base_bias", [P, D])
        tbias = sb(ctx, "thr_bias", [P, 1])
        small = sb(ctx, "small", [P, NT, SMALL])
        ex, ad, sel = (sb(ctx, n, [P, NT, E1]) for n in ("ex1", "ad", "sel"))
        th, m8, s8, z8 = (sb(ctx, n, [P, NT]) for n in ("th", "m81", "s81", "z8"))
        hw = sb(ctx, "hw", [P, NT, E1 * R1])
        hT = [sb(ctx, f"hT_{s}", [P, N], F32R) for s in ("hi", "lo")]
        z = [sb(ctx, f"z{i}", [P, D]) for i in range(2)]
        g = [sb(ctx, f"g{i}", [P, D]) for i in range(2)]

        x_in, w_in = sem("x1_in"), sem("w_in")
        c_dve, sw_ready, bw_hi, bw_ready, lw_ready = (sem(n) for n in ("c_dve", "sw_ready", "bw_hi", "bw_ready", "lw_ready"))
        small_full, small_done, shifted, ex_ready, th_ready = (
            sem(n) for n in ("small_full", "small_done", "shifted", "ex1_ready", "th_ready"))
        hw_ready, hT_full, hT_hi, hT_lo = (sem(n) for n in ("hw_ready", "hT_full", "hT_hi", "hT_lo"))
        base_full, z_ready, g_ready, out_ready, stored = (
            sem(n) for n in ("base_full", "z_ready", "g1_ready", "out_ready", "stored"))
        out_rows = A["out"].rearrange("(t p) d -> t p d", p=P)
        SM_BANKS, BASE = 2, 4
        wide = lambda v: v[:, :].unsqueeze(2).broadcast_to([P, NT, E1])

        block = ctx.enter_context(nc.Block())

        @block.sync
        def _(sp):
            loads = [(sw_raw[:, :, :], A["small_w"]), (tbias[:, :], A["thr_b"].partition_broadcast(P).rearrange("p o n -> p (o n)")),
                     (lw_raw[:, :], A["low_b"]), (bias[:, :], A["base_b"].partition_broadcast(P).rearrange("p o n -> p (o n)")),
                     (bw_raw[:, :, :], A["base_w"])]
            for dst, src in loads:
                sp.dma_start(dst, src).then_inc(w_in, 16)
            sp.wait_ge(x1_stored, 16 * NT)
            for t in range(NT):
                sp.dma_start(x[:, t, :], x1_rows[t]).then_inc(x_in, 16)
            for t in range(NT):
                sp.wait_ge(out_ready, t + 1)
                sp.dma_start(out_rows[t], x[:, t, :]).then_inc(stored, 16)
            sp.wait_ge(stored, 16 * NT)

        @block.gpsimd
        def _(pool):
            for k in range(KD):
                pool.wait_ge(bw_hi, k + 1)
                pool.tensor_tensor(bw[1][:, k, :], bw_raw[:, k, :], f32(bw[0][:, k, :]), ALU.subtract).then_inc(bw_ready, 1)

        @block.scalar
        def _(act):
            act.wait_ge(w_in, 80)
            for k in range(KD):
                act.activation(bw[0][:, k, :], bw_raw[:, k, :], ACT.Copy).then_inc(bw_hi, 1)
            for t in range(NT):
                act.wait_ge(small_full, t + 1)
                act.activation(small[:, t, :], PS[:, t % SM_BANKS, 0:SMALL], ACT.Copy).then_inc(small_done, 1)
            act.wait_ge(shifted, 1)
            act.activation(ex[:, :, :], ad[:, :, :], ACT.Exp).then_inc(ex_ready, 1)
            act.activation(th[:, :], small[:, :, E1], ACT.Sigmoid, bias=tbias[:, 0:1]).then_inc(th_ready, 1)
            for t in range(NT):
                act.wait_ge(hT_full, t + 1)
                act.activation(hT[0][:, t * P:(t + 1) * P], PS[:, 2 + t % 2, 0:P], ACT.Copy).then_inc(hT_hi, 1)
            for t in range(NT):
                act.wait_ge(z_ready, t + 1)
                if t >= 2:
                    act.wait_ge(out_ready, t - 1)
                act.activation(g[t % 2][:, :], z[t % 2][:, :], ACT.Silu).then_inc(g_ready, 1)

        @block.vector
        def _(dve):
            step = Steps(dve, c_dve)
            for s in range(2):
                step(dve.memset(f32(sw[s][:, :, SMALL:]), 0.0), wait=False)
            dve.wait_ge(w_in, 80)
            step(dve.tensor_copy(sw[0][:, :, 0:SMALL], sw_raw[:, :, :]))
            dve.tensor_tensor(sw[1][:, :, 0:SMALL], sw_raw[:, :, :], f32(sw[0][:, :, 0:SMALL]), ALU.subtract).then_inc(sw_ready, 1)
            step(dve.tensor_copy(lw[0][:, :], lw_raw[:, :]))
            dve.tensor_tensor(lw[1][:, :], lw_raw[:, :], f32(lw[0][:, :]), ALU.subtract).then_inc(lw_ready, 1)
            dve.wait_ge(small_done, NT)
            gl = small[:, :, 0:E1]
            step(dve.tensor_reduce(m8[:, :], gl, AX.X, ALU.max))
            dve.tensor_tensor(ad[:, :, :], gl, wide(m8), ALU.subtract).then_inc(shifted, 1)
            dve.wait_ge(ex_ready, 1)
            step(dve.tensor_reduce(s8[:, :], ex[:, :, :], AX.X, ALU.add))
            step(dve.reciprocal(s8[:, :], s8[:, :]))
            step(dve.tensor_tensor(ex[:, :, :], ex[:, :, :], wide(s8), ALU.mult))
            dve.wait_ge(th_ready, 1)
            step(dve.tensor_scalar(th[:, :], th[:, :], THRESHOLD, None, ALU.mult))
            step(dve.tensor_tensor(ad[:, :, :], ex[:, :, :], wide(th), ALU.subtract))
            step(dve.tensor_scalar(sel[:, :, :], ad[:, :, :], 0.0, None, ALU.is_ge))
            step(dve.tensor_tensor(ad[:, :, :], ad[:, :, :], sel[:, :, :], ALU.mult))
            step(dve.tensor_reduce(s8[:, :], ad[:, :, :], AX.X, ALU.add))
            step(dve.tensor_scalar(z8[:, :], s8[:, :], 0.0, None, ALU.is_equal))
            step(dve.tensor_tensor(s8[:, :], s8[:, :], z8[:, :], ALU.add))
            step(dve.reciprocal(s8[:, :], s8[:, :]))
            step(dve.tensor_tensor(ad[:, :, :], ad[:, :, :], wide(s8), ALU.mult))
            step(dve.tensor_scalar(ad[:, :, :], ad[:, :, :], SCALING, None, ALU.mult))
            for t in range(NT):
                dve.tensor_tensor(hw[:, t, :].rearrange("p (e r) -> p e r", e=E1),
                                  small[:, t, E1 + 1:].rearrange("p (e r) -> p e r", e=E1),
                                  ad[:, t, :].unsqueeze(2).broadcast_to([P, E1, R1]), ALU.mult).then_inc(hw_ready, 1)
            for t in range(NT):
                dve.wait_ge(hT_hi, t + 1)
                s = slice(t * P, (t + 1) * P)
                dve.tensor_tensor(hT[1][:, s], PS[:, 2 + t % 2, 0:P], f32(hT[0][:, s]), ALU.subtract).then_inc(hT_lo, 1)
            dve.wait_ge(x_in, 16 * NT)
            for t in range(NT + 1):
                if t < NT:
                    dve.wait_ge(base_full, t + 1)
                    if t >= 2:
                        dve.wait_ge(g_ready, t - 1)
                    dve.tensor_tensor(z[t % 2][:, :], PS[:, BASE + t % 4, :], bias[:, :], ALU.add).then_inc(z_ready, 1)
                if t >= 1:
                    u = t - 1
                    dve.wait_ge(g_ready, u + 1)
                    step(dve.tensor_tensor(attn[:, u, :], attn[:, u, :], g[u % 2][:, :], ALU.mult))
                    dve.tensor_tensor(x[:, u, :], x[:, u, :], attn[:, u, :], ALU.add).then_inc(out_ready, 1)

        @block.tensor
        def _(pe):
            pe.wait_ge(sw_ready, 1)
            for t in range(NT):
                if t >= SM_BANKS:
                    pe.wait_ge(small_done, t - SM_BANKS + 1)
                for k in range(KD):
                    ins = mm3(pe, PS[:, t % SM_BANKS, 0:SMALL_PAD], [x_[:, k, t * P:(t + 1) * P] for x_ in xT],
                              [w[:, k, :] for w in sw], k == 0, k == KD - 1)
                ins.then_inc(small_full, 1)
            pe.wait_ge(bw_ready, KD)

            def base(t):
                for k in range(KD):
                    mm3(pe, PS[:, BASE + t % 4, :], [x_[:, k, t * P:(t + 1) * P] for x_ in xT],
                        [w[:, k, :] for w in bw], k == 0, False)

            def turn_rows(t):
                pe.wait_ge(hw_ready, t + 1)
                if t >= 2:
                    pe.wait_ge(hT_lo, t - 1)
                pe.transpose(PS[:, 2 + t % 2, 0:P], hw[:, t, :], ident[:, :]).then_inc(hT_full, 1)

            def low_rank(t):
                pe.wait_ge(hT_lo, t + 1)
                pe.wait_ge(lw_ready, 1)
                mm3(pe, PS[:, BASE + t % 4, :], [v[:, t * P:(t + 1) * P] for v in hT], [w[:, :] for w in lw],
                    False, True).then_inc(base_full, 1)

            AHEAD = 3
            for t in range(NT + AHEAD):
                if t < NT:
                    if t >= 4:
                        pe.wait_ge(z_ready, t - 3)
                    base(t)
                if t == AHEAD - 1:
                    for u in range(NT):
                        turn_rows(u)
                if t >= AHEAD:
                    low_rank(t - AHEAD)


def tables():
    inv = (np.float32(1.0) / np.power(np.float32(10000.0), np.arange(0, DH, 2, dtype=np.float32) / np.float32(DH))).astype(np.float32)
    angle = (np.arange(T, dtype=np.float32)[None, :] * np.concatenate([inv, inv])[:, None]).astype(np.float32)
    sin = np.sin(angle).astype(np.float32)
    sin[:DH // 2] *= -1
    key, query = np.arange(P)[None, :], np.arange(P)[:, None]
    near = np.where(key >= query, 0.0, HIDDEN).astype(np.float32)
    far = np.where(key <= query, 0.0, HIDDEN).astype(np.float32)
    zero = np.zeros((P, P), np.float32)
    return {
        "ident": np.eye(P, dtype=np.float32),
        "tri": (key >= query).astype(np.float32),
        "order": np.tile(np.arange(E0, 0, -1, dtype=np.float32), (P, 1)),
        "cos": np.cos(angle).astype(np.float32),
        "sin": sin,
        "edge": np.concatenate([near, zero, zero, far], 1),
        "both": np.concatenate([near, zero, far], 1),
    }


def layouts(i):
    def by_feature(w):
        return w.T.reshape(KD, P, -1).transpose(1, 0, 2)

    wk, wq, wv = (i[f"L1_attn_{n}"] for n in ("Wk", "Wq", "Wv"))
    wo = i["L1_attn_Wo"].T
    attn_w = []
    for g in range(HKV):
        kv = slice(g * DH, (g + 1) * DH)
        qs = [wq[(g * GQ + h) * DH:(g * GQ + h + 1) * DH] for h in range(GQ)]
        attn_w += [by_feature(w).reshape(P, KD * DH) for w in (wk[kv], *qs, wv[kv])]
        attn_w += [wo[(g * GQ + h) * DH:(g * GQ + h + 1) * DH] for h in range(GQ)]
    small = np.concatenate([i["L1_ffn_W_gate"], i["L1_ffn_W_thr"][None, :], i["L1_ffn_A_w"].reshape(E1 * R1, D)], 0)
    return {
        "x": i["L0_attn_x"].reshape(N, D),
        "bv_q": i["L0_attn_bv_q"], "bv_k": i["L0_attn_bv_k"], "bv_v": i["L0_attn_bv_v"],
        "gate_w": by_feature(i["L0_ffn_gate_w"]),
        "gate_b": i["L0_ffn_gate_b"][:, None],
        "expert_w": i["L0_ffn_expert_w"].transpose(0, 2, 1).reshape(E0 * KD, P, D),
        "expert_b": i["L0_ffn_expert_b"],
        "attn_w": np.stack(attn_w),
        "base_w": by_feature(i["L1_ffn_W_base"]),
        "base_b": i["L1_ffn_b_base"][None, :],
        "small_w": by_feature(small),
        "thr_b": i["L1_ffn_b_thr"][None, :],
        "low_b": i["L1_ffn_B_w"].transpose(0, 2, 1).reshape(E1 * R1, D),
    }


def kernel(**inputs):
    import concourse.bacc as bacc
    from concourse.bass_utils import run_bass_kernel_spmd

    nc = bacc.Bacc("TRN2", target_bir_lowering=False, num_devices=1)
    arrays, A = {}, {}
    laid = layouts({k: np.asarray(v) for k, v in inputs.items()})
    for name, a in {**laid, **tables()}.items():
        a = np.ascontiguousarray(a)
        arrays[f"in_{name}"] = a
        A[name] = nc.dram_tensor(f"in_{name}", a.shape, mybir.dt.from_np(a.dtype), kind="ExternalInput").ap()
    A["out"] = nc.dram_tensor("out", (N, D), F32, kind="ExternalOutput").ap()
    program(nc, A)
    r = run_bass_kernel_spmd(nc, [arrays], core_ids=[0])
    return r.results[0]["out"].reshape(BATCH, T, D)
```

```python
from contextlib import ExitStack

import numpy as np

import concourse.bass as bass
from concourse import mybir
from concourse.alu_op_type import AluOpType as ALU

ACT = mybir.ActivationFunctionType
AX = mybir.AxisListType
F32 = mybir.dt.float32
F32R = mybir.dt.float32r
U32 = mybir.dt.uint32

P = 128
BATCH, T, D = 2, 512, 512
N = BATCH * T
NT = N // P
TB = T // P
KD = D // P
EPS = 1e-5
H0 = 4
E0 = 8
HQ, HKV, DH = 32, 8, 128
GQ = HQ // HKV
WIN = P * (TB - 1)
NPROJ = GQ + 2
E1, R1 = 8, 16
THRESHOLD, SCALING = 0.125, 2.0
SMALL = E1 + 1 + E1 * R1
SMALL_PAD = 256
HIDDEN = -3.0e38

RAW_SLOTS = 4
SLOT_TILES = NT + E0 - 1
SLOT_COLS = SLOT_TILES + 1


def f32(ap):
    return ap.bitcast(F32)


def mm3(pe, out, w, m, start, stop):
    pe.matmul(out, w[0], m[0], start=start, stop=False)
    pe.matmul(out, w[0], m[1], start=False, stop=False)
    return pe.matmul(out, w[1], m[0], start=False, stop=stop)


ROUTE_PARTS, ROUTE_COLS = [], 0
for width in (E0, E0 * E0, SLOT_TILES, SLOT_TILES):
    ROUTE_PARTS.append((ROUTE_COLS, ROUTE_COLS + width))
    ROUTE_COLS += width


class Steps:

    def __init__(self, eng, sem):
        self.eng, self.sem, self.n = eng, sem, 0

    def __call__(self, ins, wait=True):
        self.n += 1
        ins.then_inc(self.sem, 1)
        if wait:
            self.wait()

    def wait(self):
        self.eng.wait_ge(self.sem, self.n)


def program(nc, A):
    with ExitStack() as outer:
        def sem(name):
            return outer.enter_context(nc.semaphore(name))

        def sb(ctx, name, shape, dt=F32):
            return ctx.enter_context(nc.sbuf_tensor(name, shape, dt))

        PS = outer.enter_context(nc.psum_tensor("PS", [P, 8, 512], F32))
        ident = sb(outer, "ident", [P, P])
        xT = [sb(outer, f"xT_{s}", [P, KD, N], F32R) for s in ("hi", "lo")]
        xn_dram = nc.dram_tensor("xn_spill", [N, D], F32, kind="Internal").ap()
        slot_token = nc.dram_tensor("slot_token", [P * SLOT_COLS, 1], U32, kind="Internal").ap()
        expert_out = nc.dram_tensor("expert_out", [SLOT_TILES * P, D], F32, kind="Internal").ap()
        x1_dram = nc.dram_tensor("x1_spill", [N, D], F32, kind="Internal").ap()
        x1_rows = x1_dram.rearrange("(t p) d -> t p d", p=P)
        x1_stored = sem("x1_stored")

        block_a(nc, A, outer, sem, sb, PS, ident, xT, (xn_dram, slot_token, expert_out), x1_rows, x1_stored)
        attn = sb(outer, "attn", [P, NT, D])
        block_b(nc, A, outer, sem, sb, PS, ident, xT, attn)
        block_c(nc, A, outer, sem, sb, PS, ident, xT, attn, x1_rows, x1_stored)


class Norm:

    def __init__(self, sem, name, src, xn, xT, PS, ident, scratch):
        self.src, self.xn, self.xT, self.PS, self.ident = src, xn, xT, PS, ident
        self.st, self.mv, self.ve, self.sd, self.rs, self.tmp = scratch
        self.var_ready = sem(f"{name}_var_ready")
        self.sd_ready = sem(f"{name}_sd_ready")
        self.xn_ready = sem(f"{name}_xn_ready")
        self.turned = sem(f"{name}_turned")
        self.hi_ready = sem(f"{name}_hi_ready")
        self.lo_ready = sem(f"{name}_lo_ready")

    def statistics(self, dve, step, half, src_wait):
        ts = range(TB * half, TB * (half + 1))
        for t in ts:
            src_wait(t)
            step(dve.bn_stats(self.st[:, t, :], self.src[:, t, :]), wait=False)
        step.wait()
        for t in ts:
            step(dve.bn_aggr(self.mv[:, t, :], self.st[:, t, :]), wait=False)
        step.wait()
        h = slice(TB * half, TB * (half + 1))
        dve.tensor_scalar(self.ve[:, h], self.mv[:, h, 1], EPS, None, ALU.add).then_inc(self.var_ready, 1)

    def deviations(self, act, half):
        h = slice(TB * half, TB * (half + 1))
        act.wait_ge(self.var_ready, half + 1)
        act.activation(self.sd[:, h], self.ve[:, h], ACT.Sqrt).then_inc(self.sd_ready, 1)

    def normalise(self, dve, step, half):
        h = slice(TB * half, TB * (half + 1))
        rs, tmp = self.rs[:, h], self.tmp[:, h]
        dve.wait_ge(self.sd_ready, half + 1)
        step(dve.reciprocal(rs, self.sd[:, h]))
        step(dve.tensor_tensor(tmp, rs, rs, ALU.mult))
        step(dve.tensor_tensor(tmp, tmp, self.ve[:, h], ALU.mult))
        step(dve.tensor_scalar(tmp, tmp, -0.5, 1.5, ALU.mult, ALU.add))
        step(dve.tensor_tensor(rs, rs, tmp, ALU.mult))
        for t in range(TB * half, TB * (half + 1)):
            dve.tensor_scalar(self.xn[:, t, :], self.src[:, t, :], self.mv[:, t, 0:1], self.rs[:, t:t + 1],
                              ALU.subtract, ALU.mult).then_inc(self.xn_ready, 1)

    def turn(self, pe, t):
        pe.wait_ge(self.xn_ready, t + 1)
        if t >= 2:
            pe.wait_ge(self.lo_ready, t - 1)
        for k in range(KD):
            ins = pe.transpose(self.PS[:, t % 2, k * P:(k + 1) * P], self.xn[:, t, k * P:(k + 1) * P], self.ident[:, :])
        ins.then_inc(self.turned, 1)

    def bank(self, t):
        return self.PS[:, t % 2, :].rearrange("p (k n) -> p k n", k=KD)

    def high(self, act, t):
        act.wait_ge(self.turned, t + 1)
        act.activation(self.xT[0][:, :, t * P:(t + 1) * P], self.bank(t), ACT.Copy).then_inc(self.hi_ready, 1)

    def low(self, dve, t):
        dve.wait_ge(self.hi_ready, t + 1)
        s = slice(t * P, (t + 1) * P)
        dve.tensor_tensor(self.xT[1][:, :, s], self.bank(t), f32(self.xT[0][:, :, s]),
                          ALU.subtract).then_inc(self.lo_ready, 1)


def block_a(nc, A, outer, sem, sb, PS, ident, xT, spills, x1_rows, x1_stored):
    xn_dram, slot_token, expert_out = spills
    with ExitStack() as ctx:
        x = sb(ctx, "x", [P, NT, D])
        xn = sb(ctx, "xn", [P, NT, D])
        xv = [sb(ctx, f"xv_{s}", [P, NT, D], F32R) for s in ("hi", "lo")]
        y = sb(ctx, "y", [P, NT, D])
        st = sb(ctx, "st", [P, NT, 6])
        mv = sb(ctx, "mv", [P, NT, 2])
        ve, sd, rs, tmp8 = (sb(ctx, n, [P, NT]) for n in ("ve", "sd", "rs", "tmp8"))
        scratch = (st, mv, ve, sd, rs, tmp8)
        bv = sb(ctx, "bv", [3 * H0, P])
        bw = sb(ctx, "bw", [3 * H0, P])
        alpha = sb(ctx, "alpha", [3 * H0, 1])
        bind = sb(ctx, "bind", [P, 3 * H0])
        qk = sb(ctx, "qk", [P, H0])
        xf = [sb(ctx, f"xf{i}", [P, T]) for i in range(2)] + [y[:, TB + i, :] for i in range(2)]
        XF = len(xf)
        q = [[sb(ctx, f"q{i}_{s}", [P, T], F32R) for s in ("hi", "lo")] for i in range(2)]
        tri = sb(ctx, "tri", [P, P])
        af = y[:, 0:TB, :]
        a = [sb(ctx, f"a_{s}", [P, TB, T], F32R) for s in ("hi", "lo")]
        sT = [sb(ctx, f"sT{i}", [P, T]) for i in range(2)]
        gw = sb(ctx, "gw", [P, KD, E0])
        gwp = [sb(ctx, f"gwp_{s}", [P, KD, P], F32R) for s in ("hi", "lo")]
        gb = sb(ctx, "gb", [E0, 1])
        lT = sb(ctx, "lT", [E0, N])
        route = sb(ctx, "route", [P, ROUTE_COLS])
        order, below, steps, tiles = (route[:, a:b] for a, b in ROUTE_PARTS)
        lg, ex, oh = (sb(ctx, n, [P, NT, E0]) for n in ("lg", "ex", "oh"))
        ones = sb(ctx, "ones", [P, P])
        cum, rank = (sb(ctx, n, [P, NT, E0]) for n in ("cum", "rank"))
        n_tiles, first, end = (sb(ctx, n, [P, E0]) for n in ("n_tiles", "first", "end"))
        cmp = sb(ctx, "cmp", [P, SLOT_TILES * E0])
        slot, div, at = (sb(ctx, n, [P, NT]) for n in ("slot", "div", "at"))
        tile_e = sb(ctx, "tile_e", [P, SLOT_TILES])
        slot_i, at_i, token = (sb(ctx, n, [P, NT], U32) for n in ("slot_i", "at_i", "token"))
        tile_i = sb(ctx, "tile_i", [P, SLOT_TILES], U32)
        no_token, slot_t = (sb(ctx, n, [P, SLOT_COLS], U32) for n in ("no_token", "slot_t"))
        m8, s8 = (sb(ctx, n, [P, NT]) for n in ("m8", "s8"))
        ohT = sb(ctx, "ohT", [E0, N], F32R)
        eb = sb(ctx, "eb", [E0, D])
        ebs = [sb(ctx, f"eb_{s}", [E0, D], F32R) for s in ("hi", "lo")]
        raw = sb(ctx, "raw", [P, RAW_SLOTS, D])
        w = [[sb(ctx, f"w_{s}", [P, KD, D], F32R) for s in ("hi", "lo")], a]
        yt = [y[:, TB + i, :] for i in range(2)]
        xg = [y[:, TB + 2 + i, :] for i in range(2)]
        xgT = [[sb(ctx, f"xgT{i}_{s}", [P, KD, P], F32R) for s in ("hi", "lo")] for i in range(2)]

        x_in = [sem(f"x_in{t}") for t in range(NT)]
        const_in = sem("const_in")
        raw_in = [sem(f"raw_in{i}") for i in range(RAW_SLOTS)]
        a_dve = sem("a_dve")
        gw_lo = sem("gw_lo")
        bind_rows, bind_turned, bind_ready = sem("bind_rows"), sem("bind_turned"), sem("bind_ready")
        xv_hi, xv_lo = sem("xv_hi"), sem("xv_lo")
        xf_ready, q_hi, q_ready = sem("xf_ready"), sem("q_hi"), sem("q_ready")
        s_full, sig_done = sem("s_full"), sem("sig_done")
        a_hi, a_ready = sem("a_hi"), sem("a_ready")
        o_full, sT_ready, sT_turned, s_done = sem("o_full"), sem("sT_ready"), sem("sT_turned"), sem("s_done")
        gl_full, gl_done, lg_turned, lg_shifted, ex_ready = (
            sem(n) for n in ("gl_full", "gl_done", "lg_turned", "lg_shifted", "ex_ready"))
        oh_ready, oh_turned, ohT_ready = sem("oh_ready"), sem("oh_turned"), sem("ohT_ready")
        ones_ready = sem("ones_ready")
        counted = sem("counted")
        at_ready, slot_ready, tile_ready = sem("at_ready"), sem("slot_ready"), sem("tile_ready")
        token_ready, none_ready, none_stored = sem("token_ready"), sem("none_ready"), sem("none_stored")
        xn_stored, token_stored, slot_t_in = sem("xn_stored"), sem("token_stored"), sem("slot_t_in")
        xg_in = [sem(f"xg_in{i}") for i in range(2)]
        xg_turned, xgT_hi, xgT_lo = sem("xg_turned"), sem("xgT_hi"), sem("xgT_lo")
        w_hi, w_low = sem("w_hi"), [sem("w_lo_pool"), sem("w_lo_dve")]
        y_full, y_done = sem("y_full"), sem("y_done")
        y_stored = [sem(f"y_stored{i}") for i in range(2)]
        yg_in = [sem(f"yg_in{t}") for t in range(NT)]
        bias_full, biased, scaled = sem("bias_full"), sem("biased"), sem("scaled")
        g_ready, x1_ready = sem("g_ready"), sem("x1_ready")
        norm0 = Norm(sem, "norm0", x, xn, xT, PS, ident, scratch)
        norm1 = Norm(sem, "norm1", x, xn, xT, PS, ident, scratch)
        s_rows = xn

        x_rows = A["x"].rearrange("(t p) d -> t p d", p=P)
        consts = [(ident[:, :], A["ident"]), (tri[:, :], A["tri"]), (route[:, :], A["route"]),
                  (gw[:, :, :], A["gate_w"]), (gb[:, :], A["gate_b"]), (eb[:, :], A["expert_b"]),
                  (bv[0:H0, :], A["bv_q"]), (bv[H0:2 * H0, :], A["bv_k"]), (bv[2 * H0:3 * H0, :], A["bv_v"])]
        N_CONST = 16 * len(consts)
        heads = [(b, h) for b in range(BATCH) for h in range(H0)]
        NH = len(heads)
        YF0, YD0, XL0 = 1, 2, 1
        Y_BANK, TURN_BANK, BIAS_BANK, BIAS_BANKS = 0, 2, 4, 4
        PAIRS = (SLOT_TILES - 1) // 2
        HALF_K = KD // 2

        def expert_tiles(eng, step):
            with eng.Fori(0, PAIRS) as i:
                for par in range(2):
                    step(i, par, True)
            step(PAIRS, 0, False)

        def next_tile(i, par):
            return (i, 1) if par == 0 else (i + 1, 0)

        def col0(j):
            return min(P * j, T - 2 * P)

        block = ctx.enter_context(nc.Block())

        @block.sync
        def _(sp):
            for t in range(NT):
                sp.dma_start(x[:, t, :], x_rows[t]).then_inc(x_in[t], 16)
            sp.wait_ge(none_ready, 1)
            sp.dma_start(slot_token.rearrange("(p j) o -> p (j o)", p=P), no_token[:, :]).then_inc(none_stored, 16)
            for t in range(NT):
                sp.wait_ge(norm0.xn_ready, t + 1)
                sp.dma_start(xn_dram.rearrange("(t p) d -> t p d", p=P)[t], xn[:, t, :]).then_inc(xn_stored, 16)

            def load_weights(i, par, wait=True):
                e = sp.value_load(tile_i[0:1, bass.ds(2 * i + par, 1)], min_val=0, max_val=E0 - 1)
                for k in range(KD):
                    if wait:
                        sp.wait_ge(w_low[k // HALF_K], HALF_K * (2 * i + par - 1) + k % HALF_K + 1)
                    sp.dma_start(raw[:, k, :], A["expert_w"][bass.ds(e * KD + k, 1)].rearrange("o p n -> (o p) n")
                                 ).then_inc(raw_in[k], 16)

            def store_products(i, par):
                sp.wait_ge(y_done, YD0 + 2 * i + par + 1)
                sp.dma_start(expert_out.rearrange("(j p) d -> j p d", p=P)[bass.ds(2 * i + par, 1)].rearrange("o p d -> (o p) d"),
                             yt[par]).then_inc(y_stored[par], 16)

            sp.wait_ge(tile_ready, 1)
            load_weights(0, 0, wait=False)
            sp.wait_ge(token_stored, 16 * NT)
            sp.dma_start(slot_t[:, :], slot_token.rearrange("(p j) o -> p (j o)", p=P)).then_inc(slot_t_in, 16)
            load_weights(0, 1)
            with sp.Fori(0, PAIRS - 1) as i:
                for par in range(2):
                    load_weights(i + 1, par)
                    store_products(i, par)
            load_weights(PAIRS, 0)
            store_products(PAIRS - 1, 0)
            store_products(PAIRS - 1, 1)
            store_products(PAIRS, 0)
            for t in range(NT):
                sp.wait_ge(x1_ready, t + 1)
                sp.dma_start(x1_rows[t], x[:, t, :]).then_inc(x1_stored, 16)
            sp.wait_ge(x1_stored, 16 * NT)

        @block.gpsimd
        def _(pool):
            pool.memset(no_token[:, :], 0).then_inc(none_ready, 1)
            pool.memset(ones[:, :], 1.0).then_inc(ones_ready, 1)
            pool.iota(token[:, :], pattern=[[P, NT]], base=0, channel_multiplier=1).then_inc(token_ready, 1)

            def query_rows(n):
                b, h = heads[n]
                pool.wait_ge(norm0.lo_ready, TB * (b + 1))
                if n >= XF:
                    pool.wait_ge(q_ready, n - XF + 1)
                s = slice(b * T, (b + 1) * T)
                pool.tensor_tensor(xf[n % XF][:, :], f32(xT[0][:, h, s]), f32(xT[1][:, h, s]), ALU.add).then_inc(xf_ready, 1)

            query_rows(0)
            query_rows(1)
            for t in range(NT):
                pool.wait_ge(xv_hi, t + 1)
                pool.tensor_tensor(xv[1][:, t, :], xn[:, t, :], f32(xv[0][:, t, :]), ALU.subtract).then_inc(xv_lo, 1)
            EARLY = NH - 2
            for n in range(2, EARLY):
                query_rows(n)
            pool.wait_ge(at_ready, 1)
            pool.wait_ge(token_ready, 1)
            pool.wait_ge(none_stored, 16)
            for t in range(NT):
                pool.indirect_dma_start(slot_token, bass.IndirectOffsetOnAxis(at_i[:, t:t + 1], 0), token[:, t:t + 1],
                                        None).then_inc(token_stored, 16)
            for n in range(EARLY, NH):
                query_rows(n)

            def gather_rows(j):
                if j >= 2:
                    pool.wait_ge(xg_turned, j - 1)
                pool.indirect_dma_start(xg[j % 2], None, xn_dram, bass.IndirectOffsetOnAxis(slot_t[:, j:j + 1], 0)
                                        ).then_inc(xg_in[j % 2], 16)

            pool.wait_ge(slot_t_in, 16)
            pool.wait_ge(xn_stored, 16 * NT)
            for j in range(2):
                gather_rows(j)
            for j in range(SLOT_TILES):
                for k in range(HALF_K):
                    pool.wait_ge(w_hi, KD * j + k + 1)
                    pool.tensor_tensor(w[j % 2][1][:, k, :], raw[:, k, :], f32(w[j % 2][0][:, k, :]),
                                       ALU.subtract).then_inc(w_low[0], 1)
                if j + 2 < SLOT_TILES:
                    gather_rows(j + 2)
            pool.wait_ge(y_stored[0], 16 * (PAIRS + 2))
            pool.wait_ge(y_stored[1], 16 * (PAIRS + 1))
            for t in range(NT):
                pool.indirect_dma_start(y[:, t, :], None, expert_out, bass.IndirectOffsetOnAxis(slot_i[:, t:t + 1], 0)
                                        ).then_inc(yg_in[t], 16)
            pool.wait_ge(s_done, NH)
            for t in range(NT):
                pool.wait_ge(g_ready, t + 1)
                pool.tensor_tensor(y[:, t, :], y[:, t, :], s_rows[:, t, :], ALU.mult).then_inc(scaled, 1)

        @block.scalar
        def _(act):
            for dst, src in consts:
                act.dma_start(dst, src).then_inc(const_in, 16)
            for half in range(BATCH):
                norm0.deviations(act, half)
                for t in range(TB * half, TB * (half + 1)):
                    norm0.high(act, t)
            act.wait_ge(const_in, N_CONST)
            for b in range(BATCH):
                act.wait_ge(gl_full, b + 1)
                act.activation(lT[:, b * T:(b + 1) * T], PS[0:E0, 6 + b, :], ACT.Identity,
                               bias=gb[:, 0:1]).then_inc(gl_done, 1)
            for t in range(NT):
                act.activation(xv[0][:, t, :], xn[:, t, :], ACT.Copy).then_inc(xv_hi, 1)

            def sigmoids(n):
                for j in range(TB):
                    act.wait_ge(s_full, TB * n + j + 1)
                    if n >= 1:
                        act.wait_ge(a_ready, TB * (n - 1) + j + 1)
                    act.activation(af[:, j, P * j:], PS[:, j, P * j:], ACT.Sigmoid).then_inc(sig_done, 1)

            def scale_out(n):
                act.wait_ge(o_full, n + 1)
                act.wait_ge(bind_ready, 1)
                if n >= 2:
                    act.wait_ge(sT_turned, n - 1)
                h = heads[n][1]
                act.activation(sT[n % 2][:, :], PS[:, 4, :], ACT.Copy,
                               scale=bind[:, 2 * H0 + h:2 * H0 + h + 1]).then_inc(sT_ready, 1)

            def rows_out(n):
                b, h = heads[n]
                act.wait_ge(sT_turned, n + 1)
                act.wait_ge(xv_lo, NT)
                act.wait_ge(xn_stored, 16 * NT)
                act.activation(s_rows[:, b * TB:(b + 1) * TB, h * P:(h + 1) * P],
                               PS[:, 5, :].rearrange("p (t d) -> p t d", t=TB), ACT.Copy).then_inc(s_done, 1)

            sigmoids(0)
            for n in range(NH):
                if n + 1 < NH:
                    sigmoids(n + 1)
                if n == 0:
                    act.wait_ge(lg_shifted, 1)
                    act.activation(ex[:, :, :], lg[:, :, :], ACT.Exp).then_inc(ex_ready, 1)
                scale_out(n)
                if n >= 1:
                    rows_out(n - 1)
            rows_out(NH - 1)
            for b in range(BATCH):
                act.wait_ge(oh_turned, b + 1)
                act.activation(ohT[:, b * T:(b + 1) * T], PS[0:E0, 6 + b, :], ACT.Copy).then_inc(ohT_ready, 1)

            def high_halves(i, par, first=False):
                j = 2 * i + par
                for k in range(KD):
                    act.wait_ge(raw_in[k], 16 * j + 16)
                    if not first:
                        act.wait_ge(y_full, YF0 + j - 1)
                    act.activation(w[par][0][:, k, :], raw[:, k, :], ACT.Copy).then_inc(w_hi, 1)
                act.wait_ge(xg_turned, j + 1)
                act.activation(xgT[par][0][:, :, :], PS[:, TURN_BANK + par, :].rearrange("p (k n) -> p k n", k=KD),
                               ACT.Copy).then_inc(xgT_hi, 1)

            def step(i, par, follows):
                if follows:
                    high_halves(*next_tile(i, par))

            high_halves(0, 0, first=True)
            act.wait_ge(o_full, NH)
            expert_tiles(act, step)
            for t in range(NT):
                act.wait_ge(biased, t + 1)
                act.activation(y[:, t, :], y[:, t, :], ACT.Silu).then_inc(g_ready, 1)
            for half in range(BATCH):
                norm1.deviations(act, half)
                for t in range(TB * half, TB * (half + 1)):
                    norm1.high(act, t)

        @block.vector
        def _(dve):
            step = Steps(dve, a_dve)
            dve.sem_inc(y_done, YD0)
            dve.sem_inc(xgT_lo, XL0)
            for par in range(2):
                dve.sem_inc(y_stored[par], 16)
            norm0.statistics(dve, step, 0, lambda t: dve.wait_ge(x_in[t], 16))
            dve.wait_ge(const_in, N_CONST)
            step(dve.tensor_reduce(alpha[:, :], bv[:, :], AX.X, ALU.add, apply_absolute_value=True), wait=False)
            step(dve.tensor_scalar(bw[:, :], bv[:, :], 0.0, 2.0, ALU.is_ge, ALU.mult))
            step(dve.tensor_scalar(alpha[:, :], alpha[:, :], 1.0 / P, None, ALU.mult))
            step(dve.tensor_scalar(bw[:, :], bw[:, :], -1.0, alpha[:, 0:1], ALU.add, ALU.mult))
            step(dve.tensor_tensor(bw[:, :], bw[:, :], bv[:, :], ALU.subtract))
            dve.tensor_tensor(bw[:, :], bw[:, :], bv[:, :], ALU.add).then_inc(bind_rows, 1)
            norm0.normalise(dve, step, 0)
            norm0.statistics(dve, step, 1, lambda t: dve.wait_ge(x_in[t], 16))
            for t in range(TB):
                norm0.low(dve, t)
            norm0.normalise(dve, step, 1)
            for s in range(2):
                step(dve.memset(f32(gwp[s][:, :, :]), 0.0), wait=False)
            step.wait()
            step(dve.tensor_copy(gwp[0][:, :, 0:E0], gw[:, :, :]))
            dve.tensor_tensor(gwp[1][:, :, 0:E0], gw[:, :, :], f32(gwp[0][:, :, 0:E0]), ALU.subtract).then_inc(gw_lo, 1)
            step(dve.tensor_copy(ebs[0][:, :], eb[:, :]))
            step(dve.tensor_tensor(ebs[1][:, :], eb[:, :], f32(ebs[0][:, :]), ALU.subtract))
            dve.wait_ge(bind_turned, 1)
            step(dve.tensor_copy(bind[:, :], PS[:, 7, 0:3 * H0]))
            step(dve.tensor_tensor(qk[:, :], bind[:, 0:H0], bind[:, H0:2 * H0], ALU.mult))
            dve.tensor_scalar(qk[:, :], qk[:, :], 4.0 * P ** -0.5, None, ALU.mult).then_inc(bind_ready, 1)
            for t in range(TB, NT):
                norm0.low(dve, t)

            def bind_query(n):
                h = heads[n][1]
                dve.wait_ge(xf_ready, n + 1)
                dve.wait_ge(bind_ready, 1)
                if n >= 2:
                    dve.wait_ge(s_full, TB * (n - 1))
                qh, ql = q[n % 2]
                dve.tensor_scalar(qh[:, :], xf[n % XF][:, :], qk[:, h:h + 1], None, ALU.mult).then_inc(q_hi, 1)
                dve.wait_ge(q_hi, n + 1)
                dve.scalar_tensor_tensor(out=ql[:, :], in0=xf[n % XF][:, :], scalar=qk[:, h:h + 1],
                                         in1=f32(qh[:, :]), op0=ALU.mult, op1=ALU.subtract).then_inc(q_ready, 1)

            def split_weights(n):
                for j in range(TB):
                    dve.wait_ge(sig_done, TB * n + j + 1)
                    diag = slice(P * j, P * (j + 1))
                    step(dve.tensor_tensor(af[:, j, diag], af[:, j, diag], tri[:, :], ALU.mult), wait=False)
                step.wait()
                if n >= 1:
                    dve.wait_ge(o_full, n)
                for j in range(TB):
                    dve.tensor_copy(a[0][:, j, P * j:], af[:, j, P * j:]).then_inc(a_hi, 1)
                for j in range(TB):
                    dve.wait_ge(a_hi, TB * n + j + 1)
                    dve.tensor_tensor(a[1][:, j, P * j:], af[:, j, P * j:], f32(a[0][:, j, P * j:]),
                                      ALU.subtract).then_inc(a_ready, 1)

            wide = lambda v: v[:, :].unsqueeze(2).broadcast_to([P, NT, E0])

            def gate():
                dve.wait_ge(lg_turned, 1)
                step(dve.tensor_copy(lg[:, :, :], PS[:, 6, 0:NT * E0].rearrange("p (t e) -> p t e", t=NT)))
                step(dve.tensor_reduce(m8[:, :], lg[:, :, :], AX.X, ALU.max))
                dve.tensor_tensor(lg[:, :, :], lg[:, :, :], wide(m8), ALU.subtract).then_inc(lg_shifted, 1)
                dve.wait_ge(ex_ready, 1)
                step(dve.tensor_reduce(s8[:, :], ex[:, :, :], AX.X, ALU.add))
                step(dve.reciprocal(s8[:, :], s8[:, :]))
                step(dve.tensor_tensor(ex[:, :, :], ex[:, :, :], wide(s8), ALU.mult))
                step(dve.tensor_reduce(m8[:, :], ex[:, :, :], AX.X, ALU.max))
                step(dve.tensor_tensor(oh[:, :, :], ex[:, :, :], wide(m8), ALU.is_ge))
                step(dve.tensor_tensor(oh[:, :, :], oh[:, :, :], order[:, :].unsqueeze(1).broadcast_to([P, NT, E0]), ALU.mult))
                step(dve.tensor_reduce(m8[:, :], oh[:, :, :], AX.X, ALU.max))
                dve.tensor_tensor(ex[:, :, :], oh[:, :, :], wide(m8), ALU.is_equal).then_inc(oh_ready, 1)

            def routing():
                before, total = (PS[:, 7, n * NT * E0:(n + 1) * NT * E0].rearrange("p (t e) -> p t e", t=NT) for n in range(2))
                across = lambda v, n: v.unsqueeze(1).broadcast_to([P, n, v.shape[1]])
                along = lambda v, n: v.unsqueeze(2).broadcast_to([P, v.shape[1], n])
                cube = lambda n, m: cmp[:, 0:n * m].rearrange("p (n m) -> p n m", n=n)
                dve.wait_ge(counted, 1)
                step(dve.tensor_copy(cum[:, :, :], total))
                for t in range(1, NT):
                    step(dve.tensor_tensor(cum[:, t, :], cum[:, t, :], cum[:, t - 1, :], ALU.add))
                step(dve.tensor_tensor(rank[:, :, :], cum[:, :, :], total, ALU.subtract))
                step(dve.tensor_tensor(rank[:, :, :], rank[:, :, :], before, ALU.add))
                step(dve.tensor_tensor(cube(E0, NT), along(cum[:, NT - 1, :], NT), across(steps[:, 0:NT], E0), ALU.is_gt))
                step(dve.tensor_reduce(n_tiles[:, :], cube(E0, NT), AX.X, ALU.add))
                step(dve.tensor_tensor(cube(E0, E0), below.rearrange("p (e f) -> p e f", e=E0), across(n_tiles[:, :], E0), ALU.mult))
                step(dve.tensor_reduce(first[:, :], cube(E0, E0), AX.X, ALU.add))
                step(dve.tensor_tensor(end[:, :], first[:, :], n_tiles[:, :], ALU.add))
                step(dve.tensor_tensor(cube(SLOT_TILES, E0), across(end[:, :], SLOT_TILES), along(tiles, E0), ALU.is_le))
                step(dve.tensor_reduce(tile_e[:, :], cube(SLOT_TILES, E0), AX.X, ALU.add))
                step(dve.tensor_scalar(tile_e[:, :], tile_e[:, :], float(E0 - 1), None, ALU.min))
                dve.tensor_copy(tile_i[:, :], tile_e[:, :]).then_inc(tile_ready, 1)
                step(dve.tensor_scalar(first[:, :], first[:, :], float(P), -1.0, ALU.mult, ALU.add))
                step(dve.tensor_tensor(rank[:, :, :], rank[:, :, :], across(first[:, :], NT), ALU.add))
                step(dve.tensor_tensor(rank[:, :, :], rank[:, :, :], ex[:, :, :], ALU.mult))
                step(dve.tensor_reduce(slot[:, :], rank[:, :, :], AX.X, ALU.add))
                dve.tensor_copy(slot_i[:, :], slot[:, :]).then_inc(slot_ready, 1)
                step(dve.tensor_tensor(cube(NT, SLOT_TILES - 1), along(slot[:, :], SLOT_TILES - 1), across(steps[:, 1:], NT), ALU.is_ge))
                step(dve.tensor_reduce(div[:, :], cube(NT, SLOT_TILES - 1), AX.X, ALU.add))
                step(dve.tensor_scalar(at[:, :], slot[:, :], float(SLOT_COLS), None, ALU.mult))
                step(dve.tensor_scalar(div[:, :], div[:, :], float(P * SLOT_COLS - 1), None, ALU.mult))
                step(dve.tensor_tensor(at[:, :], at[:, :], div[:, :], ALU.subtract))
                dve.tensor_copy(at_i[:, :], at[:, :]).then_inc(at_ready, 1)

            bind_query(0)
            for n in range(NH):
                if n + 1 < NH:
                    bind_query(n + 1)
                split_weights(n)
                if n == 0:
                    gate()
                if n == 1:
                    routing()

            def low_halves(i, par):
                j = 2 * i + par
                for k in range(HALF_K, KD):
                    dve.wait_ge(w_hi, KD * j + k + 1)
                    dve.tensor_tensor(w[par][1][:, k, :], raw[:, k, :], f32(w[par][0][:, k, :]), ALU.subtract).then_inc(w_low[1], 1)
                dve.wait_ge(xgT_hi, j + 1)
                dve.tensor_tensor(xgT[par][1][:, :, :], PS[:, TURN_BANK + par, :].rearrange("p (k n) -> p k n", k=KD),
                                  f32(xgT[par][0][:, :, :]), ALU.subtract).then_inc(xgT_lo, 1)

            def tile_step(i, par, follows):
                if follows:
                    low_halves(*next_tile(i, par))
                dve.wait_ge(y_full, YF0 + 2 * i + par + 1)
                dve.wait_ge(y_stored[par], 16 * i + 16)
                dve.tensor_copy(yt[par], PS[:, Y_BANK + par, :]).then_inc(y_done, 1)

            low_halves(0, 0)
            expert_tiles(dve, tile_step)

            def add_bias(t):
                dve.wait_ge(bias_full, t + 1)
                dve.wait_ge(yg_in[t], 16)
                dve.tensor_tensor(y[:, t, :], y[:, t, :], PS[:, BIAS_BANK + t % BIAS_BANKS, :], ALU.add).then_inc(biased, 1)

            def add_residual(t):
                dve.wait_ge(scaled, t + 1)
                dve.tensor_tensor(x[:, t, :], x[:, t, :], y[:, t, :], ALU.add).then_inc(x1_ready, 1)

            for t in range(TB):
                add_bias(t)
            for t in range(TB):
                add_residual(t)
                add_bias(TB + t)
            norm1.statistics(dve, step, 0, lambda t: dve.wait_ge(x1_ready, t + 1))
            norm1.normalise(dve, step, 0)
            for t in range(TB, NT):
                add_residual(t)
            norm1.statistics(dve, step, 1, lambda t: dve.wait_ge(x1_ready, t + 1))
            for t in range(TB):
                norm1.low(dve, t)
            norm1.normalise(dve, step, 1)
            for t in range(TB, NT):
                norm1.low(dve, t)

        @block.tensor
        def _(pe):
            pe.sem_inc(y_full, YF0)
            pe.wait_ge(const_in, N_CONST)
            pe.wait_ge(bind_rows, 1)
            pe.transpose(PS[:, 7, 0:3 * H0], bw[:, :], ident[0:3 * H0, 0:3 * H0]).then_inc(bind_turned, 1)
            for t in range(NT):
                norm0.turn(pe, t)
            pe.wait_ge(gw_lo, 1)
            pe.wait_ge(bind_ready, 1)
            for b in range(BATCH):
                pe.wait_ge(norm0.lo_ready, TB * (b + 1))
                for k in range(KD):
                    ins = mm3(pe, PS[:, 6 + b, :], [g[:, k, :] for g in gwp],
                              [v[:, k, b * T:(b + 1) * T] for v in xT], k == 0, k == KD - 1)
                ins.then_inc(gl_full, 1)

            def scores(n):
                b, h = heads[n]
                pe.wait_ge(q_ready, n + 1)
                for j in range(TB):
                    if n >= 1:
                        pe.wait_ge(sig_done, TB * (n - 1) + j + 1)
                    keys = slice(b * T + j * P, b * T + (j + 1) * P)
                    mm3(pe, PS[:, j, col0(j):], [v[:, h, keys] for v in xT],
                        [v[:, col0(j):] for v in q[n % 2]], True, True).then_inc(s_full, 1)

            def outputs(n):
                b, h = heads[n]
                pe.wait_ge(xv_lo, NT)
                if n >= 1:
                    pe.wait_ge(sT_ready, n)
                for j in range(TB):
                    pe.wait_ge(a_ready, TB * n + j + 1)
                    ins = mm3(pe, PS[:, 4, P * j:], [v[:, b * TB + j, h * P:(h + 1) * P] for v in xv],
                              [v[:, j, P * j:] for v in a], j == 0, j == TB - 1)
                ins.then_inc(o_full, 1)

            def turn_out(n):
                pe.wait_ge(sT_ready, n + 1)
                if n >= 1:
                    pe.wait_ge(s_done, n)
                for t in range(TB):
                    ins = pe.transpose(PS[:, 5, t * P:(t + 1) * P], sT[n % 2][:, t * P:(t + 1) * P], ident[:, :])
                ins.then_inc(sT_turned, 1)

            scores(0)
            for n in range(NH):
                if n + 1 < NH:
                    scores(n + 1)
                if n == 0:
                    pe.wait_ge(gl_done, BATCH)
                    for t in range(NT):
                        ins = pe.transpose(PS[:, 6, t * E0:(t + 1) * E0], lT[:, t * P:(t + 1) * P], ident[0:E0, 0:E0])
                    ins.then_inc(lg_turned, 1)
                outputs(n)
                if n == 1:
                    pe.wait_ge(oh_ready, 1)
                    pe.wait_ge(ones_ready, 1)
                    pe.matmul(PS[:, 7, 0:NT * E0], tri[:, :], ex[:, :, :], start=True, stop=True)
                    pe.matmul(PS[:, 7, NT * E0:2 * NT * E0], ones[:, :], ex[:, :, :], start=True, stop=True).then_inc(counted, 1)
                if n >= 1:
                    turn_out(n - 1)
            turn_out(NH - 1)
            pe.wait_ge(slot_ready, 1)
            for b in range(BATCH):
                for t in range(TB):
                    ins = pe.transpose(PS[0:E0, 6 + b, t * P:(t + 1) * P], ex[:, b * TB + t, :], ident[:, :])
                ins.then_inc(oh_turned, 1)

            def turn_rows(i, par, first=False):
                j = 2 * i + par
                pe.wait_ge(xg_in[par], 16 * i + 16)
                if not first:
                    pe.wait_ge(xgT_lo, XL0 + j - 1)
                for k in range(KD):
                    ins = pe.transpose(PS[:, TURN_BANK + par, k * P:(k + 1) * P], xg[par][:, k * P:(k + 1) * P], ident[:, :])
                ins.then_inc(xg_turned, 1)

            def step(i, par, follows):
                if follows:
                    turn_rows(*next_tile(i, par))
                j = 2 * i + par
                pe.wait_ge(xgT_lo, XL0 + j + 1)
                for low in w_low:
                    pe.wait_ge(low, HALF_K * (j + 1))
                pe.wait_ge(y_done, YD0 + j - 1)
                for k in range(KD):
                    ins = mm3(pe, PS[:, Y_BANK + par, :], [v[:, k, :] for v in xgT[par]], [v[:, k, :] for v in w[par]],
                              k == 0, k == KD - 1)
                ins.then_inc(y_full, 1)

            def bias(t):
                pe.wait_ge(ohT_ready, BATCH)
                if t >= BIAS_BANKS:
                    pe.wait_ge(biased, t - BIAS_BANKS + 1)
                bank = PS[:, BIAS_BANK + t % BIAS_BANKS, :]
                pe.matmul(bank, ohT[:, t * P:(t + 1) * P], ebs[0][:, :], start=True, stop=False)
                pe.matmul(bank, ohT[:, t * P:(t + 1) * P], ebs[1][:, :], start=False, stop=True).then_inc(bias_full, 1)

            pe.wait_ge(sig_done, TB * NH)
            turn_rows(0, 0, first=True)
            expert_tiles(pe, step)
            for t in range(NT):
                bias(t)
            for t in range(NT):
                norm1.turn(pe, t)


def block_b(nc, A, outer, sem, sb, PS, ident, xT, attn):
    with ExitStack() as ctx:
        cos, sin = (sb(ctx, n, [P, T]) for n in ("cos", "sin"))
        edge = sb(ctx, "edge", [P, TB * P])
        both = sb(ctx, "both", [P, WIN])
        raw = sb(ctx, "rawb", [P, RAW_SLOTS, D])
        wp = [[sb(ctx, f"wp{j}_{s}", [P, D], F32R) for s in ("hi", "lo")] for j in range(NPROJ)]
        wo = [[[sb(ctx, f"wo{o}{h}_{s}", [P, D], F32R) for s in ("hi", "lo")] for h in range(GQ)] for o in range(2)]
        kT = [[sb(ctx, f"kT{b}_{s}", [P, T + 2 * P], F32R) for s in ("hi", "lo")] for b in range(BATCH)]
        qT = [[sb(ctx, f"qT{b}_{s}", [P, GQ, T], F32R) for s in ("hi", "lo")] for b in range(BATCH)]
        vT = sb(ctx, "vT", [P, T])
        v = [sb(ctx, f"v_{s}", [P, TB, DH], F32R) for s in ("hi", "lo")]
        rot = [sb(ctx, f"rot{i}", [P, T]) for i in range(2)]
        full = [sb(ctx, f"full{i}", [P, T]) for i in range(2)]
        pr = [sb(ctx, f"pr{i}", [P, GQ, WIN]) for i in range(2)]
        pT = [sb(ctx, f"pT_{s}", [P, TB - 1, GQ * P], F32R) for s in ("hi", "lo")]
        oT = [sb(ctx, f"oT_{s}", [P, GQ * P], F32R) for s in ("hi", "lo")]
        nmax, rsum, rinv = ([sb(ctx, f"{n}{i}", [P, GQ]) for i in range(2)] for n in ("nmax", "rsum", "rinv"))

        table_in = sem("table_in")
        raw_in = [sem(f"rawb_in{i}") for i in range(RAW_SLOTS)]
        wb_hi, wb_lo = sem("wb_hi"), sem("wb_lo")
        proj_full = sem("proj_full")
        rope_read, roped = sem("rope_read"), sem("roped")
        kq_hi, kq_lo = sem("kq_hi"), sem("kq_lo")
        vT_done, v_turned, v_hi, v_lo = (sem(n) for n in ("vT_done", "v_turned", "v_hi", "v_lo"))
        sb_full, max_done, exp_done = sem("sb_full"), sem("max_done"), sem("exp_done")
        rinv_done = sem("rinv_done")
        max_wait, norm_wait = sem("max_wait"), sem("norm_wait")
        pr_first, pr_last = sem("pr_first"), sem("pr_last")
        pT_full, pT_hi, pT_lo = sem("pT_full"), sem("pT_hi"), sem("pT_lo")
        pv_full, oT_hi, oT_lo = sem("pv_full"), sem("oT_hi"), sem("oT_lo")
        wo_full, wo_done = sem("wo_full"), sem("wo_done")

        SEQ = NPROJ + GQ
        TURNS = HKV // 2
        PP = 2 * BATCH
        KQ = NPROJ
        HALF = DH // 2
        SCALE = float(np.float32(1.0) / np.sqrt(np.float32(DH)))
        SC, TW, PJ, OB = (0, 1, 2, 0), 3, 5, 7
        WB0, KQ0, PT0, WD0, WF0 = RAW_SLOTS, 2, 2, NT, 1
        V_, ALL, FRONT, BACK = NPROJ - 1, range(KD), range(KD // 2), range(KD // 2, KD)
        FILLERS = {0: ((0, ALL), (1, ALL)), 1: ((2, ALL), (3, ALL)), 2: ((4, FRONT), (4, BACK)), 3: ((V_, FRONT), (V_, BACK))}
        ROPES = {0: (0, 1), 1: (2, 3), 2: (None, 4), 3: (None, None)}
        SPLITS = {(0, 1): (0, 1), (0, 2): (2, 3), (0, 3): (4,), (1, 0): (5, 6), (1, 1): (7,), (1, 2): (8,), (1, 3): (9,)}

        def mask(i):
            return {0: edge[:, 0:WIN], TB - 1: edge[:, P:P + WIN]}.get(i, both[:, :])

        def keys(b, i):
            first = ((i + 1) % TB) * P
            return [t[:, first:first + WIN] for t in kT[b]]

        def kq_count(p, j):
            return KQ * p + j + 2

        def kq_before(p, j):
            return kq_count(p, j - 2) if j >= 2 else kq_count(p - 1, j + GQ - 1)

        def turned_bank(pp, i, c):
            return TW + ((TB - 1) * (TB * pp + i) + c) % 2

        def following(pp, i):
            return (pp, i + 1) if i + 1 < TB else (pp + 1, 0)

        def stages(last):
            for pp in range(PP):
                for i in range(TB):
                    pair_follows = not (last and pp == PP - 1)
                    yield pp, i, pair_follows or i + 1 < TB, pair_follows

        def splits(gg, pp, i, last):
            odd, b = divmod(pp, BATCH)
            if last and odd == 1:
                return
            for r in SPLITS.get((b, i), ()):
                yield weight_tile(gg, odd + 1, r)

        def weight_tile(gg, go, r):
            c = SEQ * go + r
            return (2 * SEQ * gg + c, c % RAW_SLOTS, (2 * SEQ // RAW_SLOTS) * gg + c // RAW_SLOTS + 1,
                    2 * gg + go, r, wp[r] if r < NPROJ else wo[go % 2][r - NPROJ])

        block = ctx.enter_context(nc.Block())

        @block.sync
        def _(sp):
            for dst, src in ((cos[:, :], A["cos"]), (sin[:, :], A["sin"]), (edge[:, :], A["edge"]), (both[:, :], A["both"])):
                sp.dma_start(dst, src).then_inc(table_in, 16)
            with sp.Fori(0, TURNS) as gg:
                for c in range(2 * SEQ):
                    sp.wait_ge(wb_lo, 2 * SEQ * gg + c + 1)
                    sp.dma_start(raw[:, c % RAW_SLOTS, :],
                                 A["attn_w"][bass.ds(2 * SEQ * gg + c, 1)].rearrange("o p n -> (o p) n")
                                 ).then_inc(raw_in[c % RAW_SLOTS], 16)

        @block.gpsimd
        def _(pool):
            pool.sem_inc(wb_lo, WB0)
            pool.sem_inc(kq_lo, KQ0)

            def split_low(tile):
                at, slot, _, _, _, halves = tile
                pool.wait_ge(wb_hi, at + 1)
                pool.tensor_tensor(halves[1][:, :], raw[:, slot, :], f32(halves[0][:, :]), ALU.subtract).then_inc(wb_lo, 1)

            def rope_sum(gg, pp, j):
                m, p = (NPROJ - 1) * pp + j, PP * gg + pp
                pool.wait_ge(rope_read, 3 * ((NPROJ - 1) * p + j + 1))
                pool.tensor_tensor(full[m % 2][:, :], full[m % 2][:, :], rot[m % 2][:, :], ALU.add).then_inc(roped, 1)

            def rope_low(gg, pp, j):
                m, p, b = (NPROJ - 1) * pp + j, PP * gg + pp, pp % BATCH
                if j == 0:
                    for at, n in ((0, T), (T, 2 * P)):
                        pool.wait_ge(kq_hi, kq_count(p, 0) - (at == 0))
                        pool.tensor_tensor(kT[b][1][:, at:at + n], full[m % 2][:, 0:n], f32(kT[b][0][:, at:at + n]),
                                           ALU.subtract).then_inc(kq_lo, 1)
                else:
                    pool.wait_ge(kq_hi, kq_count(p, j))
                    pool.tensor_tensor(qT[b][1][:, j - 1, :], full[m % 2][:, :], f32(qT[b][0][:, j - 1, :]),
                                       ALU.subtract).then_inc(kq_lo, 1)

            def norm_first(gg, pp, i):
                s, par = TB * (PP * gg + pp) + i, (TB * pp + i) % 2
                pool.wait_ge(rinv_done, 2 * s + 1)
                pool.sem_inc(norm_wait, 1)
                for h in range(2):
                    pool.tensor_scalar(pr[par][:, h, :], pr[par][:, h, :], rinv[par][:, h:h + 1], 1.0,
                                       ALU.mult, ALU.mult).then_inc(pr_first, 1)

            def turn(gg, last):
                for pp, i, stage_follows, pair_follows in stages(last):
                    ropes = [j for j in ROPES[i] if j is not None and pair_follows]
                    if stage_follows:
                        norm_first(gg, *following(pp, i))
                    for j in ropes:
                        rope_sum(gg, pp + 1, j)
                    for j in ropes:
                        rope_low(gg, pp + 1, j)
                    for tile in splits(gg, pp, i, last):
                        split_low(tile)

            for r in range(NPROJ):
                split_low(weight_tile(0, 0, r))
            for j in range(NPROJ - 1):
                rope_sum(0, 0, j)
                rope_low(0, 0, j)
            for r in range(NPROJ, SEQ):
                split_low(weight_tile(0, 0, r))
            norm_first(0, 0, 0)
            with pool.Fori(0, TURNS - 1) as gg:
                turn(gg, False)
            turn(TURNS - 1, True)

        @block.scalar
        def _(act):
            def split_high(tile):
                at, slot, loads, g, r, halves = tile
                act.wait_ge(raw_in[slot], 16 * loads)
                if not (isinstance(g, int) and g == 0):
                    if r < NPROJ:
                        act.wait_ge(proj_full, NPROJ * (2 * g - 1) + r + 1)
                    else:
                        act.wait_ge(wo_full, WF0 + BATCH * TB * (g - 1))
                act.activation(halves[0][:, :], raw[:, slot, :], ACT.Copy).then_inc(wb_hi, 1)

            def rope_high(gg, pp, j):
                m, p, b = (NPROJ - 1) * pp + j, PP * gg + pp, pp % BATCH
                act.wait_ge(roped, (NPROJ - 1) * p + j + 1)
                if j == 0:
                    act.activation(kT[b][0][:, 0:T], full[m % 2][:, :], ACT.Copy).then_inc(kq_hi, 1)
                    act.activation(kT[b][0][:, T:], full[m % 2][:, 0:2 * P], ACT.Copy).then_inc(kq_hi, 1)
                else:
                    act.activation(qT[b][0][:, j - 1, :], full[m % 2][:, :], ACT.Copy).then_inc(kq_hi, 1)

            def value_out(gg, pp):
                p = PP * gg + pp
                act.wait_ge(proj_full, NPROJ * (p + 1))
                act.activation(vT[:, :], PS[:, PJ + V_ % 2, :], ACT.Copy).then_inc(vT_done, 1)

            def value_high(gg, pp):
                p = PP * gg + pp
                act.wait_ge(v_turned, p + 1)
                act.activation(v[0][:, :, :], PS[:, PJ + V_ % 2, :].rearrange("p (t d) -> p t d", t=TB), ACT.Copy).then_inc(v_hi, 1)

            def exps(gg, pp, i, hs):
                s, par = TB * (PP * gg + pp) + i, (TB * pp + i) % 2
                for h in hs:
                    act.wait_ge(max_done, GQ * s + h + 1)
                    act.activation(pr[par][:, h, :], PS[:, SC[h], 0:WIN], ACT.Exp, bias=nmax[par][:, h:h + 1], scale=-1.0,
                                   accum_out=rsum[par][:, h:h + 1]).then_inc(exp_done, 1)

            def turned_high(gg, pp, i, chunks):
                s = TB * (PP * gg + pp) + i
                for c in chunks:
                    bank = turned_bank(pp, i, c)
                    act.wait_ge(pT_full, (TB - 1) * s + c + 1)
                    act.activation(pT[0][:, c, :], PS[:, bank, :], ACT.Copy).then_inc(pT_hi, 1)

            def out_high(gg, pp, i):
                s = TB * (PP * gg + pp) + i
                act.wait_ge(pv_full, s + 1)
                act.activation(oT[0][:, :], PS[:, OB, :], ACT.Copy).then_inc(oT_hi, 1)

            def turn(gg, last):
                for pp, i, stage_follows, pair_follows in stages(last):
                    if stage_follows:
                        exps(gg, *following(pp, i), range(GQ))
                    out_high(gg, pp, i)
                    if i == TB - 1 and pair_follows:
                        value_out(gg, pp + 1)
                    if stage_follows:
                        turned_high(gg, *following(pp, i), (0, 1))
                    for j in ROPES[i]:
                        if j is not None and pair_follows:
                            rope_high(gg, pp + 1, j)
                    if stage_follows:
                        turned_high(gg, *following(pp, i), (2,))
                    if i == TB - 1 and pair_follows:
                        value_high(gg, pp + 1)
                    for tile in splits(gg, pp, i, last):
                        split_high(tile)

            for r in range(NPROJ):
                split_high(weight_tile(0, 0, r))
            for j in range(NPROJ - 1):
                rope_high(0, 0, j)
            value_out(0, 0)
            value_high(0, 0)
            for r in range(NPROJ, SEQ):
                split_high(weight_tile(0, 0, r))
            exps(0, 0, 0, range(GQ))
            turned_high(0, 0, 0, range(TB - 1))
            with act.Fori(0, TURNS - 1) as gg:
                turn(gg, False)
            turn(TURNS - 1, True)

        @block.vector
        def _(dve):
            dve.sem_inc(pT_lo, PT0)
            for t in range(NT):
                dve.memset(attn[:, t, :], 0.0).then_inc(wo_done, 1)
            dve.wait_ge(table_in, 64)

            def rope(gg, pp, j):
                m, p = (NPROJ - 1) * pp + j, PP * gg + pp
                dve.wait_ge(proj_full, NPROJ * p + j + 1)
                dve.wait_ge(kq_lo, KQ0 + kq_before(p, j))
                dve.tensor_tensor(full[m % 2][:, :], PS[:, PJ + j % 2, :], cos[:, :], ALU.mult).then_inc(rope_read, 1)
                for to, at in ((0, HALF), (HALF, 0)):
                    dve.tensor_tensor(rot[m % 2][to:to + HALF, :], PS[at:at + HALF, PJ + j % 2, :], sin[to:to + HALF, :],
                                      ALU.mult).then_inc(rope_read, 1)

            def value_low(gg, pp):
                p = PP * gg + pp
                dve.wait_ge(v_hi, p + 1)
                dve.tensor_tensor(v[1][:, :, :], PS[:, PJ + V_ % 2, :].rearrange("p (t d) -> p t d", t=TB), f32(v[0][:, :, :]),
                                  ALU.subtract).then_inc(v_lo, 1)

            def maxima(gg, pp, i, hs):
                s, par = TB * (PP * gg + pp) + i, (TB * pp + i) % 2
                for h in hs:
                    dve.wait_ge(sb_full, GQ * s + h + 1)
                    dve.sem_inc(max_wait, 1)
                    dve.tensor_tensor_reduce(PS[:, SC[h], 0:WIN], PS[:, SC[h], 0:WIN], mask(i), -SCALE, 3.0e38,
                                             ALU.add, ALU.min, nmax[par][:, h:h + 1]).then_inc(max_done, 1)

            def inverses(gg, pp, i, half):
                s, par = TB * (PP * gg + pp) + i, (TB * pp + i) % 2
                hs = slice(2 * half, 2 * half + 2)
                dve.wait_ge(exp_done, GQ * s + 2 * half + 2)
                dve.reciprocal(rinv[par][:, hs], rsum[par][:, hs]).then_inc(rinv_done, 1)

            def norm_last(gg, pp, i):
                s, par = TB * (PP * gg + pp) + i, (TB * pp + i) % 2
                dve.wait_ge(rinv_done, 2 * s + 2)
                for h in (2, 3):
                    dve.tensor_scalar(pr[par][:, h, :], pr[par][:, h, :], rinv[par][:, h:h + 1], None,
                                      ALU.mult).then_inc(pr_last, 1)

            def turned_low(gg, pp, i, chunks):
                s = TB * (PP * gg + pp) + i
                for c in chunks:
                    bank = turned_bank(pp, i, c)
                    dve.wait_ge(pT_hi, (TB - 1) * s + c + 1)
                    dve.tensor_tensor(pT[1][:, c, :], PS[:, bank, :], f32(pT[0][:, c, :]), ALU.subtract).then_inc(pT_lo, 1)

            def out_low(gg, pp, i):
                s = TB * (PP * gg + pp) + i
                dve.wait_ge(oT_hi, s + 1)
                dve.tensor_tensor(oT[1][:, :], PS[:, OB, :], f32(oT[0][:, :]), ALU.subtract).then_inc(oT_lo, 1)

            def accumulate(gg, pp, i):
                s, t = TB * (PP * gg + pp) + i, TB * (pp % BATCH) + i
                dve.wait_ge(wo_full, WF0 + s + 1)
                dve.wait_ge(wo_done, WD0 + s + 1 - NT)
                dve.tensor_tensor(attn[:, t, :], PS[:, OB, :], attn[:, t, :], ALU.add).then_inc(wo_done, 1)

            def turn(gg, last):
                for pp, i, stage_follows, pair_follows in stages(last):
                    ra, rb = ROPES[i] if pair_follows else (None, None)
                    if stage_follows:
                        maxima(gg, *following(pp, i), (0, 1, 2))
                        inverses(gg, *following(pp, i), 0)
                        maxima(gg, *following(pp, i), (3,))
                    if ra is not None:
                        rope(gg, pp + 1, ra)
                    if stage_follows:
                        inverses(gg, *following(pp, i), 1)
                        norm_last(gg, *following(pp, i))
                    out_low(gg, pp, i)
                    if rb is not None:
                        rope(gg, pp + 1, rb)
                    if stage_follows:
                        turned_low(gg, *following(pp, i), (0, 1))
                    accumulate(gg, pp, i)
                    if stage_follows:
                        turned_low(gg, *following(pp, i), (2,))
                    if i == TB - 1 and pair_follows:
                        value_low(gg, pp + 1)

            for j in range(NPROJ - 1):
                rope(0, 0, j)
            value_low(0, 0)
            maxima(0, 0, 0, (0, 1, 2))
            inverses(0, 0, 0, 0)
            maxima(0, 0, 0, (3,))
            inverses(0, 0, 0, 1)
            norm_last(0, 0, 0)
            turned_low(0, 0, 0, range(TB - 1))
            with dve.Fori(0, TURNS - 1) as gg:
                turn(gg, False)
            turn(TURNS - 1, True)

        @block.tensor
        def _(pe):
            pe.sem_inc(wo_full, WF0)

            def project(gg, pp, j, ks=ALL):
                p, b = PP * gg + pp, pp % BATCH
                go = pp // BATCH
                if ks[0] == 0:
                    if not (isinstance(p, int) and p == 0 and j < 2):
                        pe.wait_ge(v_lo, p) if j == 1 else pe.wait_ge(rope_read, 3 * ((NPROJ - 1) * p + max(j - 1, 0)))
                    pe.wait_ge(wb_lo, WB0 + 2 * SEQ * gg + SEQ * go + j + 1)
                for k in ks:
                    ins = mm3(pe, PS[:, PJ + j % 2, :], [w[:, k * DH:(k + 1) * DH] for w in wp[j]],
                              [x[:, k, b * T:(b + 1) * T] for x in xT], k == 0, k == KD - 1)
                if ks[-1] == KD - 1:
                    ins.then_inc(proj_full, 1)

            def turn_values(gg, pp):
                p = PP * gg + pp
                pe.wait_ge(vT_done, p + 1)
                for t in range(TB):
                    ins = pe.transpose(PS[:, PJ + V_ % 2, t * P:(t + 1) * P], vT[:, t * P:(t + 1) * P], ident[:, :])
                ins.then_inc(v_turned, 1)

            def scores(gg, pp, i, hs):
                s, p, b = TB * (PP * gg + pp) + i, PP * gg + pp, pp % BATCH
                for h in hs:
                    pe.wait_ge(kq_lo, KQ0 + kq_count(p, h + 1))
                    if h == 3:
                        pe.wait_ge(exp_done, GQ * s + 1)
                    elif not (isinstance(s, int) and s == 0):
                        pe.wait_ge(exp_done, GQ * (s - 1) + (GQ if h == 0 else h + 1))
                    mm3(pe, PS[:, SC[h], 0:WIN], [q[:, h, i * P:(i + 1) * P] for q in qT[b]], keys(b, i),
                        True, True).then_inc(sb_full, 1)

            def turn_weights(gg, pp, i, chunks):
                s, par = TB * (PP * gg + pp) + i, (TB * pp + i) % 2
                if chunks[0] == 0:
                    pe.wait_ge(pr_first, 2 * s + 2)
                    pe.wait_ge(pr_last, 2 * s + 2)
                for c in chunks:
                    bank = turned_bank(pp, i, c)
                    pe.wait_ge(pT_lo, PT0 + (TB - 1) * s + c - 1)
                    for h in range(GQ):
                        ins = pe.transpose(PS[:, bank, h * P:(h + 1) * P], pr[par][:, h, c * P:(c + 1) * P], ident[:, :])
                    ins.then_inc(pT_full, 1)

            def values(gg, pp, i):
                s, p = TB * (PP * gg + pp) + i, PP * gg + pp
                pe.wait_ge(v_lo, p + 1)
                pe.wait_ge(wo_done, WD0 + s)
                for c in range(TB - 1):
                    pe.wait_ge(pT_lo, PT0 + (TB - 1) * s + c + 1)
                    tile = (i + 1 + c) % TB
                    ins = mm3(pe, PS[:, OB, :], [x[:, tile, :] for x in v], [x[:, c, :] for x in pT], c == 0, c == TB - 2)
                ins.then_inc(pv_full, 1)

            def out_project(gg, pp, i):
                s, go = TB * (PP * gg + pp) + i, pp // BATCH
                pe.wait_ge(oT_lo, s + 1)
                pe.wait_ge(wb_lo, WB0 + 2 * SEQ * gg + SEQ * (go + 1))
                for h in range(GQ):
                    ins = mm3(pe, PS[:, OB, :], [x[:, h * P:(h + 1) * P] for x in oT], [x[:, :] for x in wo[go][h]],
                              h == 0, h == GQ - 1)
                ins.then_inc(wo_full, 1)

            def turn(gg, last):
                for pp, i, stage_follows, pair_follows in stages(last):
                    (ja, ka), (jb, kb) = FILLERS[i]
                    if stage_follows:
                        scores(gg, *following(pp, i), (0, 1, 2))
                    if pair_follows:
                        project(gg, pp + 1, ja, ka)
                    if stage_follows:
                        scores(gg, *following(pp, i), (3,))
                    values(gg, pp, i)
                    if pair_follows:
                        project(gg, pp + 1, jb, kb)
                    if stage_follows:
                        turn_weights(gg, *following(pp, i), (0, 1))
                    out_project(gg, pp, i)
                    if i == TB - 1 and pair_follows:
                        turn_values(gg, pp + 1)
                    if stage_follows:
                        turn_weights(gg, *following(pp, i), (2,))

            for j in range(NPROJ):
                project(0, 0, j)
            turn_values(0, 0)
            scores(0, 0, 0, range(GQ))
            turn_weights(0, 0, 0, range(TB - 1))
            with pe.Fori(0, TURNS - 1) as gg:
                turn(gg, False)
            turn(TURNS - 1, True)


def block_c(nc, A, outer, sem, sb, PS, ident, xT, attn, x1_rows, x1_stored):
    with ExitStack() as ctx:
        x = sb(ctx, "x1", [P, NT, D])
        sw_raw, sw = sb(ctx, "sw_raw", [P, KD, SMALL]), [sb(ctx, f"sw_{s}", [P, KD, SMALL_PAD], F32R) for s in ("hi", "lo")]
        bw_raw, bw = sb(ctx, "bw_raw", [P, KD, D]), [sb(ctx, f"basew_{s}", [P, KD, D], F32R) for s in ("hi", "lo")]
        lw_raw, lw = sb(ctx, "lw_raw", [P, D]), [sb(ctx, f"lw_{s}", [P, D], F32R) for s in ("hi", "lo")]
        bias = sb(ctx, "base_bias", [P, D])
        tbias = sb(ctx, "thr_bias", [P, 1])
        small = sb(ctx, "small", [P, NT, SMALL])
        ex, ad, sel = (sb(ctx, n, [P, NT, E1]) for n in ("ex1", "ad", "sel"))
        th, m8, s8, z8 = (sb(ctx, n, [P, NT]) for n in ("th", "m81", "s81", "z8"))
        hw = sb(ctx, "hw", [P, NT, E1 * R1])
        hT = [sb(ctx, f"hT_{s}", [P, N], F32R) for s in ("hi", "lo")]
        z = [sb(ctx, f"z{i}", [P, D]) for i in range(2)]
        g = [sb(ctx, f"g{i}", [P, D]) for i in range(2)]

        x_in, w_in = sem("x1_in"), sem("w_in")
        c_dve, sw_ready, bw_hi, bw_ready, lw_ready = (sem(n) for n in ("c_dve", "sw_ready", "bw_hi", "bw_ready", "lw_ready"))
        small_full, small_done, shifted, ex_ready, th_ready = (
            sem(n) for n in ("small_full", "small_done", "shifted", "ex1_ready", "th_ready"))
        hw_ready, hT_full, hT_hi, hT_lo = (sem(n) for n in ("hw_ready", "hT_full", "hT_hi", "hT_lo"))
        base_full, z_ready, g_ready, out_ready, stored = (
            sem(n) for n in ("base_full", "z_ready", "g1_ready", "out_ready", "stored"))
        out_rows = A["out"].rearrange("(t p) d -> t p d", p=P)
        SM_BANKS, BASE = 2, 4
        wide = lambda v: v[:, :].unsqueeze(2).broadcast_to([P, NT, E1])

        block = ctx.enter_context(nc.Block())

        @block.sync
        def _(sp):
            loads = [(sw_raw[:, :, :], A["small_w"]), (tbias[:, :], A["thr_b"].partition_broadcast(P).rearrange("p o n -> p (o n)")),
                     (lw_raw[:, :], A["low_b"]), (bias[:, :], A["base_b"].partition_broadcast(P).rearrange("p o n -> p (o n)")),
                     (bw_raw[:, :, :], A["base_w"])]
            for dst, src in loads:
                sp.dma_start(dst, src).then_inc(w_in, 16)
            sp.wait_ge(x1_stored, 16 * NT)
            for t in range(NT):
                sp.dma_start(x[:, t, :], x1_rows[t]).then_inc(x_in, 16)
            for t in range(NT):
                sp.wait_ge(out_ready, t + 1)
                sp.dma_start(out_rows[t], x[:, t, :]).then_inc(stored, 16)
            sp.wait_ge(stored, 16 * NT)

        @block.gpsimd
        def _(pool):
            for k in range(KD):
                pool.wait_ge(bw_hi, k + 1)
                pool.tensor_tensor(bw[1][:, k, :], bw_raw[:, k, :], f32(bw[0][:, k, :]), ALU.subtract).then_inc(bw_ready, 1)

        @block.scalar
        def _(act):
            act.wait_ge(w_in, 80)
            for k in range(KD):
                act.activation(bw[0][:, k, :], bw_raw[:, k, :], ACT.Copy).then_inc(bw_hi, 1)
            for t in range(NT):
                act.wait_ge(small_full, t + 1)
                act.activation(small[:, t, :], PS[:, t % SM_BANKS, 0:SMALL], ACT.Copy).then_inc(small_done, 1)
            act.wait_ge(shifted, 1)
            act.activation(ex[:, :, :], ad[:, :, :], ACT.Exp).then_inc(ex_ready, 1)
            act.activation(th[:, :], small[:, :, E1], ACT.Sigmoid, bias=tbias[:, 0:1]).then_inc(th_ready, 1)
            for t in range(NT):
                act.wait_ge(hT_full, t + 1)
                act.activation(hT[0][:, t * P:(t + 1) * P], PS[:, 2 + t % 2, 0:P], ACT.Copy).then_inc(hT_hi, 1)
            for t in range(NT):
                act.wait_ge(z_ready, t + 1)
                if t >= 2:
                    act.wait_ge(out_ready, t - 1)
                act.activation(g[t % 2][:, :], z[t % 2][:, :], ACT.Silu).then_inc(g_ready, 1)

        @block.vector
        def _(dve):
            step = Steps(dve, c_dve)
            for s in range(2):
                step(dve.memset(f32(sw[s][:, :, SMALL:]), 0.0), wait=False)
            dve.wait_ge(w_in, 80)
            step(dve.tensor_copy(sw[0][:, :, 0:SMALL], sw_raw[:, :, :]))
            dve.tensor_tensor(sw[1][:, :, 0:SMALL], sw_raw[:, :, :], f32(sw[0][:, :, 0:SMALL]), ALU.subtract).then_inc(sw_ready, 1)
            step(dve.tensor_copy(lw[0][:, :], lw_raw[:, :]))
            dve.tensor_tensor(lw[1][:, :], lw_raw[:, :], f32(lw[0][:, :]), ALU.subtract).then_inc(lw_ready, 1)
            dve.wait_ge(small_done, NT)
            gl = small[:, :, 0:E1]
            step(dve.tensor_reduce(m8[:, :], gl, AX.X, ALU.max))
            dve.tensor_tensor(ad[:, :, :], gl, wide(m8), ALU.subtract).then_inc(shifted, 1)
            dve.wait_ge(ex_ready, 1)
            step(dve.tensor_reduce(s8[:, :], ex[:, :, :], AX.X, ALU.add))
            step(dve.reciprocal(s8[:, :], s8[:, :]))
            step(dve.tensor_tensor(ex[:, :, :], ex[:, :, :], wide(s8), ALU.mult))
            dve.wait_ge(th_ready, 1)
            step(dve.tensor_scalar(th[:, :], th[:, :], THRESHOLD, None, ALU.mult))
            step(dve.tensor_tensor(ad[:, :, :], ex[:, :, :], wide(th), ALU.subtract))
            step(dve.tensor_scalar(sel[:, :, :], ad[:, :, :], 0.0, None, ALU.is_ge))
            step(dve.tensor_tensor(ad[:, :, :], ad[:, :, :], sel[:, :, :], ALU.mult))
            step(dve.tensor_reduce(s8[:, :], ad[:, :, :], AX.X, ALU.add))
            step(dve.tensor_scalar(z8[:, :], s8[:, :], 0.0, None, ALU.is_equal))
            step(dve.tensor_tensor(s8[:, :], s8[:, :], z8[:, :], ALU.add))
            step(dve.reciprocal(s8[:, :], s8[:, :]))
            step(dve.tensor_tensor(ad[:, :, :], ad[:, :, :], wide(s8), ALU.mult))
            step(dve.tensor_scalar(ad[:, :, :], ad[:, :, :], SCALING, None, ALU.mult))
            for t in range(NT):
                dve.tensor_tensor(hw[:, t, :].rearrange("p (e r) -> p e r", e=E1),
                                  small[:, t, E1 + 1:].rearrange("p (e r) -> p e r", e=E1),
                                  ad[:, t, :].unsqueeze(2).broadcast_to([P, E1, R1]), ALU.mult).then_inc(hw_ready, 1)
            for t in range(NT):
                dve.wait_ge(hT_hi, t + 1)
                s = slice(t * P, (t + 1) * P)
                dve.tensor_tensor(hT[1][:, s], PS[:, 2 + t % 2, 0:P], f32(hT[0][:, s]), ALU.subtract).then_inc(hT_lo, 1)
            dve.wait_ge(x_in, 16 * NT)
            for t in range(NT + 1):
                if t < NT:
                    dve.wait_ge(base_full, t + 1)
                    if t >= 2:
                        dve.wait_ge(g_ready, t - 1)
                    dve.tensor_tensor(z[t % 2][:, :], PS[:, BASE + t % 4, :], bias[:, :], ALU.add).then_inc(z_ready, 1)
                if t >= 1:
                    u = t - 1
                    dve.wait_ge(g_ready, u + 1)
                    step(dve.tensor_tensor(attn[:, u, :], attn[:, u, :], g[u % 2][:, :], ALU.mult))
                    dve.tensor_tensor(x[:, u, :], x[:, u, :], attn[:, u, :], ALU.add).then_inc(out_ready, 1)

        @block.tensor
        def _(pe):
            pe.wait_ge(sw_ready, 1)
            for t in range(NT):
                if t >= SM_BANKS:
                    pe.wait_ge(small_done, t - SM_BANKS + 1)
                for k in range(KD):
                    ins = mm3(pe, PS[:, t % SM_BANKS, 0:SMALL_PAD], [x_[:, k, t * P:(t + 1) * P] for x_ in xT],
                              [w[:, k, :] for w in sw], k == 0, k == KD - 1)
                ins.then_inc(small_full, 1)
            pe.wait_ge(bw_ready, KD)

            def base(t):
                for k in range(KD):
                    mm3(pe, PS[:, BASE + t % 4, :], [x_[:, k, t * P:(t + 1) * P] for x_ in xT],
                        [w[:, k, :] for w in bw], k == 0, False)

            def turn_rows(t):
                pe.wait_ge(hw_ready, t + 1)
                if t >= 2:
                    pe.wait_ge(hT_lo, t - 1)
                pe.transpose(PS[:, 2 + t % 2, 0:P], hw[:, t, :], ident[:, :]).then_inc(hT_full, 1)

            def low_rank(t):
                pe.wait_ge(hT_lo, t + 1)
                pe.wait_ge(lw_ready, 1)
                mm3(pe, PS[:, BASE + t % 4, :], [v[:, t * P:(t + 1) * P] for v in hT], [w[:, :] for w in lw],
                    False, True).then_inc(base_full, 1)

            AHEAD = 3
            for t in range(NT + AHEAD):
                if t < NT:
                    if t >= 4:
                        pe.wait_ge(z_ready, t - 3)
                    base(t)
                if t == AHEAD - 1:
                    for u in range(NT):
                        turn_rows(u)
                if t >= AHEAD:
                    low_rank(t - AHEAD)


def tables():
    inv = (np.float32(1.0) / np.power(np.float32(10000.0), np.arange(0, DH, 2, dtype=np.float32) / np.float32(DH))).astype(np.float32)
    angle = (np.arange(T, dtype=np.float32)[None, :] * np.concatenate([inv, inv])[:, None]).astype(np.float32)
    sin = np.sin(angle).astype(np.float32)
    sin[:DH // 2] *= -1
    key, query = np.arange(P)[None, :], np.arange(P)[:, None]
    near = np.where(key >= query, 0.0, HIDDEN).astype(np.float32)
    far = np.where(key <= query, 0.0, HIDDEN).astype(np.float32)
    zero = np.zeros((P, P), np.float32)
    return {
        "ident": np.eye(P, dtype=np.float32),
        "tri": (key >= query).astype(np.float32),
        "route": np.tile(np.concatenate([np.arange(E0, 0, -1), np.tril(np.ones((E0, E0)), -1).ravel(),
                                         np.arange(SLOT_TILES) * P, np.arange(SLOT_TILES)]).astype(np.float32), (P, 1)),
        "cos": np.cos(angle).astype(np.float32),
        "sin": sin,
        "edge": np.concatenate([near, zero, zero, far], 1),
        "both": np.concatenate([near, zero, far], 1),
    }


def layouts(i):
    def by_feature(w):
        return w.T.reshape(KD, P, -1).transpose(1, 0, 2)

    wk, wq, wv = (i[f"L1_attn_{n}"] for n in ("Wk", "Wq", "Wv"))
    wo = i["L1_attn_Wo"].T
    attn_w = []
    for g in range(HKV):
        kv = slice(g * DH, (g + 1) * DH)
        qs = [wq[(g * GQ + h) * DH:(g * GQ + h + 1) * DH] for h in range(GQ)]
        attn_w += [by_feature(w).reshape(P, KD * DH) for w in (wk[kv], *qs, wv[kv])]
        attn_w += [wo[(g * GQ + h) * DH:(g * GQ + h + 1) * DH] for h in range(GQ)]
    small = np.concatenate([i["L1_ffn_W_gate"], i["L1_ffn_W_thr"][None, :], i["L1_ffn_A_w"].reshape(E1 * R1, D)], 0)
    return {
        "x": i["L0_attn_x"].reshape(N, D),
        "bv_q": i["L0_attn_bv_q"], "bv_k": i["L0_attn_bv_k"], "bv_v": i["L0_attn_bv_v"],
        "gate_w": by_feature(i["L0_ffn_gate_w"]),
        "gate_b": i["L0_ffn_gate_b"][:, None],
        "expert_w": i["L0_ffn_expert_w"].transpose(0, 2, 1).reshape(E0 * KD, P, D),
        "expert_b": i["L0_ffn_expert_b"],
        "attn_w": np.stack(attn_w),
        "base_w": by_feature(i["L1_ffn_W_base"]),
        "base_b": i["L1_ffn_b_base"][None, :],
        "small_w": by_feature(small),
        "thr_b": i["L1_ffn_b_thr"][None, :],
        "low_b": i["L1_ffn_B_w"].transpose(0, 2, 1).reshape(E1 * R1, D),
    }


def kernel(**inputs):
    import concourse.bacc as bacc
    from concourse.bass_utils import run_bass_kernel_spmd

    nc = bacc.Bacc("TRN2", target_bir_lowering=False, num_devices=1)
    arrays, A = {}, {}
    laid = layouts({k: np.asarray(v) for k, v in inputs.items()})
    for name, a in {**laid, **tables()}.items():
        a = np.ascontiguousarray(a)
        arrays[f"in_{name}"] = a
        A[name] = nc.dram_tensor(f"in_{name}", a.shape, mybir.dt.from_np(a.dtype), kind="ExternalInput").ap()
    A["out"] = nc.dram_tensor("out", (N, D), F32, kind="ExternalOutput").ap()
    program(nc, A)
    r = run_bass_kernel_spmd(nc, [arrays], core_ids=[0])
    return r.results[0]["out"].reshape(BATCH, T, D)
```

```python
from contextlib import ExitStack

import numpy as np

import concourse.bass as bass
from concourse import mybir
from concourse.alu_op_type import AluOpType as ALU

ACT = mybir.ActivationFunctionType
AX = mybir.AxisListType
F32 = mybir.dt.float32
F32R = mybir.dt.float32r
U32 = mybir.dt.uint32

P = 128
BATCH, T, D = 2, 512, 512
N = BATCH * T
NT = N // P
TB = T // P
KD = D // P
EPS = 1e-5
H0 = 4
E0 = 8
HQ, HKV, DH = 32, 8, 128
GQ = HQ // HKV
WIN = P * (TB - 1)
NPROJ = GQ + 2
E1, R1 = 8, 16
THRESHOLD, SCALING = 0.125, 2.0
SMALL = E1 + 1 + E1 * R1
SMALL_PAD = 256
HIDDEN = -3.0e38

RAW_SLOTS = 4
FIRST_SPLIT = 2
PJ = 5
SLOT_TILES = NT + E0 - 1
SLOT_COLS = SLOT_TILES + 1


def f32(ap):
    return ap.bitcast(F32)


def mm3(pe, out, w, m, start, stop):
    pe.matmul(out, w[0], m[0], start=start, stop=False)
    pe.matmul(out, w[0], m[1], start=False, stop=False)
    return pe.matmul(out, w[1], m[0], start=False, stop=stop)


ROUTE_PARTS, ROUTE_COLS = [], 0
for width in (E0, E0 * E0, SLOT_TILES, SLOT_TILES):
    ROUTE_PARTS.append((ROUTE_COLS, ROUTE_COLS + width))
    ROUTE_COLS += width


def project(pe, out, halves, xT, b, ks=range(KD)):
    for k in ks:
        ins = mm3(pe, out, [w[:, k * P:(k + 1) * P] for w in halves], [x[:, k, b * T:(b + 1) * T] for x in xT], k == 0, k == KD - 1)
    return ins


def wake(pe, out, ident, n):
    for _ in range(n):
        pe.transpose(out[:, 0:P], ident[:, :], ident[:, :])


class Steps:

    def __init__(self, eng, sem):
        self.eng, self.sem, self.n = eng, sem, 0

    def __call__(self, ins, wait=True):
        self.n += 1
        ins.then_inc(self.sem, 1)
        if wait:
            self.wait()

    def wait(self):
        self.eng.wait_ge(self.sem, self.n)


def program(nc, A):
    with ExitStack() as outer:
        def sem(name):
            return outer.enter_context(nc.semaphore(name))

        def sb(ctx, name, shape, dt=F32):
            return ctx.enter_context(nc.sbuf_tensor(name, shape, dt))

        PS = outer.enter_context(nc.psum_tensor("PS", [P, 8, 512], F32))
        ident = sb(outer, "ident", [P, P])
        xT = [sb(outer, f"xT_{s}", [P, KD, N], F32R) for s in ("hi", "lo")]
        xn_dram = nc.dram_tensor("xn_spill", [N, D], F32, kind="Internal").ap()
        slot_token = nc.dram_tensor("slot_token", [P * SLOT_COLS, 1], U32, kind="Internal").ap()
        expert_out = nc.dram_tensor("expert_out", [SLOT_TILES * P, D], F32, kind="Internal").ap()
        x1_dram = nc.dram_tensor("x1_spill", [N, D], F32, kind="Internal").ap()
        x1_rows = x1_dram.rearrange("(t p) d -> t p d", p=P)
        x1_stored = sem("x1_stored")

        kept = Kept(lambda name, shape, dt=F32: sb(outer, name, shape, dt), sem)
        block_a(nc, A, sem, sb, PS, ident, xT, kept, (xn_dram, slot_token, expert_out), x1_rows, x1_stored)
        kept.grow()
        block_b(nc, A, sem, sb, PS, ident, xT, kept)
        block_c(nc, A, sem, sb, PS, ident, xT, kept, x1_rows, x1_stored)


class Kept:

    def __init__(self, tile, sem):
        self.tile = tile
        self.raw = tile("raw", [P, RAW_SLOTS, D])
        self.raw_in = [sem(f"ring_in{i}") for i in range(RAW_SLOTS)]
        self.hi, self.lo = sem("ring_hi"), sem("ring_lo")
        self.projected = sem("projected")
        self.wp = [self.halves(f"wp{j}") for j in range(FIRST_SPLIT)]
        self.cos, self.sin, self.table_in = tile("cos", [P, T]), tile("sin", [P, T]), sem("table_in")

    def halves(self, name):
        return [self.tile(f"{name}_{s}", [P, D], F32R) for s in ("hi", "lo")]

    def grow(self):
        self.wp += [self.halves(f"wp{j}") for j in range(FIRST_SPLIT, NPROJ)]
        self.wo = [[self.halves(f"wo{o}{h}") for h in range(GQ)] for o in range(2)]
        self.attn = self.tile("attn", [P, NT, D])
        self.small_w = self.wo[0][0:2]
        self.base_w = self.wp[0:KD]
        self.low_w = self.wo[0][2]
        self.ropes = self.tile("ropes", [P, 4, T])
        self.small = self.ropes[:, :, :].rearrange("p i t -> p (i t)")[:, 0:NT * SMALL].rearrange("p (t n) -> p t n", t=NT)


class Norm:
    BANKS = 4

    def __init__(self, sem, name, src, xn, xT, PS, ident, scratch):
        self.src, self.xn, self.xT, self.PS, self.ident = src, xn, xT, PS, ident
        self.st, self.mv, self.ve, self.sd, self.rs, self.tmp = scratch
        self.var_ready = sem(f"{name}_var_ready")
        self.sd_ready = sem(f"{name}_sd_ready")
        self.xn_ready = sem(f"{name}_xn_ready")
        self.turned = sem(f"{name}_turned")
        self.hi_ready = sem(f"{name}_hi_ready")
        self.lo_ready = sem(f"{name}_lo_ready")

    def statistics(self, dve, step, half, src_wait, amid=None):
        ts = range(TB * half, TB * (half + 1))
        for t in ts:
            src_wait(t)
            step(dve.bn_stats(self.st[:, t, :], self.src[:, t, :]), wait=False)
            if amid:
                amid(t)
        step.wait()
        for t in ts:
            step(dve.bn_aggr(self.mv[:, t, :], self.st[:, t, :]), wait=False)
        step.wait()
        h = slice(TB * half, TB * (half + 1))
        dve.tensor_scalar(self.ve[:, h], self.mv[:, h, 1], EPS, None, ALU.add).then_inc(self.var_ready, 1)

    def deviations(self, act, half):
        h = slice(TB * half, TB * (half + 1))
        act.wait_ge(self.var_ready, half + 1)
        act.activation(self.sd[:, h], self.ve[:, h], ACT.Sqrt).then_inc(self.sd_ready, 1)

    def normalise(self, dve, step, half):
        h = slice(TB * half, TB * (half + 1))
        rs, tmp = self.rs[:, h], self.tmp[:, h]
        dve.wait_ge(self.sd_ready, half + 1)
        step(dve.reciprocal(rs, self.sd[:, h]))
        step(dve.tensor_tensor(tmp, rs, rs, ALU.mult))
        step(dve.tensor_tensor(tmp, tmp, self.ve[:, h], ALU.mult))
        step(dve.tensor_scalar(tmp, tmp, -0.5, 1.5, ALU.mult, ALU.add))
        step(dve.tensor_tensor(rs, rs, tmp, ALU.mult))
        for t in range(TB * half, TB * (half + 1)):
            dve.tensor_scalar(self.xn[:, t, :], self.src[:, t, :], self.mv[:, t, 0:1], self.rs[:, t:t + 1],
                              ALU.subtract, ALU.mult).then_inc(self.xn_ready, 1)

    def turn(self, pe, t):
        pe.wait_ge(self.xn_ready, t + 1)
        if t >= self.BANKS:
            pe.wait_ge(self.lo_ready, t - self.BANKS + 1)
        for k in range(KD):
            ins = pe.transpose(self.PS[:, t % self.BANKS, k * P:(k + 1) * P], self.xn[:, t, k * P:(k + 1) * P], self.ident[:, :])
        ins.then_inc(self.turned, 1)

    def bank(self, t):
        return self.PS[:, t % self.BANKS, :].rearrange("p (k n) -> p k n", k=KD)

    def high(self, act, t):
        act.wait_ge(self.turned, t + 1)
        act.activation(self.xT[0][:, :, t * P:(t + 1) * P], self.bank(t), ACT.Copy).then_inc(self.hi_ready, 1)

    def low(self, dve, t):
        dve.wait_ge(self.hi_ready, t + 1)
        s = slice(t * P, (t + 1) * P)
        dve.tensor_tensor(self.xT[1][:, :, s], self.bank(t), f32(self.xT[0][:, :, s]),
                          ALU.subtract).then_inc(self.lo_ready, 1)


def block_a(nc, A, sem, sb, PS, ident, xT, kept, spills, x1_rows, x1_stored):
    xn_dram, slot_token, expert_out = spills
    with ExitStack() as ctx:
        x = sb(ctx, "x", [P, NT, D])
        xn = sb(ctx, "xn", [P, NT, D])
        xv = [sb(ctx, f"xv_{s}", [P, NT, D], F32R) for s in ("hi", "lo")]
        y = sb(ctx, "y", [P, NT, D])
        st = sb(ctx, "st", [P, NT, 6])
        mv = sb(ctx, "mv", [P, NT, 2])
        ve, sd, rs, tmp8 = (sb(ctx, n, [P, NT]) for n in ("ve", "sd", "rs", "tmp8"))
        scratch = (st, mv, ve, sd, rs, tmp8)
        bv = sb(ctx, "bv", [3 * H0, P])
        bw = sb(ctx, "bw", [3 * H0, P])
        alpha = sb(ctx, "alpha", [3 * H0, 1])
        bind = sb(ctx, "bind", [P, 3 * H0])
        qk = sb(ctx, "qk", [P, H0])
        xf = [sb(ctx, f"xf{i}", [P, T]) for i in range(2)] + [y[:, TB + i, :] for i in range(2)]
        XF = len(xf)
        q = [[sb(ctx, f"q{i}_{s}", [P, T], F32R) for s in ("hi", "lo")] for i in range(2)]
        tri = sb(ctx, "tri", [P, P])
        af = y[:, 0:TB, :]
        a = [sb(ctx, f"a_{s}", [P, TB, T], F32R) for s in ("hi", "lo")]
        sT = [sb(ctx, f"sT{i}", [P, T]) for i in range(2)]
        gw = sb(ctx, "gw", [P, KD, E0])
        gwp = [sb(ctx, f"gwp_{s}", [P, KD, P], F32R) for s in ("hi", "lo")]
        gb = sb(ctx, "gb", [E0, 1])
        lT = y[0:E0, NT - 2:NT, :].rearrange("e t n -> e (t n)")
        route = sb(ctx, "route", [P, ROUTE_COLS])
        order, below, steps, tiles = (route[:, a:b] for a, b in ROUTE_PARTS)
        lg, oh = (sb(ctx, n, [P, NT, E0]) for n in ("lg", "oh"))
        ex_end = sb(ctx, "ex", [P, NT + 1, E0])
        ex = ex_end[:, 0:NT, :]
        ones = sb(ctx, "ones", [P, P])
        rank = sb(ctx, "rank", [P, NT, E0])
        n_tiles, first, end, before = (sb(ctx, n, [P, E0]) for n in ("n_tiles", "first", "end", "before"))
        cmp = [sb(ctx, f"cmp{i}", [P, SLOT_TILES * E0]) for i in range(2)]
        slot, div, at = (sb(ctx, n, [P, NT]) for n in ("slot", "div", "at"))
        tile_e = sb(ctx, "tile_e", [P, SLOT_TILES])
        slot_i, at_i, token = (sb(ctx, n, [P, NT], U32) for n in ("slot_i", "at_i", "token"))
        tile_i = sb(ctx, "tile_i", [P, SLOT_TILES], U32)
        no_token, slot_t = (sb(ctx, n, [P, SLOT_COLS], U32) for n in ("no_token", "slot_t"))
        m8, s8 = (sb(ctx, n, [P, NT]) for n in ("m8", "s8"))
        eb = sT[1][0:E0, :]
        expert_id = sb(ctx, "expert_id", [E0, P])
        sel = [sb(ctx, f"sel{i}", [E0, P], F32R) for i in range(2)]
        ebs = [sb(ctx, f"eb_{s}", [E0, D], F32R) for s in ("hi", "lo")]
        raw = [kept.raw, sb(ctx, "raw1", [P, KD, D]), x[:, TB:, :], x[:, 0:TB, :]]
        QUAD = len(raw)
        w = [[sb(ctx, f"w_{s}", [P, KD, D], F32R) for s in ("hi", "lo")], a]
        yt = [y[:, TB + i, :] for i in range(2)]
        xg = [y[:, TB + 2 + i, :] for i in range(2)]
        xgT = [gwp, [half[:, :].rearrange("p (k n) -> p k n", k=KD) for half in q[0]]]

        x_in = [sem(f"x_in{t}") for t in range(NT)]
        early_in, late_in = sem("early_in"), sem("late_in")
        raw_in = [[sem(f"raw_in{i}_{k}") for k in range(KD)] for i in range(QUAD)]
        a_dve = sem("a_dve")
        gw_lo = sem("gw_lo")
        bind_rows, bind_turned, bind_ready, eb_ready = (sem(n) for n in ("bind_rows", "bind_turned", "bind_ready", "eb_ready"))
        xv_hi, xv_lo = sem("xv_hi"), sem("xv_lo")
        xf_ready, q_hi, q_ready = sem("xf_ready"), sem("q_hi"), sem("q_ready")
        s_full, sig_done = sem("s_full"), sem("sig_done")
        a_hi, a_ready = sem("a_hi"), sem("a_ready")
        o_full, sT_ready, sT_turned, s_done = sem("o_full"), sem("sT_ready"), sem("sT_turned"), sem("s_done")
        gl_full, gl_done, lg_turned, lg_shifted, ex_ready = (
            sem(n) for n in ("gl_full", "gl_done", "lg_turned", "lg_shifted", "ex_ready"))
        oh_ready, sel_ready = sem("oh_ready"), sem("sel_ready")
        counted = sem("counted")
        at_ready, tile_ready = sem("at_ready"), sem("tile_ready")
        prepared, none_stored = sem("prepared"), sem("none_stored")
        xn_stored, token_stored, slot_t_in = sem("xn_stored"), sem("token_stored"), sem("slot_t_in")
        xg_in = [sem(f"xg_in{i}") for i in range(2)]
        xg_turned, xgT_hi, xgT_lo = sem("xg_turned"), sem("xgT_hi"), sem("xgT_lo")
        w_hi, w_low = sem("w_hi"), [sem("w_lo_pool"), sem("w_lo_dve")]
        y_full, y_done = sem("y_full"), sem("y_done")
        y_stored = [sem(f"y_stored{i}") for i in range(2)]
        yg_in = [sem(f"yg_in{t}") for t in range(NT)]
        scaled = sem("scaled")
        g_ready, x1_ready, x1_pool = sem("g_ready"), sem("x1_ready"), sem("x1_pool")
        norm0 = Norm(sem, "norm0", x, xn, xT, PS, ident, scratch)
        norm1 = Norm(sem, "norm1", x, xn, xT, PS, ident, scratch)
        s_rows = xn

        x_rows = A["x"].rearrange("(t p) d -> t p d", p=P)
        early = [(ident[:, :], A["ident"]), (bv[0:H0, :], A["bv_q"]), (bv[H0:2 * H0, :], A["bv_k"]), (bv[2 * H0:3 * H0, :], A["bv_v"]),
                 (gw[:, :, :], A["gate_w"])]
        late = [(tri[:, :], A["tri"]), (route[:, :], A["route"]), (gb[:, :], A["gate_b"]), (eb[:, :], A["expert_b"]),
                (expert_id[:, :], A["expert_id"])]
        heads = [(b, h) for b in range(BATCH) for h in range(H0)]
        NH = len(heads)
        YF0, YD0, XL0 = 1, 2, 1
        Y_BANK, TURN_BANK = 0, 2
        TURNS = SLOT_TILES // QUAD
        HALF_K = KD // 2

        def expert_tiles(eng, step, turns=TURNS, tiles=SLOT_TILES):
            with eng.Fori(0, turns) as i:
                for q in range(QUAD):
                    step(i, q, True)
            for j in range(QUAD * turns, tiles):
                step(j // QUAD, j % QUAD, j + 1 < SLOT_TILES)

        def next_tile(i, q):
            return (i, q + 1) if q + 1 < QUAD else (i + 1, 0)

        def col0(j):
            return min(P * j, T - 2 * P)

        block = ctx.enter_context(nc.Block())

        @block.sync
        def _(sp):
            for t in range(NT):
                sp.dma_start(x[:, t, :], x_rows[t]).then_inc(x_in[t], 16)
            sp.wait_ge(prepared, 1)
            sp.dma_start(slot_token.rearrange("(p j) o -> p (j o)", p=P), no_token[:, :]).then_inc(none_stored, 16)
            for t in range(NT):
                sp.wait_ge(norm0.xn_ready, t + 1)
                sp.dma_start(xn_dram.rearrange("(t p) d -> t p d", p=P)[t], xn[:, t, :]).then_inc(xn_stored, 16)

            def load_weights(i, q, first=False):
                e = sp.value_load(tile_i[0:1, bass.ds(QUAD * i + q, 1)], min_val=0, max_val=E0 - 1)
                for k in range(KD):
                    if not first:
                        sp.wait_ge(w_low[k // HALF_K], HALF_K * (QUAD * (i - 1) + q) + k % HALF_K + 1)
                    sp.dma_start(raw[q][:, k, :], A["expert_w"][bass.ds(e * KD + k, 1)].rearrange("o p n -> (o p) n")
                                 ).then_inc(raw_in[q][k], 16)

            def store_products(i, q):
                sp.wait_ge(y_done, YD0 + QUAD * i + q + 1)
                sp.dma_start(expert_out.rearrange("(j p) d -> j p d", p=P)[bass.ds(QUAD * i + q, 1)].rearrange("o p d -> (o p) d"),
                             yt[q % 2]).then_inc(y_stored[q % 2], 16)

            def step(i, q, follows):
                load_weights(i + 1, q)
                store_products(i, q)

            sp.wait_ge(tile_ready, 1)
            load_weights(0, 0, first=True)
            load_weights(0, 1, first=True)
            sp.wait_ge(token_stored, 16 * NT)
            sp.dma_start(slot_t[:, :], slot_token.rearrange("(p j) o -> p (j o)", p=P)).then_inc(slot_t_in, 16)
            sp.wait_ge(norm0.xn_ready, NT)
            load_weights(0, 2, first=True)
            load_weights(0, 3, first=True)
            expert_tiles(sp, step, TURNS - 1, SLOT_TILES - QUAD)
            for j in range(SLOT_TILES - QUAD, SLOT_TILES):
                store_products(j // QUAD, j % QUAD)
                if j in (SLOT_TILES - 4, SLOT_TILES - 1):
                    for low in w_low:
                        sp.wait_ge(low, HALF_K * (j + 1))
                    for t in (range(TB) if j < SLOT_TILES - 1 else range(TB, NT)):
                        sp.dma_start(x[:, t, :], x_rows[t]).then_inc(x_in[t], 16)
                if j == SLOT_TILES - 3:
                    for low in w_low:
                        sp.wait_ge(low, HALF_K * (j + 1))
                    for c in range(RAW_SLOTS):
                        sp.dma_start(kept.raw[:, c, :], A["attn_w"][c]).then_inc(kept.raw_in[c], 16)
                    for dst, src in ((kept.cos[:, :], A["cos"]), (kept.sin[:, :], A["sin"])):
                        sp.dma_start(dst, src).then_inc(kept.table_in, 16)
            for t in range(NT):
                sp.wait_ge(*((x1_ready, t + 1) if t < TB else (x1_pool, t - TB + 1)))
                sp.dma_start(x1_rows[t], x[:, t, :]).then_inc(x1_stored, 16)
            sp.wait_ge(x1_stored, 16 * NT)

        @block.gpsimd
        def _(pool):
            pool.memset(no_token[:, :], 0).then_inc(prepared, 1)
            pool.memset(ones[:, :], 1.0).then_inc(prepared, 1)
            pool.iota(token[:, :], pattern=[[P, NT]], base=0, channel_multiplier=1).then_inc(prepared, 1)

            def query_rows(n):
                b, h = heads[n]
                pool.wait_ge(norm0.lo_ready, TB * (b + 1))
                if n >= XF:
                    pool.wait_ge(q_ready, n - XF + 1)
                s = slice(b * T, (b + 1) * T)
                pool.tensor_tensor(xf[n % XF][:, :], f32(xT[0][:, h, s]), f32(xT[1][:, h, s]), ALU.add).then_inc(xf_ready, 1)

            def value_low(b):
                for t in range(TB * b, TB * (b + 1)):
                    pool.wait_ge(xv_hi, t + 1)
                    pool.tensor_tensor(xv[1][:, t, :], xn[:, t, :], f32(xv[0][:, t, :]), ALU.subtract).then_inc(xv_lo, 1)

            query_rows(0)
            query_rows(1)
            value_low(0)
            query_rows(2)
            query_rows(3)
            value_low(1)
            EARLY = NH - 2
            for n in range(4, EARLY):
                query_rows(n)
            pool.wait_ge(at_ready, 1)
            pool.wait_ge(prepared, 3)
            pool.wait_ge(none_stored, 16)
            for t in range(NT):
                pool.indirect_dma_start(slot_token, bass.IndirectOffsetOnAxis(at_i[:, t:t + 1], 0), token[:, t:t + 1],
                                        None).then_inc(token_stored, 16)
            for n in range(EARLY, NH):
                query_rows(n)

            def gather_rows(j):
                if j >= 2:
                    pool.wait_ge(xg_turned, j - 1)
                pool.indirect_dma_start(xg[j % 2], None, xn_dram, bass.IndirectOffsetOnAxis(slot_t[:, j:j + 1], 0)
                                        ).then_inc(xg_in[j % 2], 16)

            pool.wait_ge(slot_t_in, 16)
            pool.wait_ge(xn_stored, 16 * NT)
            for j in range(2):
                gather_rows(j)
            for j in range(SLOT_TILES):
                for k in range(HALF_K):
                    pool.wait_ge(w_hi, KD * j + k + 1)
                    pool.tensor_tensor(w[j % 2][1][:, k, :], raw[j % QUAD][:, k, :], f32(w[j % 2][0][:, k, :]),
                                       ALU.subtract).then_inc(w_low[0], 1)
                if j + 2 < SLOT_TILES:
                    gather_rows(j + 2)
            pool.sem_inc(kept.lo, RAW_SLOTS)
            for c, (high, low) in enumerate(kept.wp):
                pool.wait_ge(kept.hi, c + 1)
                pool.tensor_tensor(low[:, :], kept.raw[:, c, :], f32(high[:, :]), ALU.subtract).then_inc(kept.lo, 1)
            pool.wait_ge(y_stored[0], 16 * (SLOT_TILES // 2 + 2))
            pool.wait_ge(y_stored[1], 16 * (SLOT_TILES // 2 + 1))
            for t in range(NT):
                pool.indirect_dma_start(y[:, t, :], None, expert_out, bass.IndirectOffsetOnAxis(slot_i[:, t:t + 1], 0)
                                        ).then_inc(yg_in[t], 16)
            pool.wait_ge(s_done, NH)
            for t in range(TB, NT):
                pool.wait_ge(g_ready, t + 1)
                pool.tensor_tensor(y[:, t, :], y[:, t, :], s_rows[:, t, :], ALU.mult).then_inc(scaled, 1)
                pool.wait_ge(scaled, t - TB + 1)
                pool.wait_ge(x_in[t], 32)
                pool.tensor_tensor(x[:, t, :], x[:, t, :], y[:, t, :], ALU.add).then_inc(x1_pool, 1)

        @block.scalar
        def _(act):
            for dst, src in early:
                act.dma_start(dst, src).then_inc(early_in, 16)
            for half in range(BATCH):
                norm0.deviations(act, half)
                if half == 0:
                    for dst, src in late:
                        act.dma_start(dst, src).then_inc(late_in, 16)
                for t in range(TB * half, TB * (half + 1)):
                    norm0.high(act, t)
            def value_high(b):
                for t in range(TB * b, TB * (b + 1)):
                    act.activation(xv[0][:, t, :], xn[:, t, :], ACT.Copy).then_inc(xv_hi, 1)

            value_high(0)
            act.wait_ge(late_in, 16 * len(late))
            for b in range(BATCH):
                act.wait_ge(gl_full, b + 1)
                act.activation(lT[:, b * T:(b + 1) * T], PS[0:E0, 6 + b, :], ACT.Identity,
                               bias=gb[:, 0:1]).then_inc(gl_done, 1)

            def query_high(n):
                h = heads[n][1]
                act.wait_ge(xf_ready, n + 1)
                act.wait_ge(bind_ready, 1)
                if n >= 2:
                    act.wait_ge(s_full, TB * (n - 1))
                act.activation(q[n % 2][0][:, :], xf[n % XF][:, :], ACT.Copy, scale=qk[:, h:h + 1]).then_inc(q_hi, 1)

            def sigmoids(n):
                for j in range(TB):
                    act.wait_ge(s_full, TB * n + j + 1)
                    if n >= 1:
                        act.wait_ge(a_ready, TB * (n - 1) + j + 1)
                    act.activation(af[:, j, P * j:], PS[:, j, P * j:], ACT.Sigmoid).then_inc(sig_done, 1)

            def scale_out(n):
                act.wait_ge(o_full, n + 1)
                act.wait_ge(bind_ready, 1)
                act.wait_ge(eb_ready, 1)
                if n >= 2:
                    act.wait_ge(sT_turned, n - 1)
                h = heads[n][1]
                act.activation(sT[n % 2][:, :], PS[:, 4, :], ACT.Copy,
                               scale=bind[:, 2 * H0 + h:2 * H0 + h + 1]).then_inc(sT_ready, 1)

            def rows_out(n):
                b, h = heads[n]
                act.wait_ge(sT_turned, n + 1)
                act.wait_ge(xv_lo, NT)
                act.wait_ge(xn_stored, 16 * NT)
                act.activation(s_rows[:, b * TB:(b + 1) * TB, h * P:(h + 1) * P],
                               PS[:, 5, :].rearrange("p (t d) -> p t d", t=TB), ACT.Copy).then_inc(s_done, 1)

            query_high(0)
            query_high(1)
            sigmoids(0)
            for n in range(NH):
                if 1 <= n < NH - 2:
                    query_high(n + 2)
                if n + 1 < NH:
                    sigmoids(n + 1)
                if n == 1:
                    value_high(1)
                if n == 0:
                    act.wait_ge(lg_shifted, 1)
                    act.activation(ex, lg[:, :, :], ACT.Exp).then_inc(ex_ready, 1)
                    query_high(2)
                scale_out(n)
                if n >= 1:
                    rows_out(n - 1)
            rows_out(NH - 1)
            def high_halves(i, q, first=False):
                j, par = QUAD * i + q, q % 2
                for k in range(KD):
                    act.wait_ge(raw_in[q][k], 16 * i + 16)
                    if not first:
                        act.wait_ge(y_full, YF0 + j - 1)
                    act.activation(w[par][0][:, k, :], raw[q][:, k, :], ACT.Copy).then_inc(w_hi, 1)
                act.wait_ge(xg_turned, j + 1)
                act.activation(xgT[par][0][:, :, :], PS[:, TURN_BANK + par, :].rearrange("p (k n) -> p k n", k=KD),
                               ACT.Copy).then_inc(xgT_hi, 1)

            def step(i, q, follows):
                if follows:
                    high_halves(*next_tile(i, q))

            high_halves(0, 0, first=True)
            act.wait_ge(o_full, NH)
            expert_tiles(act, step)
            for c, (high, _) in enumerate(kept.wp):
                act.wait_ge(kept.raw_in[c], 16)
                act.activation(high[:, :], kept.raw[:, c, :], ACT.Copy).then_inc(kept.hi, 1)
            for t in range(NT):
                act.wait_ge(yg_in[t], 16)
                act.activation(y[:, t, :], y[:, t, :], ACT.Silu).then_inc(g_ready, 1)
            for half in range(BATCH):
                norm1.deviations(act, half)
                for t in range(TB * half, TB * (half + 1)):
                    norm1.high(act, t)

        @block.vector
        def _(dve):
            step = Steps(dve, a_dve)
            dve.sem_inc(y_done, YD0)
            dve.sem_inc(xgT_lo, XL0)
            for par in range(2):
                dve.sem_inc(y_stored[par], 16)
            step(dve.memset(ex_end[:, NT, :], 0.0), wait=False)
            for half in gwp:
                step(dve.memset(f32(half[:, :, :]), 0.0), wait=False)
            norm0.statistics(dve, step, 0, lambda t: dve.wait_ge(x_in[t], 16))
            norm0.normalise(dve, step, 0)
            norm0.statistics(dve, step, 1, lambda t: dve.wait_ge(x_in[t], 16))
            for t in range(HALF_K):
                norm0.low(dve, t)
            norm0.normalise(dve, step, 1)
            for t in range(HALF_K, TB):
                norm0.low(dve, t)
            dve.wait_ge(early_in, 16 * len(early))
            step(dve.tensor_copy(gwp[0][:, :, 0:E0], gw[:, :, :]))
            dve.tensor_tensor(gwp[1][:, :, 0:E0], gw[:, :, :], f32(gwp[0][:, :, 0:E0]), ALU.subtract).then_inc(gw_lo, 1)
            for t in range(TB, NT):
                norm0.low(dve, t)
            step(dve.tensor_reduce(alpha[:, :], bv[:, :], AX.X, ALU.add, apply_absolute_value=True), wait=False)
            step(dve.tensor_scalar(bw[:, :], bv[:, :], 0.0, 2.0, ALU.is_ge, ALU.mult))
            step(dve.tensor_scalar(alpha[:, :], alpha[:, :], 1.0 / P, None, ALU.mult))
            step(dve.tensor_scalar(bw[:, :], bw[:, :], -1.0, alpha[:, 0:1], ALU.add, ALU.mult))
            step(dve.tensor_tensor(bw[:, :], bw[:, :], bv[:, :], ALU.subtract))
            dve.tensor_tensor(bw[:, :], bw[:, :], bv[:, :], ALU.add).then_inc(bind_rows, 1)
            dve.wait_ge(late_in, 16 * len(late))
            step(dve.tensor_copy(ebs[0][:, :], eb[:, :]))
            dve.tensor_tensor(ebs[1][:, :], eb[:, :], f32(ebs[0][:, :]), ALU.subtract).then_inc(eb_ready, 1)
            dve.wait_ge(bind_turned, 1)
            step(dve.tensor_copy(bind[:, :], PS[:, 5, 0:3 * H0]))
            step(dve.tensor_tensor(qk[:, :], bind[:, 0:H0], bind[:, H0:2 * H0], ALU.mult))
            dve.tensor_scalar(qk[:, :], qk[:, :], 4.0 * P ** -0.5, None, ALU.mult).then_inc(bind_ready, 1)

            def query_low(n):
                h = heads[n][1]
                dve.wait_ge(q_hi, n + 1)
                dve.scalar_tensor_tensor(out=q[n % 2][1][:, :], in0=xf[n % XF][:, :], scalar=qk[:, h:h + 1],
                                         in1=f32(q[n % 2][0][:, :]), op0=ALU.mult, op1=ALU.subtract).then_inc(q_ready, 1)

            def split_weights(n):
                dve.wait_ge(sig_done, TB * (n + 1))
                diag = y[:, 0:TB + 1, :].rearrange("p t n -> p (t n)").rearrange("p (j c) -> p j c", c=T + P)[:, :, 0:P]
                step(dve.tensor_tensor(diag, diag, tri[:, :].unsqueeze(1).broadcast_to([P, TB, P]), ALU.mult))
                if n >= 1:
                    dve.wait_ge(o_full, n)
                for j in range(TB):
                    dve.tensor_copy(a[0][:, j, P * j:], af[:, j, P * j:]).then_inc(a_hi, 1)
                for j in range(TB):
                    dve.wait_ge(a_hi, TB * n + j + 1)
                    dve.tensor_tensor(a[1][:, j, P * j:], af[:, j, P * j:], f32(a[0][:, j, P * j:]),
                                      ALU.subtract).then_inc(a_ready, 1)

            wide = lambda v: v[:, :].unsqueeze(2).broadcast_to([P, NT, E0])

            def gate():
                dve.wait_ge(lg_turned, 1)
                step(dve.tensor_copy(lg[:, :, :], PS[:, 6, 0:NT * E0].rearrange("p (t e) -> p t e", t=NT)))
                step(dve.tensor_reduce(m8[:, :], lg[:, :, :], AX.X, ALU.max))
                dve.tensor_tensor(lg[:, :, :], lg[:, :, :], wide(m8), ALU.subtract).then_inc(lg_shifted, 1)
                dve.wait_ge(ex_ready, 1)
                step(dve.tensor_reduce(s8[:, :], ex, AX.X, ALU.add))
                step(dve.reciprocal(s8[:, :], s8[:, :]))
                step(dve.tensor_tensor(ex, ex, wide(s8), ALU.mult))
                step(dve.tensor_reduce(m8[:, :], ex, AX.X, ALU.max))
                step(dve.tensor_tensor(oh[:, :, :], ex, wide(m8), ALU.is_ge))
                step(dve.tensor_tensor(oh[:, :, :], oh[:, :, :], order[:, :].unsqueeze(1).broadcast_to([P, NT, E0]), ALU.mult))
                step(dve.tensor_reduce(m8[:, :], oh[:, :, :], AX.X, ALU.max))
                dve.tensor_tensor(ex, oh[:, :, :], wide(m8), ALU.is_equal).then_inc(oh_ready, 1)

            def routing():
                ranks = PS[:, 7, 0:NT * E0].rearrange("p (t e) -> p t e", t=NT)
                counts = PS[:, 7, NT * E0:(NT + 1) * E0]
                across = lambda v, n: v.unsqueeze(1).broadcast_to([P, n, v.shape[1]])
                along = lambda v, m: v.unsqueeze(2).broadcast_to([P, v.shape[1], m])
                cube = lambda i, n, m: cmp[i][:, 0:n * m].rearrange("p (n m) -> p n m", n=n)
                dve.wait_ge(counted, 1)
                step(dve.tensor_tensor(cube(0, E0, NT), along(counts, NT), across(steps[:, 0:NT], E0), ALU.is_gt))
                step(dve.tensor_reduce(n_tiles[:, :], cube(0, E0, NT), AX.X, ALU.add))
                step(dve.tensor_tensor(cube(0, E0, E0), below.rearrange("p (e f) -> p e f", e=E0), across(n_tiles[:, :], E0), ALU.mult))
                step(dve.tensor_reduce(first[:, :], cube(0, E0, E0), AX.X, ALU.add))
                step(dve.tensor_tensor(end[:, :], first[:, :], n_tiles[:, :], ALU.add), wait=False)
                step(dve.tensor_scalar(before[:, :], first[:, :], float(P), -1.0, ALU.mult, ALU.add))
                step(dve.tensor_tensor(cube(0, SLOT_TILES, E0), across(end[:, :], SLOT_TILES), along(tiles, E0), ALU.is_le), wait=False)
                step(dve.tensor_tensor(rank[:, :, :], ranks, across(before[:, :], NT), ALU.add))
                step(dve.tensor_reduce(tile_e[:, :], cube(0, SLOT_TILES, E0), AX.X, ALU.add), wait=False)
                step(dve.tensor_tensor(rank[:, :, :], rank[:, :, :], ex, ALU.mult))
                dve.tensor_scalar(tile_i[:, :], tile_e[:, :], float(E0 - 1), None, ALU.min).then_inc(tile_ready, 1)
                step(dve.tensor_reduce(slot[:, :], rank[:, :, :], AX.X, ALU.add))
                step(dve.tensor_copy(slot_i[:, :], slot[:, :]), wait=False)
                step(dve.tensor_scalar(at[:, :], slot[:, :], float(SLOT_COLS), None, ALU.mult), wait=False)
                step(dve.tensor_tensor(cube(1, NT, SLOT_TILES - 1), along(slot[:, :], SLOT_TILES - 1), across(steps[:, 1:], NT), ALU.is_ge))
                step(dve.tensor_reduce(div[:, :], cube(1, NT, SLOT_TILES - 1), AX.X, ALU.add))
                dve.scalar_tensor_tensor(out=at_i[:, :], in0=div[:, :], scalar=-float(P * SLOT_COLS - 1), in1=at[:, :],
                                         op0=ALU.mult, op1=ALU.add).then_inc(at_ready, 1)

            query_low(0)
            for n in range(NH):
                if n + 1 < NH:
                    query_low(n + 1)
                split_weights(n)
                if n == 0:
                    gate()
                if n == 1:
                    routing()

            def low_halves(i, q):
                j, par = QUAD * i + q, q % 2
                for k in range(HALF_K, KD):
                    dve.wait_ge(w_hi, KD * j + k + 1)
                    dve.tensor_tensor(w[par][1][:, k, :], raw[q][:, k, :], f32(w[par][0][:, k, :]), ALU.subtract).then_inc(w_low[1], 1)
                dve.wait_ge(xgT_hi, j + 1)
                dve.tensor_tensor(xgT[par][1][:, :, :], PS[:, TURN_BANK + par, :].rearrange("p (k n) -> p k n", k=KD),
                                  f32(xgT[par][0][:, :, :]), ALU.subtract).then_inc(xgT_lo, 1)

            def select_bias(i, q):
                j, par = QUAD * i + q, q % 2
                if not (isinstance(j, int) and j == 0):
                    dve.wait_ge(y_full, YF0 + j - 1)
                e = tile_e[0:E0, bass.ds(j, 1)]
                dve.tensor_tensor(sel[par][:, :], expert_id[:, :], e.broadcast_to([E0, P]), ALU.is_equal).then_inc(sel_ready, 1)

            def tile_step(i, q, follows):
                par = q % 2
                if follows:
                    low_halves(*next_tile(i, q))
                    select_bias(*next_tile(i, q))
                dve.wait_ge(y_full, YF0 + QUAD * i + q + 1)
                dve.wait_ge(y_stored[par], 16 * (QUAD // 2 * i + q // 2) + 16)
                dve.tensor_copy(yt[par], PS[:, Y_BANK + par, :]).then_inc(y_done, 1)

            low_halves(0, 0)
            select_bias(0, 0)
            expert_tiles(dve, tile_step)

            dve.wait_ge(s_done, NH)
            def add_residual(t):
                dve.wait_ge(g_ready, t + 1)
                step(dve.tensor_tensor(y[:, t, :], y[:, t, :], s_rows[:, t, :], ALU.mult))
                dve.wait_ge(x_in[t], 32)
                dve.tensor_tensor(x[:, t, :], x[:, t, :], y[:, t, :], ALU.add).then_inc(x1_ready, 1)

            for t in range(TB):
                add_residual(t)
            norm1.statistics(dve, step, 0, lambda t: dve.wait_ge(x1_ready, t + 1))
            norm1.normalise(dve, step, 0)

            def first_lows(t):
                for u in {TB: (0, 1, 2, 3)}.get(t, ()):
                    norm1.low(dve, u)

            norm1.statistics(dve, step, 1, lambda t: dve.wait_ge(x1_pool, t - TB + 1), first_lows)
            norm1.normalise(dve, step, 1)
            for t in range(TB, NT):
                norm1.low(dve, t)

        @block.tensor
        def _(pe):
            pe.sem_inc(y_full, YF0)
            pe.wait_ge(early_in, 16 * len(early))
            for t in range(NT):
                norm0.turn(pe, t)
                if t == TB - 1:
                    wake(pe, PS[:, 7, :], ident, 24)
            pe.wait_ge(gw_lo, 1)
            for b in range(BATCH):
                pe.wait_ge(norm0.lo_ready, TB * (b + 1))
                for k in range(KD):
                    ins = mm3(pe, PS[:, 6 + b, :], [g[:, k, :] for g in gwp],
                              [v[:, k, b * T:(b + 1) * T] for v in xT], k == 0, k == KD - 1)
                ins.then_inc(gl_full, 1)
            pe.wait_ge(bind_rows, 1)
            pe.transpose(PS[:, 5, 0:3 * H0], bw[:, :], ident[0:3 * H0, 0:3 * H0]).then_inc(bind_turned, 1)

            def scores(n):
                b, h = heads[n]
                pe.wait_ge(q_ready, n + 1)
                for j in range(TB):
                    if n >= 1:
                        pe.wait_ge(sig_done, TB * (n - 1) + j + 1)
                    keys = slice(b * T + j * P, b * T + (j + 1) * P)
                    mm3(pe, PS[:, j, col0(j):], [v[:, h, keys] for v in xT],
                        [v[:, col0(j):] for v in q[n % 2]], True, True).then_inc(s_full, 1)

            def outputs(n):
                b, h = heads[n]
                pe.wait_ge(xv_lo, TB * (b + 1))
                if n >= 1:
                    pe.wait_ge(sT_ready, n)
                for j in range(TB):
                    pe.wait_ge(a_ready, TB * n + j + 1)
                    ins = mm3(pe, PS[:, 4, P * j:], [v[:, b * TB + j, h * P:(h + 1) * P] for v in xv],
                              [v[:, j, P * j:] for v in a], j == 0, j == TB - 1)
                ins.then_inc(o_full, 1)

            def turn_out(n):
                pe.wait_ge(sT_ready, n + 1)
                if n >= 1:
                    pe.wait_ge(s_done, n)
                for t in range(TB):
                    ins = pe.transpose(PS[:, 5, t * P:(t + 1) * P], sT[n % 2][:, t * P:(t + 1) * P], ident[:, :])
                ins.then_inc(sT_turned, 1)

            def count_tokens():
                pe.wait_ge(oh_ready, 1)
                pe.wait_ge(prepared, 2)
                pe.matmul(PS[:, 7, 0:(NT + 1) * E0], tri[:, :], ex_end[:, :, :], start=True, stop=False)
                for back in range(1, NT + 1):
                    ins = pe.matmul(PS[:, 7, back * E0:(NT + 1) * E0], ones[:, :], ex_end[:, 0:NT + 1 - back, :],
                                    start=False, stop=back == NT)
                ins.then_inc(counted, 1)

            wake(pe, PS[:, 4, :], ident, 24)
            scores(0)
            for n in range(NH):
                if n + 1 < NH:
                    scores(n + 1)
                if n == 1:
                    count_tokens()
                if n == 0:
                    pe.wait_ge(gl_done, BATCH)
                    for t in range(NT):
                        ins = pe.transpose(PS[:, 6, t * E0:(t + 1) * E0], lT[:, t * P:(t + 1) * P], ident[0:E0, 0:E0])
                    ins.then_inc(lg_turned, 1)
                outputs(n)
                if n >= 1:
                    turn_out(n - 1)
            turn_out(NH - 1)
            def turn_rows(i, q, first=False):
                j, par = QUAD * i + q, q % 2
                pe.wait_ge(xg_in[par], 16 * (QUAD // 2 * i + q // 2) + 16)
                if not first:
                    pe.wait_ge(xgT_lo, XL0 + j - 1)
                for k in range(KD):
                    ins = pe.transpose(PS[:, TURN_BANK + par, k * P:(k + 1) * P], xg[par][:, k * P:(k + 1) * P], ident[:, :])
                ins.then_inc(xg_turned, 1)

            def step(i, q, follows):
                if follows:
                    turn_rows(*next_tile(i, q))
                j, par = QUAD * i + q, q % 2
                pe.wait_ge(xgT_lo, XL0 + j + 1)
                for low in w_low:
                    pe.wait_ge(low, HALF_K * (j + 1))
                pe.wait_ge(y_done, YD0 + j - 1)
                for k in range(KD):
                    mm3(pe, PS[:, Y_BANK + par, :], [v[:, k, :] for v in xgT[par]], [v[:, k, :] for v in w[par]],
                              k == 0, False)
                pe.wait_ge(sel_ready, j + 1)
                pe.matmul(PS[:, Y_BANK + par, :], sel[par][:, :], ebs[0][:, :], start=False, stop=False)
                pe.matmul(PS[:, Y_BANK + par, :], sel[par][:, :], ebs[1][:, :], start=False, stop=True).then_inc(y_full, 1)

            pe.wait_ge(sig_done, TB * NH)
            turn_rows(0, 0, first=True)
            wake(pe, PS[:, 6, :], ident, 30)
            expert_tiles(pe, step)
            pe.wait_ge(x1_ready, TB)
            wake(pe, PS[:, TURN_BANK, :], ident, 24)
            for t in range(TB):
                norm1.turn(pe, t)
            pe.wait_ge(norm1.lo_ready, TB)
            for j, halves in enumerate(kept.wp):
                pe.wait_ge(kept.lo, RAW_SLOTS + j + 1)
                project(pe, PS[:, PJ + j % 2, :], halves, xT, 0).then_inc(kept.projected, 1)
                if j == 0:
                    for t in range(TB, NT):
                        norm1.turn(pe, t)


def block_b(nc, A, sem, sb, PS, ident, xT, kept):
    with ExitStack() as ctx:
        cos, sin, table_in = kept.cos, kept.sin, kept.table_in
        edge = sb(ctx, "edge", [P, TB * P])
        both = sb(ctx, "both", [P, WIN])
        raw, raw_in, wb_hi, wb_lo = kept.raw, kept.raw_in, kept.hi, kept.lo
        wp, wo, attn = kept.wp, kept.wo, kept.attn
        kT = [[sb(ctx, f"kT{b}_{s}", [P, T + 2 * P], F32R) for s in ("hi", "lo")] for b in range(BATCH)]
        qT = [[sb(ctx, f"qT{b}_{s}", [P, GQ, T], F32R) for s in ("hi", "lo")] for b in range(BATCH)]
        vT = sb(ctx, "vT", [P, T])
        v = [sb(ctx, f"v_{s}", [P, TB, DH], F32R) for s in ("hi", "lo")]
        rot, full = ([kept.ropes[:, 2 * n + i, :] for i in range(2)] for n in range(2))
        pr = [sb(ctx, f"pr{i}", [P, GQ, WIN]) for i in range(2)]
        pT = [sb(ctx, f"pT_{s}", [P, TB - 1, GQ * P], F32R) for s in ("hi", "lo")]
        oT = [sb(ctx, f"oT_{s}", [P, GQ * P], F32R) for s in ("hi", "lo")]
        nmax, rsum, rinv = ([sb(ctx, f"{n}{i}", [P, GQ]) for i in range(2)] for n in ("nmax", "rsum", "rinv"))

        mask_in = sem("mask_in")
        proj_full = kept.projected
        rope_read, roped = sem("rope_read"), sem("roped")
        kq_hi, kq_lo = sem("kq_hi"), sem("kq_lo")
        vT_done, v_turned, v_hi, v_lo = (sem(n) for n in ("vT_done", "v_turned", "v_hi", "v_lo"))
        sb_full, max_done, exp_done = sem("sb_full"), sem("max_done"), sem("exp_done")
        rinv_done = sem("rinv_done")
        max_wait, norm_wait = sem("max_wait"), sem("norm_wait")
        pr_first, pr_last = sem("pr_first"), sem("pr_last")
        pT_full, pT_hi, pT_lo = sem("pT_full"), sem("pT_hi"), sem("pT_lo")
        pv_full, oT_hi, oT_lo = sem("pv_full"), sem("oT_hi"), sem("oT_lo")
        wo_full, wo_done = sem("wo_full"), sem("wo_done")
        small_full, small_done = sem("small_full"), sem("small_done")

        SEQ = NPROJ + GQ
        TURNS = HKV // 2
        PP = 2 * BATCH
        KQ = NPROJ
        HALF = DH // 2
        SCALE = float(np.float32(1.0) / np.sqrt(np.float32(DH)))
        SC, TW, OB = (0, 1, 2, 0), 3, 7
        WB0, KQ0, PT0, WD0, WF0 = RAW_SLOTS, 2, 2, NT, 1
        V_, ALL, FRONT, BACK = NPROJ - 1, range(KD), range(KD // 2), range(KD // 2, KD)
        FILLERS = {0: ((0, ALL), (1, ALL)), 1: ((2, ALL), (3, ALL)), 2: ((4, FRONT), (4, BACK)), 3: ((V_, FRONT), (V_, BACK))}
        ROPES = {0: (0, 1), 1: (2, 3), 2: (None, 4), 3: (None, None)}
        SPLITS = {(0, 1): (0, 1), (0, 2): (2, 3), (0, 3): (4,), (1, 0): (5, 6), (1, 1): (7,), (1, 2): (8,), (1, 3): (9,)}

        def rope_low(eng, gg, pp, j):
            m, p, b = (NPROJ - 1) * pp + j, PP * gg + pp, pp % BATCH
            if j == 0:
                for at, n in ((0, T), (T, 2 * P)):
                    eng.wait_ge(kq_hi, kq_count(p, 0) - (at == 0))
                    eng.tensor_tensor(kT[b][1][:, at:at + n], full[m % 2][:, 0:n], f32(kT[b][0][:, at:at + n]),
                                      ALU.subtract).then_inc(kq_lo, 1)
            else:
                eng.wait_ge(kq_hi, kq_count(p, j))
                eng.tensor_tensor(qT[b][1][:, j - 1, :], full[m % 2][:, :], f32(qT[b][0][:, j - 1, :]),
                                  ALU.subtract).then_inc(kq_lo, 1)

        def mask(i):
            return {0: edge[:, 0:WIN], TB - 1: edge[:, P:P + WIN]}.get(i, both[:, :])

        def keys(b, i):
            first = ((i + 1) % TB) * P
            return [t[:, first:first + WIN] for t in kT[b]]

        def kq_count(p, j):
            return KQ * p + j + 2

        def kq_before(p, j):
            return kq_count(p, j - 2) if j >= 2 else kq_count(p - 1, j + GQ - 1)

        def turned_bank(pp, i, c):
            return TW + ((TB - 1) * (TB * pp + i) + c) % 2

        def following(pp, i):
            return (pp, i + 1) if i + 1 < TB else (pp + 1, 0)

        def stages(last):
            for pp in range(PP):
                for i in range(TB):
                    pair_follows = not (last and pp == PP - 1)
                    yield pp, i, pair_follows or i + 1 < TB, pair_follows

        def splits(gg, pp, i, last):
            odd, b = divmod(pp, BATCH)
            if last and odd == 1:
                return
            for r in SPLITS.get((b, i), ()):
                yield weight_tile(gg, odd + 1, r)

        def weight_tile(gg, go, r):
            c = SEQ * go + r
            return (2 * SEQ * gg + c, c % RAW_SLOTS, (2 * SEQ // RAW_SLOTS) * gg + c // RAW_SLOTS + 1,
                    2 * gg + go, r, wp[r] if r < NPROJ else wo[go % 2][r - NPROJ])

        FFN_TILES = [(A["small_w"][:, k, :], SMALL, [w[:, k % 2 * SMALL_PAD:k % 2 * SMALL_PAD + SMALL] for w in kept.small_w[k // 2]])
                     for k in range(KD)]
        FFN_TILES += [(A["base_w"][:, k, :], D, [w[:, :] for w in kept.base_w[k]]) for k in range(KD)]
        FFN_TILES += [(A["low_b"], D, [w[:, :] for w in kept.low_w])]
        FFN_SPLITS = {(2, 1): (0, 1), (2, 2): (2, 3), (3, 0): (4, 5), (3, 1): (6, 7), (3, 2): (8,)}
        ATTN_TILES = 2 * SEQ * TURNS

        def ffn_tiles(pp, i, last):
            for n in FFN_SPLITS.get((pp, i), ()) if last else ():
                c = ATTN_TILES + n
                yield c, raw[:, c % RAW_SLOTS, 0:FFN_TILES[n][1]], FFN_TILES[n][2]

        def small_products(pp, i, last):
            return (2 * i, 2 * i + 1) if last and pp == PP - 1 else None

        block = ctx.enter_context(nc.Block())

        @block.sync
        def _(sp):
            for dst, src in ((edge[:, :], A["edge"]), (both[:, :], A["both"])):
                sp.dma_start(dst, src).then_inc(mask_in, 16)

            def load(gg, c, slot):
                c = 2 * SEQ * gg + c
                sp.wait_ge(wb_lo, c + 1)
                sp.dma_start(raw[:, slot, :], A["attn_w"][bass.ds(c, 1)].rearrange("o p n -> (o p) n")).then_inc(raw_in[slot], 16)

            with sp.Fori(0, TURNS - 1) as gg:
                for c in range(RAW_SLOTS, 2 * SEQ + RAW_SLOTS):
                    load(gg, c, c % RAW_SLOTS)
            for c in range(RAW_SLOTS, 2 * SEQ):
                load(TURNS - 1, c, c % RAW_SLOTS)
            for n, (src, width, _) in enumerate(FFN_TILES):
                c = ATTN_TILES + n
                sp.wait_ge(wb_lo, c + 1)
                sp.dma_start(raw[:, c % RAW_SLOTS, 0:width], src).then_inc(raw_in[c % RAW_SLOTS], 16)

        @block.gpsimd
        def _(pool):

            def split_low(tile):
                at, slot, _, _, _, halves = tile
                pool.wait_ge(wb_hi, at + 1)
                pool.tensor_tensor(halves[1][:, :], raw[:, slot, :], f32(halves[0][:, :]), ALU.subtract).then_inc(wb_lo, 1)

            def rope_sum(gg, pp, j):
                m, p = (NPROJ - 1) * pp + j, PP * gg + pp
                pool.wait_ge(rope_read, 3 * ((NPROJ - 1) * p + j + 1))
                pool.tensor_tensor(full[m % 2][:, :], full[m % 2][:, :], rot[m % 2][:, :], ALU.add).then_inc(roped, 1)

            def norm_first(gg, pp, i):
                s, par = TB * (PP * gg + pp) + i, (TB * pp + i) % 2
                pool.wait_ge(rinv_done, 2 * s + 1)
                pool.sem_inc(norm_wait, 1)
                for h in range(2):
                    pool.tensor_scalar(pr[par][:, h, :], pr[par][:, h, :], rinv[par][:, h:h + 1], 1.0,
                                       ALU.mult, ALU.mult).then_inc(pr_first, 1)

            def turn(gg, last):
                for pp, i, stage_follows, pair_follows in stages(last):
                    ropes = [j for j in ROPES[i] if j is not None and pair_follows]
                    if stage_follows:
                        norm_first(gg, *following(pp, i))
                    for j in ropes:
                        rope_sum(gg, pp + 1, j)
                    for j in ropes:
                        rope_low(pool, gg, pp + 1, j)
                    for tile in splits(gg, pp, i, last):
                        split_low(tile)
                    for c, whole, halves in ffn_tiles(pp, i, last):
                        pool.wait_ge(wb_hi, c + 1)
                        pool.tensor_tensor(halves[1], whole, f32(halves[0]), ALU.subtract).then_inc(wb_lo, 1)

            split_low(weight_tile(0, 0, FIRST_SPLIT))
            for j in range(NPROJ - 1):
                rope_sum(0, 0, j)
                if FIRST_SPLIT + 1 + j < NPROJ:
                    split_low(weight_tile(0, 0, FIRST_SPLIT + 1 + j))
                for t in {1: range(0, 4), 4: range(4, NT)}.get(j, ()):
                    pool.memset(attn[:, t, :], 0.0).then_inc(wo_done, 1)
            norm_first(0, 0, 0)
            for r in range(NPROJ, SEQ):
                split_low(weight_tile(0, 0, r))
            with pool.Fori(0, TURNS - 1) as gg:
                turn(gg, False)
            turn(TURNS - 1, True)

        @block.scalar
        def _(act):
            def split_high(tile):
                at, slot, loads, g, r, halves = tile
                act.wait_ge(raw_in[slot], 16 * loads)
                if not (isinstance(g, int) and g == 0):
                    if r < NPROJ:
                        act.wait_ge(proj_full, NPROJ * (2 * g - 1) + r + 1)
                    else:
                        act.wait_ge(wo_full, WF0 + BATCH * TB * (g - 1))
                act.activation(halves[0][:, :], raw[:, slot, :], ACT.Copy).then_inc(wb_hi, 1)

            def rope_high(gg, pp, j):
                m, p, b = (NPROJ - 1) * pp + j, PP * gg + pp, pp % BATCH
                act.wait_ge(roped, (NPROJ - 1) * p + j + 1)
                if j == 0:
                    act.activation(kT[b][0][:, 0:T], full[m % 2][:, :], ACT.Copy).then_inc(kq_hi, 1)
                    act.activation(kT[b][0][:, T:], full[m % 2][:, 0:2 * P], ACT.Copy).then_inc(kq_hi, 1)
                else:
                    act.activation(qT[b][0][:, j - 1, :], full[m % 2][:, :], ACT.Copy).then_inc(kq_hi, 1)

            def value_out(gg, pp):
                p = PP * gg + pp
                act.wait_ge(proj_full, NPROJ * (p + 1))
                act.activation(vT[:, :], PS[:, PJ + V_ % 2, :], ACT.Copy).then_inc(vT_done, 1)

            def value_high(gg, pp):
                p = PP * gg + pp
                act.wait_ge(v_turned, p + 1)
                act.activation(v[0][:, :, :], PS[:, PJ + V_ % 2, :].rearrange("p (t d) -> p t d", t=TB), ACT.Copy).then_inc(v_hi, 1)

            def exps(gg, pp, i, hs):
                s, par = TB * (PP * gg + pp) + i, (TB * pp + i) % 2
                for h in hs:
                    act.wait_ge(max_done, GQ * s + h + 1)
                    act.activation(pr[par][:, h, :], PS[:, SC[h], 0:WIN], ACT.Exp, bias=nmax[par][:, h:h + 1], scale=-1.0,
                                   accum_out=rsum[par][:, h:h + 1]).then_inc(exp_done, 1)

            def small_out(t):
                act.wait_ge(small_full, t + 1)
                act.activation(kept.small[:, t, :], PS[:, PJ + t % 2, 0:SMALL], ACT.Copy).then_inc(small_done, 1)

            def turned_high(gg, pp, i, chunks):
                s = TB * (PP * gg + pp) + i
                for c in chunks:
                    bank = turned_bank(pp, i, c)
                    act.wait_ge(pT_full, (TB - 1) * s + c + 1)
                    act.activation(pT[0][:, c, :], PS[:, bank, :], ACT.Copy).then_inc(pT_hi, 1)

            def out_high(gg, pp, i):
                s = TB * (PP * gg + pp) + i
                act.wait_ge(pv_full, s + 1)
                act.activation(oT[0][:, :], PS[:, OB, :], ACT.Copy).then_inc(oT_hi, 1)

            def turn(gg, last):
                for pp, i, stage_follows, pair_follows in stages(last):
                    smalls = small_products(pp, i, last)
                    if stage_follows:
                        exps(gg, *following(pp, i), range(GQ))
                    if smalls:
                        small_out(smalls[0])
                    out_high(gg, pp, i)
                    if i == TB - 1 and pair_follows:
                        value_out(gg, pp + 1)
                    if stage_follows:
                        turned_high(gg, *following(pp, i), (0, 1))
                    for j in ROPES[i]:
                        if j is not None and pair_follows:
                            rope_high(gg, pp + 1, j)
                    if stage_follows:
                        turned_high(gg, *following(pp, i), (2,))
                    if i == TB - 1 and pair_follows:
                        value_high(gg, pp + 1)
                    if smalls:
                        small_out(smalls[1])
                    for tile in splits(gg, pp, i, last):
                        split_high(tile)
                    for c, whole, halves in ffn_tiles(pp, i, last):
                        act.wait_ge(raw_in[c % RAW_SLOTS], 16 * (c // RAW_SLOTS + 1))
                        act.wait_ge(wo_full, WF0 + TB * (PP * TURNS - 2))
                        if pp == PP - 1:
                            act.wait_ge(proj_full, NPROJ * PP * TURNS)
                        act.activation(halves[0], whole, ACT.Copy).then_inc(wb_hi, 1)

            for r in range(FIRST_SPLIT, NPROJ):
                split_high(weight_tile(0, 0, r))
                if r == FIRST_SPLIT:
                    act.activation(rsum[0][:, 0:1], ident[:, 0:1], ACT.Exp)
            for j in range(GQ):
                rope_high(0, 0, j)
            exps(0, 0, 0, (0,))
            value_out(0, 0)
            rope_high(0, 0, GQ)
            exps(0, 0, 0, (1, 2))
            value_high(0, 0)
            exps(0, 0, 0, (3,))
            for r in (NPROJ, NPROJ + 1):
                split_high(weight_tile(0, 0, r))
            turned_high(0, 0, 0, (0, 1))
            for r in (NPROJ + 2, NPROJ + 3):
                split_high(weight_tile(0, 0, r))
            turned_high(0, 0, 0, (2,))
            with act.Fori(0, TURNS - 1) as gg:
                turn(gg, False)
            turn(TURNS - 1, True)

        @block.vector
        def _(dve):
            dve.sem_inc(pT_lo, PT0)
            dve.sem_inc(kq_lo, KQ0)
            dve.wait_ge(table_in, 32)

            def rope(gg, pp, j):
                m, p = (NPROJ - 1) * pp + j, PP * gg + pp
                dve.wait_ge(proj_full, NPROJ * p + j + 1)
                dve.wait_ge(kq_lo, KQ0 + kq_before(p, j))
                dve.tensor_tensor(full[m % 2][:, :], PS[:, PJ + j % 2, :], cos[:, :], ALU.mult).then_inc(rope_read, 1)
                for to, at in ((0, HALF), (HALF, 0)):
                    dve.tensor_tensor(rot[m % 2][to:to + HALF, :], PS[at:at + HALF, PJ + j % 2, :], sin[to:to + HALF, :],
                                      ALU.mult).then_inc(rope_read, 1)

            def value_low(gg, pp):
                p = PP * gg + pp
                dve.wait_ge(v_hi, p + 1)
                dve.tensor_tensor(v[1][:, :, :], PS[:, PJ + V_ % 2, :].rearrange("p (t d) -> p t d", t=TB), f32(v[0][:, :, :]),
                                  ALU.subtract).then_inc(v_lo, 1)

            def maxima(gg, pp, i, hs):
                s, par = TB * (PP * gg + pp) + i, (TB * pp + i) % 2
                for h in hs:
                    dve.wait_ge(sb_full, GQ * s + h + 1)
                    dve.sem_inc(max_wait, 1)
                    dve.tensor_tensor_reduce(PS[:, SC[h], 0:WIN], PS[:, SC[h], 0:WIN], mask(i), -SCALE, 3.0e38,
                                             ALU.add, ALU.min, nmax[par][:, h:h + 1]).then_inc(max_done, 1)

            def inverses(gg, pp, i, half):
                s, par = TB * (PP * gg + pp) + i, (TB * pp + i) % 2
                hs = slice(2 * half, 2 * half + 2)
                dve.wait_ge(exp_done, GQ * s + 2 * half + 2)
                dve.reciprocal(rinv[par][:, hs], rsum[par][:, hs]).then_inc(rinv_done, 1)

            def norm_last(gg, pp, i):
                s, par = TB * (PP * gg + pp) + i, (TB * pp + i) % 2
                dve.wait_ge(rinv_done, 2 * s + 2)
                for h in (2, 3):
                    dve.tensor_scalar(pr[par][:, h, :], pr[par][:, h, :], rinv[par][:, h:h + 1], None,
                                      ALU.mult).then_inc(pr_last, 1)

            def turned_low(gg, pp, i, chunks):
                s = TB * (PP * gg + pp) + i
                for c in chunks:
                    bank = turned_bank(pp, i, c)
                    dve.wait_ge(pT_hi, (TB - 1) * s + c + 1)
                    dve.tensor_tensor(pT[1][:, c, :], PS[:, bank, :], f32(pT[0][:, c, :]), ALU.subtract).then_inc(pT_lo, 1)

            def out_low(gg, pp, i):
                s = TB * (PP * gg + pp) + i
                dve.wait_ge(oT_hi, s + 1)
                dve.tensor_tensor(oT[1][:, :], PS[:, OB, :], f32(oT[0][:, :]), ALU.subtract).then_inc(oT_lo, 1)

            def accumulate(gg, pp, i):
                s, t = TB * (PP * gg + pp) + i, TB * (pp % BATCH) + i
                dve.wait_ge(wo_full, WF0 + s + 1)
                dve.wait_ge(wo_done, WD0 + s + 1 - NT)
                dve.tensor_tensor(attn[:, t, :], PS[:, OB, :], attn[:, t, :], ALU.add).then_inc(wo_done, 1)

            def turn(gg, last):
                for pp, i, stage_follows, pair_follows in stages(last):
                    ra, rb = ROPES[i] if pair_follows else (None, None)
                    if stage_follows:
                        maxima(gg, *following(pp, i), (0, 1, 2))
                        inverses(gg, *following(pp, i), 0)
                        maxima(gg, *following(pp, i), (3,))
                    if ra is not None:
                        rope(gg, pp + 1, ra)
                    if stage_follows:
                        inverses(gg, *following(pp, i), 1)
                        norm_last(gg, *following(pp, i))
                    out_low(gg, pp, i)
                    if rb is not None:
                        rope(gg, pp + 1, rb)
                    if stage_follows:
                        turned_low(gg, *following(pp, i), (0, 1))
                    accumulate(gg, pp, i)
                    if stage_follows:
                        turned_low(gg, *following(pp, i), (2,))
                    if i == TB - 1 and pair_follows:
                        value_low(gg, pp + 1)

            for j in range(NPROJ - 1):
                rope(0, 0, j)
                if 1 <= j < GQ:
                    rope_low(dve, 0, 0, j - 1)
            dve.wait_ge(mask_in, 32)
            maxima(0, 0, 0, (0,))
            rope_low(dve, 0, 0, GQ - 1)
            maxima(0, 0, 0, (1, 2))
            rope_low(dve, 0, 0, GQ)
            inverses(0, 0, 0, 0)
            maxima(0, 0, 0, (3,))
            inverses(0, 0, 0, 1)
            norm_last(0, 0, 0)
            value_low(0, 0)
            turned_low(0, 0, 0, range(TB - 1))
            with dve.Fori(0, TURNS - 1) as gg:
                turn(gg, False)
            turn(TURNS - 1, True)

        @block.tensor
        def _(pe):
            pe.sem_inc(wo_full, WF0)

            def project_pair(gg, pp, j, ks=ALL):
                p, b = PP * gg + pp, pp % BATCH
                go = pp // BATCH
                if ks[0] == 0:
                    if not (isinstance(p, int) and p == 0 and j < 2):
                        pe.wait_ge(v_lo, p) if j == 1 else pe.wait_ge(rope_read, 3 * ((NPROJ - 1) * p + max(j - 1, 0)))
                    pe.wait_ge(wb_lo, WB0 + 2 * SEQ * gg + SEQ * go + j + 1)
                ins = project(pe, PS[:, PJ + j % 2, :], wp[j], xT, b, ks)
                if ks[-1] == KD - 1:
                    ins.then_inc(proj_full, 1)

            def turn_values(gg, pp):
                p = PP * gg + pp
                pe.wait_ge(vT_done, p + 1)
                for t in range(TB):
                    ins = pe.transpose(PS[:, PJ + V_ % 2, t * P:(t + 1) * P], vT[:, t * P:(t + 1) * P], ident[:, :])
                ins.then_inc(v_turned, 1)

            def scores(gg, pp, i, hs):
                s, p, b = TB * (PP * gg + pp) + i, PP * gg + pp, pp % BATCH
                for h in hs:
                    pe.wait_ge(kq_lo, KQ0 + kq_count(p, h + 1))
                    if h == 3:
                        pe.wait_ge(exp_done, GQ * s + 1)
                    elif not (isinstance(s, int) and s == 0):
                        pe.wait_ge(exp_done, GQ * (s - 1) + (GQ if h == 0 else h + 1))
                    mm3(pe, PS[:, SC[h], 0:WIN], [q[:, h, i * P:(i + 1) * P] for q in qT[b]], keys(b, i),
                        True, True).then_inc(sb_full, 1)

            def small_product(t):
                pe.wait_ge(wb_lo, WB0 + ATTN_TILES + KD)
                if t < 2:
                    pe.wait_ge(*((rope_read, 3 * (NPROJ - 1) * PP * TURNS), (v_lo, PP * TURNS))[t])
                else:
                    pe.wait_ge(small_done, t - 1)
                for k in range(KD):
                    ins = mm3(pe, PS[:, PJ + t % 2, 0:SMALL_PAD], [x[:, k, t * P:(t + 1) * P] for x in xT],
                              [w[:, k % 2 * SMALL_PAD:(k % 2 + 1) * SMALL_PAD] for w in kept.small_w[k // 2]], k == 0, k == KD - 1)
                ins.then_inc(small_full, 1)

            def turn_weights(gg, pp, i, chunks):
                s, par = TB * (PP * gg + pp) + i, (TB * pp + i) % 2
                if chunks[0] == 0:
                    pe.wait_ge(pr_first, 2 * s + 2)
                    pe.wait_ge(pr_last, 2 * s + 2)
                for c in chunks:
                    bank = turned_bank(pp, i, c)
                    pe.wait_ge(pT_lo, PT0 + (TB - 1) * s + c - 1)
                    for h in range(GQ):
                        ins = pe.transpose(PS[:, bank, h * P:(h + 1) * P], pr[par][:, h, c * P:(c + 1) * P], ident[:, :])
                    ins.then_inc(pT_full, 1)

            def values(gg, pp, i):
                s, p = TB * (PP * gg + pp) + i, PP * gg + pp
                pe.wait_ge(v_lo, p + 1)
                pe.wait_ge(wo_done, WD0 + s)
                for c in range(TB - 1):
                    pe.wait_ge(pT_lo, PT0 + (TB - 1) * s + c + 1)
                    tile = (i + 1 + c) % TB
                    ins = mm3(pe, PS[:, OB, :], [x[:, tile, :] for x in v], [x[:, c, :] for x in pT], c == 0, c == TB - 2)
                ins.then_inc(pv_full, 1)

            def out_project(gg, pp, i):
                s, go = TB * (PP * gg + pp) + i, pp // BATCH
                pe.wait_ge(oT_lo, s + 1)
                pe.wait_ge(wb_lo, WB0 + 2 * SEQ * gg + SEQ * (go + 1))
                for h in range(GQ):
                    ins = mm3(pe, PS[:, OB, :], [x[:, h * P:(h + 1) * P] for x in oT], [x[:, :] for x in wo[go][h]],
                              h == 0, h == GQ - 1)
                ins.then_inc(wo_full, 1)

            def turn(gg, last):
                for pp, i, stage_follows, pair_follows in stages(last):
                    (ja, ka), (jb, kb) = FILLERS[i]
                    if stage_follows:
                        scores(gg, *following(pp, i), (0, 1, 2))
                    smalls = small_products(pp, i, last)
                    if pair_follows:
                        project_pair(gg, pp + 1, ja, ka)
                    elif smalls:
                        small_product(smalls[0])
                    if stage_follows:
                        scores(gg, *following(pp, i), (3,))
                    values(gg, pp, i)
                    if pair_follows:
                        project_pair(gg, pp + 1, jb, kb)
                    elif smalls:
                        small_product(smalls[1])
                    if stage_follows:
                        turn_weights(gg, *following(pp, i), (0, 1))
                    out_project(gg, pp, i)
                    if i == TB - 1 and pair_follows:
                        turn_values(gg, pp + 1)
                    if stage_follows:
                        turn_weights(gg, *following(pp, i), (2,))

            for j in range(FIRST_SPLIT, V_):
                project_pair(0, 0, j)
            scores(0, 0, 0, (0, 1))
            project_pair(0, 0, V_)
            scores(0, 0, 0, (2,))
            turn_values(0, 0)
            scores(0, 0, 0, (3,))
            wake(pe, PS[:, OB, :], ident, 12)
            turn_weights(0, 0, 0, (0, 1))
            turn_weights(0, 0, 0, (2,))
            with pe.Fori(0, TURNS - 1) as gg:
                turn(gg, False)
            turn(TURNS - 1, True)


def block_c(nc, A, sem, sb, PS, ident, xT, kept, x1_rows, x1_stored):
    with ExitStack() as ctx:
        x = sb(ctx, "x1", [P, NT, D])
        attn, bw, lw, small = kept.attn, kept.base_w, kept.low_w, kept.small
        bias = sb(ctx, "base_bias", [P, D])
        tbias = sb(ctx, "thr_bias", [P, 1])
        ex, ad, sel = (sb(ctx, n, [P, NT, E1]) for n in ("ex1", "ad", "sel"))
        th, m8, s8, z8 = (sb(ctx, n, [P, NT]) for n in ("th", "m81", "s81", "z8"))
        hw = sb(ctx, "hw", [P, NT, E1 * R1])
        hT = [sb(ctx, f"hT_{s}", [P, N], F32R) for s in ("hi", "lo")]
        z = [sb(ctx, f"z{i}", [P, D]) for i in range(2)]
        g = [sb(ctx, f"g{i}", [P, D]) for i in range(2)]

        x_in, w_in = [sem(f"x1_in{t}") for t in range(NT)], sem("w_in")
        c_dve, shifted, ex_ready, th_ready = (sem(n) for n in ("c_dve", "shifted", "ex1_ready", "th_ready"))
        hw_ready, hT_full, hT_hi, hT_lo = (sem(n) for n in ("hw_ready", "hT_full", "hT_hi", "hT_lo"))
        base_full, z_ready, g_ready, s_ready, out_ready, stored = (
            sem(n) for n in ("base_full", "z_ready", "g1_ready", "s1_ready", "out_ready", "stored"))
        out_rows = A["out"].rearrange("(t p) d -> t p d", p=P)
        BASE_BANKS, TURNED = 6, 6
        wide = lambda v: v[:, :].unsqueeze(2).broadcast_to([P, NT, E1])

        block = ctx.enter_context(nc.Block())

        @block.sync
        def _(sp):
            for dst, src in ((tbias[:, :], A["thr_b"]), (bias[:, :], A["base_b"])):
                sp.dma_start(dst, src.partition_broadcast(P).rearrange("p o n -> p (o n)")).then_inc(w_in, 16)
            sp.wait_ge(x1_stored, 16 * NT)
            for t in range(NT):
                sp.dma_start(x[:, t, :], x1_rows[t]).then_inc(x_in[t], 16)
            for t in range(NT):
                sp.wait_ge(out_ready, t + 1)
                sp.dma_start(out_rows[t], x[:, t, :]).then_inc(stored, 16)
            sp.wait_ge(stored, 16 * NT)

        @block.gpsimd
        def _(pool):
            for t in range(NT):
                pool.wait_ge(g_ready, t + 1)
                pool.tensor_tensor(attn[:, t, :], attn[:, t, :], g[t % 2][:, :], ALU.mult).then_inc(s_ready, 1)

        @block.scalar
        def _(act):
            act.wait_ge(w_in, 32)
            act.activation(th[:, :], small[:, :, E1], ACT.Sigmoid, bias=tbias[:, 0:1]).then_inc(th_ready, 1)
            act.wait_ge(shifted, 1)
            act.activation(ex[:, :, :], ad[:, :, :], ACT.Exp).then_inc(ex_ready, 1)
            for t in range(NT + 2):
                if t < NT:
                    act.wait_ge(hT_full, t + 1)
                    act.activation(hT[0][:, t * P:(t + 1) * P], PS[:, TURNED + t % 2, 0:P], ACT.Copy).then_inc(hT_hi, 1)
                if t >= 2:
                    u = t - 2
                    act.wait_ge(z_ready, u + 1)
                    if u >= 2:
                        act.wait_ge(s_ready, u - 1)
                    act.activation(g[u % 2][:, :], z[u % 2][:, :], ACT.Silu).then_inc(g_ready, 1)

        @block.vector
        def _(dve):
            step = Steps(dve, c_dve)
            gl = small[:, :, 0:E1]
            step(dve.tensor_reduce(m8[:, :], gl, AX.X, ALU.max))
            dve.tensor_tensor(ad[:, :, :], gl, wide(m8), ALU.subtract).then_inc(shifted, 1)
            dve.wait_ge(ex_ready, 1)
            step(dve.tensor_reduce(s8[:, :], ex[:, :, :], AX.X, ALU.add))
            step(dve.reciprocal(s8[:, :], s8[:, :]))
            step(dve.tensor_tensor(ex[:, :, :], ex[:, :, :], wide(s8), ALU.mult))
            dve.wait_ge(th_ready, 1)
            step(dve.tensor_scalar(th[:, :], th[:, :], THRESHOLD, None, ALU.mult))
            step(dve.tensor_tensor(ad[:, :, :], ex[:, :, :], wide(th), ALU.subtract))
            step(dve.tensor_scalar(sel[:, :, :], ad[:, :, :], 0.0, None, ALU.is_ge))
            step(dve.tensor_tensor(ad[:, :, :], ad[:, :, :], sel[:, :, :], ALU.mult))
            step(dve.tensor_reduce(s8[:, :], ad[:, :, :], AX.X, ALU.add))
            step(dve.tensor_scalar(z8[:, :], s8[:, :], 0.0, None, ALU.is_equal))
            step(dve.tensor_tensor(s8[:, :], s8[:, :], z8[:, :], ALU.add))
            step(dve.reciprocal(s8[:, :], s8[:, :]))
            step(dve.tensor_tensor(ad[:, :, :], ad[:, :, :], wide(s8), ALU.mult))
            step(dve.tensor_scalar(ad[:, :, :], ad[:, :, :], SCALING, None, ALU.mult))
            for t in range(NT):
                dve.tensor_tensor(hw[:, t, :].rearrange("p (e r) -> p e r", e=E1),
                                  small[:, t, E1 + 1:].rearrange("p (e r) -> p e r", e=E1),
                                  ad[:, t, :].unsqueeze(2).broadcast_to([P, E1, R1]), ALU.mult).then_inc(hw_ready, 1)
            dve.wait_ge(w_in, 32)
            for t in range(NT + 3):
                if t < NT:
                    dve.wait_ge(hT_hi, t + 1)
                    s = slice(t * P, (t + 1) * P)
                    dve.tensor_tensor(hT[1][:, s], PS[:, TURNED + t % 2, 0:P], f32(hT[0][:, s]), ALU.subtract).then_inc(hT_lo, 1)
                if 1 <= t <= NT:
                    u = t - 1
                    dve.wait_ge(base_full, u + 1)
                    if u >= 2:
                        dve.wait_ge(g_ready, u - 1)
                    dve.tensor_tensor(z[u % 2][:, :], PS[:, u % BASE_BANKS, :], bias[:, :], ALU.add).then_inc(z_ready, 1)
                if t >= 3:
                    u = t - 3
                    dve.wait_ge(x_in[u], 16)
                    dve.wait_ge(s_ready, u + 1)
                    dve.tensor_tensor(x[:, u, :], x[:, u, :], attn[:, u, :], ALU.add).then_inc(out_ready, 1)

        @block.tensor
        def _(pe):
            def base(t):
                if t >= BASE_BANKS:
                    pe.wait_ge(z_ready, t - BASE_BANKS + 1)
                for k in range(KD):
                    mm3(pe, PS[:, t % BASE_BANKS, :], [x_[:, k, t * P:(t + 1) * P] for x_ in xT],
                        [w[:, :] for w in bw[k]], k == 0, False)

            def turn_rows(t):
                pe.wait_ge(hw_ready, t + 1)
                if t >= 2:
                    pe.wait_ge(hT_lo, t - 1)
                pe.transpose(PS[:, TURNED + t % 2, 0:P], hw[:, t, :], ident[:, :]).then_inc(hT_full, 1)

            def low_rank(t):
                pe.wait_ge(hT_lo, t + 1)
                mm3(pe, PS[:, t % BASE_BANKS, :], [v[:, t * P:(t + 1) * P] for v in hT], [w[:, :] for w in lw],
                    False, True).then_inc(base_full, 1)

            AHEAD = 3
            for t in range(AHEAD):
                base(t)
            turn_rows(0)
            for t in range(NT):
                if t + 1 < NT:
                    turn_rows(t + 1)
                if t + AHEAD < NT:
                    base(t + AHEAD)
                low_rank(t)




def tables():
    inv = (np.float32(1.0) / np.power(np.float32(10000.0), np.arange(0, DH, 2, dtype=np.float32) / np.float32(DH))).astype(np.float32)
    angle = (np.arange(T, dtype=np.float32)[None, :] * np.concatenate([inv, inv])[:, None]).astype(np.float32)
    sin = np.sin(angle).astype(np.float32)
    sin[:DH // 2] *= -1
    key, query = np.arange(P)[None, :], np.arange(P)[:, None]
    near = np.where(key >= query, 0.0, HIDDEN).astype(np.float32)
    far = np.where(key <= query, 0.0, HIDDEN).astype(np.float32)
    zero = np.zeros((P, P), np.float32)
    return {
        "ident": np.eye(P, dtype=np.float32),
        "tri": (key >= query).astype(np.float32),
        "route": np.tile(np.concatenate([np.arange(E0, 0, -1), np.tril(np.ones((E0, E0)), -1).ravel(),
                                         np.arange(SLOT_TILES) * P, np.arange(SLOT_TILES)]).astype(np.float32), (P, 1)),
        "expert_id": np.tile(np.arange(E0, dtype=np.float32)[:, None], (1, P)),
        "cos": np.cos(angle).astype(np.float32),
        "sin": sin,
        "edge": np.concatenate([near, zero, zero, far], 1),
        "both": np.concatenate([near, zero, far], 1),
    }


def layouts(i):
    def by_feature(w):
        return w.T.reshape(KD, P, -1).transpose(1, 0, 2)

    wk, wq, wv = (i[f"L1_attn_{n}"] for n in ("Wk", "Wq", "Wv"))
    wo = i["L1_attn_Wo"].T
    attn_w = []
    for g in range(HKV):
        kv = slice(g * DH, (g + 1) * DH)
        qs = [wq[(g * GQ + h) * DH:(g * GQ + h + 1) * DH] for h in range(GQ)]
        attn_w += [by_feature(w).reshape(P, KD * DH) for w in (wk[kv], *qs, wv[kv])]
        attn_w += [wo[(g * GQ + h) * DH:(g * GQ + h + 1) * DH] for h in range(GQ)]
    small = np.concatenate([i["L1_ffn_W_gate"], i["L1_ffn_W_thr"][None, :], i["L1_ffn_A_w"].reshape(E1 * R1, D)], 0)
    return {
        "x": i["L0_attn_x"].reshape(N, D),
        "bv_q": i["L0_attn_bv_q"], "bv_k": i["L0_attn_bv_k"], "bv_v": i["L0_attn_bv_v"],
        "gate_w": by_feature(i["L0_ffn_gate_w"]),
        "gate_b": i["L0_ffn_gate_b"][:, None],
        "expert_w": i["L0_ffn_expert_w"].transpose(0, 2, 1).reshape(E0 * KD, P, D),
        "expert_b": i["L0_ffn_expert_b"],
        "attn_w": np.stack(attn_w),
        "base_w": by_feature(i["L1_ffn_W_base"]),
        "base_b": i["L1_ffn_b_base"][None, :],
        "small_w": by_feature(small),
        "thr_b": i["L1_ffn_b_thr"][None, :],
        "low_b": i["L1_ffn_B_w"].transpose(0, 2, 1).reshape(E1 * R1, D),
    }


def kernel(**inputs):
    import concourse.bacc as bacc
    from concourse.bass_utils import run_bass_kernel_spmd

    nc = bacc.Bacc("TRN2", target_bir_lowering=False, num_devices=1)
    arrays, A = {}, {}
    laid = layouts({k: np.asarray(v) for k, v in inputs.items()})
    for name, a in {**laid, **tables()}.items():
        a = np.ascontiguousarray(a)
        arrays[f"in_{name}"] = a
        A[name] = nc.dram_tensor(f"in_{name}", a.shape, mybir.dt.from_np(a.dtype), kind="ExternalInput").ap()
    A["out"] = nc.dram_tensor("out", (N, D), F32, kind="ExternalOutput").ap()
    program(nc, A)
    r = run_bass_kernel_spmd(nc, [arrays], core_ids=[0])
    return r.results[0]["out"].reshape(BATCH, T, D)
```
